# Optimizing a Trainium2 kernel written in Bass

```python
import numpy as np
import jax
import jax.numpy as jnp

def _softmax(x, axis=-1):
    return jax.nn.softmax(x, axis=axis)

def _gelu(x):
    return jax.nn.gelu(x, approximate=True)

def _silu(x):
    return jax.nn.silu(x)

def _sigmoid(x):
    return jax.nn.sigmoid(x)

def _layernorm(x, axis=-1, eps=1e-05):
    m = jnp.mean(x, axis=axis, keepdims=True)
    v = jnp.var(x, axis=axis, keepdims=True)
    return (x - m) / jnp.sqrt(v + eps)

def _scatter_add(tgt, idx, src, axis=0):
    return tgt.at[idx].add(src)

def _segment_sum(src, seg, n):
    return jax.ops.segment_sum(src, seg, n)
kernel_name = 'mk_audio_tower_d2_tok_audfeat256_r4_b1e804'

def setup_inputs(seed: int=0):
    np.random.seed(seed)
    _w = jnp.asarray

    def _rec_inputs():
        import jax
        import jax.numpy as jnp
        _rk = jax.random.key(seed)
        x = -0.000392918 + 0.999932 * jax.random.normal(jax.random.fold_in(_rk, 1), (16, 2048, 16), jnp.float32)
        return x
    x = _rec_inputs()

    def _L0_tok_setup():
        import jax, jax.numpy as jnp
        import numpy as np
        PATCH = 16
        STRIDE = 8
        EPS = 1e-05
        key = jax.random.key(seed)
        k1, k2, k3 = jax.random.split(key, 3)
        B, S, F, D = (128, 2048, 16, 64)
        in_dim = F * PATCH
        x = jax.random.normal(k1, (B, S, F), dtype=jnp.float32)
        bound = 1.0 / np.sqrt(in_dim)
        W = jax.random.uniform(k2, (D, in_dim), minval=-bound, maxval=bound, dtype=jnp.float32)
        b = jax.random.uniform(k3, (D,), minval=-bound, maxval=bound, dtype=jnp.float32)
        gamma = jnp.ones((D,), dtype=jnp.float32)
        beta = jnp.zeros((D,), dtype=jnp.float32)
        return {'x': x, 'W': W, 'b': b, 'gamma': gamma, 'beta': beta}
    _L0_tok_all = _L0_tok_setup()
    _L0_tok_in = {k: v for k, v in _L0_tok_all.items() if k in ('W', 'b', 'gamma', 'beta')}
    del _L0_tok_all

    def _L0_attn_setup():
        import jax, jax.numpy as jnp
        import numpy as np
        B, S, D, H, K = (8, 256, 64, 8, 5)
        DK = D // H

        def _layernorm(x, w, b, eps=1e-12):
            m = x.mean(-1, keepdims=True)
            v = ((x - m) ** 2).mean(-1, keepdims=True)
            return w * (x - m) / jnp.sqrt(v + eps) + b

        def _forward(x, conv_w, conv_b, sqrt_beta, ln_w, ln_b, q_w, q_b, k_w, k_b, v_w, v_b, out_w, out_b, gammas):
            b, s, d = x.shape
            h = gammas.shape[0]
            dk = d // h
            xc = x.transpose(0, 2, 1)
            low = jax.lax.conv_general_dilated(xc, conv_w, window_strides=(1,), padding=[(K - 1, 0)], dimension_numbers=('NCH', 'OIH', 'NCH'))
            low = low.transpose(0, 2, 1) + conv_b
            high = x - low
            hid = _layernorm(low + sqrt_beta ** 2 * high + x, ln_w, ln_b)

            def proj(w, bb):
                return (hid @ w.T + bb).reshape(b, s, h, dk).transpose(0, 2, 1, 3)
            q, k, v = (proj(q_w, q_b), proj(k_w, k_b), proj(v_w, v_b))
            scores = jnp.einsum('bhqd,bhkd->bhqk', q, k) / jnp.sqrt(jnp.float32(dk))
            mask = jnp.tril(jnp.ones((s, s), bool))
            p_ = jax.nn.softmax(jnp.where(mask, scores, -1e+32), axis=-1) * mask
            distcum = jnp.cumsum(p_, axis=-1)
            disttotal = p_.sum(-1, keepdims=True)
            idx = jnp.arange(s)
            pos = jnp.abs(idx[:, None] - idx[None, :]).astype(jnp.float32)
            dist = jax.lax.stop_gradient(jnp.sqrt(jnp.clip((disttotal - distcum) * pos, 0.0)))
            gamma = -jax.nn.softplus(gammas)[None]
            total_effect = jnp.clip(jnp.exp(dist * gamma), 1e-05, 100000.0)
            scores = jnp.where(mask, scores * total_effect, -1e+32)
            p = jax.nn.softmax(scores, axis=-1)
            p = p.at[:, :, 0, :].set(0.0)
            out = jnp.einsum('bhqk,bhkd->bhqd', p, v)
            out = out.transpose(0, 2, 1, 3).reshape(b, s, d)
            return out @ out_w.T + out_b
        key = jax.random.key(seed)
        ks = jax.random.split(key, 8)
        s = 0.05
        return dict(x=jax.random.normal(ks[0], (B, S, D), jnp.float32), conv_w=jax.random.normal(ks[1], (D, D, K), jnp.float32) * s, conv_b=jnp.zeros((D,), jnp.float32), sqrt_beta=jax.random.normal(ks[2], (1, 1, D), jnp.float32), ln_w=jnp.ones((D,), jnp.float32), ln_b=jnp.zeros((D,), jnp.float32), q_w=jax.random.normal(ks[3], (D, D), jnp.float32) * s, q_b=jnp.zeros((D,), jnp.float32), k_w=jax.random.normal(ks[4], (D, D), jnp.float32) * s, k_b=jnp.zeros((D,), jnp.float32), v_w=jax.random.normal(ks[5], (D, D), jnp.float32) * s, v_b=jnp.zeros((D,), jnp.float32), out_w=jax.random.normal(ks[6], (D, D), jnp.float32) * s, out_b=jnp.zeros((D,), jnp.float32), gammas=jax.random.normal(ks[7], (H, 1, 1), jnp.float32) * 0.1)
    _L0_attn_all = _L0_attn_setup()
    _L0_attn_in = {k: v for k, v in _L0_attn_all.items() if k in ('conv_w', 'conv_b', 'sqrt_beta', 'ln_w', 'ln_b', 'q_w', 'q_b', 'k_w', 'k_b', 'v_w', 'v_b', 'out_w', 'out_b', 'gammas')}
    del _L0_attn_all

    def _L0_ffn_setup():
        import jax, jax.numpy as jnp
        import numpy as np
        DIM = 64
        H = 8
        D = 64
        G = 64
        INNER = H * D
        SCALE = D ** (-0.5)
        key = jax.random.key(seed)
        ks = jax.random.split(key, 12)
        B, N = (4, 4096)
        x = jax.random.normal(ks[0], (B, N, DIM), dtype=jnp.float32)
        s = lambda fan_in: 1.0 / np.sqrt(fan_in)
        W_fx = jax.random.normal(ks[1], (DIM, INNER), dtype=jnp.float32) * s(DIM)
        b_fx = jnp.zeros((INNER,), dtype=jnp.float32)
        W_x = jax.random.normal(ks[2], (DIM, INNER), dtype=jnp.float32) * s(DIM)
        b_x = jnp.zeros((INNER,), dtype=jnp.float32)
        A = jax.random.normal(ks[3], (G, D), dtype=jnp.float32)
        Q, _ = jnp.linalg.qr(A.T)
        W_slice = Q[:, :G].astype(jnp.float32)
        b_slice = jnp.zeros((G,), dtype=jnp.float32)
        W_q = jax.random.normal(ks[4], (D, D), dtype=jnp.float32) * s(D)
        W_k = jax.random.normal(ks[5], (D, D), dtype=jnp.float32) * s(D)
        W_v = jax.random.normal(ks[6], (D, D), dtype=jnp.float32) * s(D)
        W_out = jax.random.normal(ks[7], (INNER, DIM), dtype=jnp.float32) * s(INNER)
        b_out = jnp.zeros((DIM,), dtype=jnp.float32)
        temperature = jnp.ones((1, H, 1, 1), dtype=jnp.float32) * 0.5
        return {'x': x, 'W_fx': W_fx, 'b_fx': b_fx, 'W_x': W_x, 'b_x': b_x, 'W_slice': W_slice, 'b_slice': b_slice, 'W_q': W_q, 'W_k': W_k, 'W_v': W_v, 'W_out': W_out, 'b_out': b_out, 'temperature': temperature}
    _L0_ffn_all = _L0_ffn_setup()
    _L0_ffn_in = {k: v for k, v in _L0_ffn_all.items() if k in ('W_fx', 'b_fx', 'W_x', 'b_x', 'W_slice', 'b_slice', 'W_q', 'W_k', 'W_v', 'W_out', 'b_out', 'temperature')}
    del _L0_ffn_all

    def _L1_attn_setup():
        import jax, jax.numpy as jnp
        import numpy as np
        DIM = 64
        WS = 64
        H = 8
        HD = DIM // H
        SCALE = HD ** (-0.5)
        key = jax.random.key(seed)
        k1, k2, k3, k4 = jax.random.split(key, 4)
        B, L = (8, 4096)
        x = jax.random.normal(k1, (B, L, DIM), dtype=jnp.float32)
        w_qkv = jax.random.normal(k2, (3 * DIM, DIM), dtype=jnp.float32) * DIM ** (-0.5)
        w_proj = jax.random.normal(k3, (DIM, DIM), dtype=jnp.float32) * DIM ** (-0.5)
        b_proj = jnp.zeros((DIM,), dtype=jnp.float32)
        rel_bias = jax.random.normal(k4, (2 * WS - 1,), dtype=jnp.float32) * 0.02
        return {'x': x, 'w_qkv': w_qkv, 'w_proj': w_proj, 'b_proj': b_proj, 'rel_bias': rel_bias}
    _L1_attn_all = _L1_attn_setup()
    _L1_attn_in = {k: v for k, v in _L1_attn_all.items() if k in ('w_qkv', 'w_proj', 'b_proj', 'rel_bias')}
    del _L1_attn_all

    def _L1_ffn_setup():
        import jax, jax.numpy as jnp
        import numpy as np
        NUM_EXPERTS = 8
        TOP_K = 2
        B, S, D = (8, 2048, 64)

        def _moe(tokens, router_w, w1, b1, w2, b2):
            N = tokens.shape[0]
            E = router_w.shape[0]
            logits = tokens.astype(jnp.float32) @ router_w.astype(jnp.float32).T
            probs = jax.nn.softmax(logits, axis=-1)
            rw, re = jax.lax.top_k(probs, TOP_K)
            if TOP_K > 1:
                rw = rw / jnp.maximum(rw.sum(-1, keepdims=True), 1e-12)
            rw = rw.astype(tokens.dtype)
            combine = jnp.zeros((N, E), tokens.dtype).at[jnp.arange(N)[:, None], re].set(rw)
            out = tokens
            for e in range(E):
                h = jax.nn.gelu(tokens @ w1[e] + b1[e], approximate=False)
                y = h @ w2[e] + b2[e]
                out = out + combine[:, e:e + 1] * y
            return out
        key = jax.random.key(seed)
        ks = jax.random.split(key, 4)
        scale = 1.0 / np.sqrt(D).astype(np.float32)
        return {'input_embeddings': jax.random.normal(ks[0], (B, S, D), jnp.float32), 'router_w': jax.random.normal(ks[1], (NUM_EXPERTS, D), jnp.float32) * scale, 'w1': jax.random.normal(ks[2], (NUM_EXPERTS, D, D), jnp.float32) * scale, 'b1': jnp.zeros((NUM_EXPERTS, D), jnp.float32), 'w2': jax.random.normal(ks[3], (NUM_EXPERTS, D, D), jnp.float32) * scale, 'b2': jnp.zeros((NUM_EXPERTS, D), jnp.float32)}
    _L1_ffn_all = _L1_ffn_setup()
    _L1_ffn_in = {k: v for k, v in _L1_ffn_all.items() if k in ('router_w', 'w1', 'b1', 'w2', 'b2')}
    del _L1_ffn_all
    return {'x': x, 'L0_tok_W': _L0_tok_in['W'], 'L0_tok_b': _L0_tok_in['b'], 'L0_tok_gamma': _L0_tok_in['gamma'], 'L0_tok_beta': _L0_tok_in['beta'], 'L0_attn_conv_w': _L0_attn_in['conv_w'], 'L0_attn_conv_b': _L0_attn_in['conv_b'], 'L0_attn_sqrt_beta': _L0_attn_in['sqrt_beta'], 'L0_attn_ln_w': _L0_attn_in['ln_w'], 'L0_attn_ln_b': _L0_attn_in['ln_b'], 'L0_attn_q_w': _L0_attn_in['q_w'], 'L0_attn_q_b': _L0_attn_in['q_b'], 'L0_attn_k_w': _L0_attn_in['k_w'], 'L0_attn_k_b': _L0_attn_in['k_b'], 'L0_attn_v_w': _L0_attn_in['v_w'], 'L0_attn_v_b': _L0_attn_in['v_b'], 'L0_attn_out_w': _L0_attn_in['out_w'], 'L0_attn_out_b': _L0_attn_in['out_b'], 'L0_attn_gammas': _L0_attn_in['gammas'], 'L0_ffn_W_fx': _L0_ffn_in['W_fx'], 'L0_ffn_b_fx': _L0_ffn_in['b_fx'], 'L0_ffn_W_x': _L0_ffn_in['W_x'], 'L0_ffn_b_x': _L0_ffn_in['b_x'], 'L0_ffn_W_slice': _L0_ffn_in['W_slice'], 'L0_ffn_b_slice': _L0_ffn_in['b_slice'], 'L0_ffn_W_q': _L0_ffn_in['W_q'], 'L0_ffn_W_k': _L0_ffn_in['W_k'], 'L0_ffn_W_v': _L0_ffn_in['W_v'], 'L0_ffn_W_out': _L0_ffn_in['W_out'], 'L0_ffn_b_out': _L0_ffn_in['b_out'], 'L0_ffn_temperature': _L0_ffn_in['temperature'], 'L1_attn_w_qkv': _L1_attn_in['w_qkv'], 'L1_attn_w_proj': _L1_attn_in['w_proj'], 'L1_attn_b_proj': _L1_attn_in['b_proj'], 'L1_attn_rel_bias': _L1_attn_in['rel_bias'], 'L1_ffn_router_w': _L1_ffn_in['router_w'], 'L1_ffn_w1': _L1_ffn_in['w1'], 'L1_ffn_b1': _L1_ffn_in['b1'], 'L1_ffn_w2': _L1_ffn_in['w2'], 'L1_ffn_b2': _L1_ffn_in['b2']}

def reference(x, L0_tok_W, L0_tok_b, L0_tok_gamma, L0_tok_beta, L0_attn_conv_w, L0_attn_conv_b, L0_attn_sqrt_beta, L0_attn_ln_w, L0_attn_ln_b, L0_attn_q_w, L0_attn_q_b, L0_attn_k_w, L0_attn_k_b, L0_attn_v_w, L0_attn_v_b, L0_attn_out_w, L0_attn_out_b, L0_attn_gammas, L0_ffn_W_fx, L0_ffn_b_fx, L0_ffn_W_x, L0_ffn_b_x, L0_ffn_W_slice, L0_ffn_b_slice, L0_ffn_W_q, L0_ffn_W_k, L0_ffn_W_v, L0_ffn_W_out, L0_ffn_b_out, L0_ffn_temperature, L1_attn_w_qkv, L1_attn_w_proj, L1_attn_b_proj, L1_attn_rel_bias, L1_ffn_router_w, L1_ffn_w1, L1_ffn_b1, L1_ffn_w2, L1_ffn_b2):
    import jax
    import jax.numpy as jnp

    def _L0_tok_ref(x, W, b, gamma, beta):
        import jax, jax.numpy as jnp
        import numpy as np
        PATCH = 16
        STRIDE = 8
        EPS = 1e-05
        B, S, F = x.shape
        starts = jnp.arange(0, S - PATCH + 1, STRIDE)
        idx = starts[:, None] + jnp.arange(PATCH)[None, :]
        patches = x[:, idx, :].reshape(B, idx.shape[0], PATCH * F)
        y = jnp.einsum('bpi,di->bpd', patches, W) + b
        mu = jnp.mean(y, axis=-1, keepdims=True)
        var = jnp.mean(jnp.square(y - mu), axis=-1, keepdims=True)
        return (y - mu) * jax.lax.rsqrt(var + EPS) * gamma + beta

    def _L0_attn_ref(x, conv_w, conv_b, sqrt_beta, ln_w, ln_b, q_w, q_b, k_w, k_b, v_w, v_b, out_w, out_b, gammas):
        import jax, jax.numpy as jnp
        import numpy as np
        B, S, D, H, K = (8, 256, 64, 8, 5)
        DK = D // H

        def _layernorm(x, w, b, eps=1e-12):
            m = x.mean(-1, keepdims=True)
            v = ((x - m) ** 2).mean(-1, keepdims=True)
            return w * (x - m) / jnp.sqrt(v + eps) + b

        def _forward(x, conv_w, conv_b, sqrt_beta, ln_w, ln_b, q_w, q_b, k_w, k_b, v_w, v_b, out_w, out_b, gammas):
            b, s, d = x.shape
            h = gammas.shape[0]
            dk = d // h
            xc = x.transpose(0, 2, 1)
            low = jax.lax.conv_general_dilated(xc, conv_w, window_strides=(1,), padding=[(K - 1, 0)], dimension_numbers=('NCH', 'OIH', 'NCH'))
            low = low.transpose(0, 2, 1) + conv_b
            high = x - low
            hid = _layernorm(low + sqrt_beta ** 2 * high + x, ln_w, ln_b)

            def proj(w, bb):
                return (hid @ w.T + bb).reshape(b, s, h, dk).transpose(0, 2, 1, 3)
            q, k, v = (proj(q_w, q_b), proj(k_w, k_b), proj(v_w, v_b))
            scores = jnp.einsum('bhqd,bhkd->bhqk', q, k) / jnp.sqrt(jnp.float32(dk))
            mask = jnp.tril(jnp.ones((s, s), bool))
            p_ = jax.nn.softmax(jnp.where(mask, scores, -1e+32), axis=-1) * mask
            distcum = jnp.cumsum(p_, axis=-1)
            disttotal = p_.sum(-1, keepdims=True)
            idx = jnp.arange(s)
            pos = jnp.abs(idx[:, None] - idx[None, :]).astype(jnp.float32)
            dist = jax.lax.stop_gradient(jnp.sqrt(jnp.clip((disttotal - distcum) * pos, 0.0)))
            gamma = -jax.nn.softplus(gammas)[None]
            total_effect = jnp.clip(jnp.exp(dist * gamma), 1e-05, 100000.0)
            scores = jnp.where(mask, scores * total_effect, -1e+32)
            p = jax.nn.softmax(scores, axis=-1)
            p = p.at[:, :, 0, :].set(0.0)
            out = jnp.einsum('bhqk,bhkd->bhqd', p, v)
            out = out.transpose(0, 2, 1, 3).reshape(b, s, d)
            return out @ out_w.T + out_b
        return _forward(x, conv_w, conv_b, sqrt_beta, ln_w, ln_b, q_w, q_b, k_w, k_b, v_w, v_b, out_w, out_b, gammas)

    def _L0_ffn_ref(x, W_fx, b_fx, W_x, b_x, W_slice, b_slice, W_q, W_k, W_v, W_out, b_out, temperature):
        import jax, jax.numpy as jnp
        import numpy as np
        DIM = 64
        H = 8
        D = 64
        G = 64
        INNER = H * D
        SCALE = D ** (-0.5)
        B, N, _ = x.shape
        fx_mid = (x @ W_fx + b_fx).reshape(B, N, H, D).transpose(0, 2, 1, 3)
        x_mid = (x @ W_x + b_x).reshape(B, N, H, D).transpose(0, 2, 1, 3)
        temp = jnp.clip(temperature, 0.1, 5.0)
        slice_weights = jax.nn.softmax((x_mid @ W_slice + b_slice) / temp, axis=-1)
        slice_norm = slice_weights.sum(axis=2)
        slice_token = jnp.einsum('bhnc,bhng->bhgc', fx_mid, slice_weights)
        slice_token = slice_token / (slice_norm[..., None] + 1e-05)
        q = slice_token @ W_q
        k = slice_token @ W_k
        v = slice_token @ W_v
        attn = jax.nn.softmax(jnp.einsum('bhgc,bhkc->bhgk', q, k) * SCALE, axis=-1)
        out_slice = jnp.einsum('bhgk,bhkc->bhgc', attn, v)
        out_x = jnp.einsum('bhgc,bhng->bhnc', out_slice, slice_weights)
        out_x = out_x.transpose(0, 2, 1, 3).reshape(B, N, INNER)
        return out_x @ W_out + b_out

    def _L1_attn_ref(x, w_qkv, w_proj, b_proj, rel_bias):
        import jax, jax.numpy as jnp
        import numpy as np
        DIM = 64
        WS = 64
        H = 8
        HD = DIM // H
        SCALE = HD ** (-0.5)
        B, L, C = x.shape
        pad_len = (WS - L % WS) % WS
        if pad_len > 0:
            x = jnp.pad(x, ((0, 0), (0, pad_len), (0, 0)))
        padded_L = x.shape[1]
        nw = padded_L // WS
        xw = x.reshape(B, nw, WS, C)
        qkv = jnp.einsum('bnwc,oc->bnwo', xw, w_qkv)
        qkv = qkv.reshape(B, nw, WS, 3, H, HD)
        q = jnp.transpose(qkv[..., 0, :, :], (0, 1, 3, 2, 4))
        k = jnp.transpose(qkv[..., 1, :, :], (0, 1, 3, 2, 4))
        v = jnp.transpose(qkv[..., 2, :, :], (0, 1, 3, 2, 4))
        attn = jnp.einsum('bnhqd,bnhkd->bnhqk', q, k) * SCALE
        pos = jnp.arange(WS)
        rel_idx = pos[None, :] - pos[:, None] + WS - 1
        attn = attn + rel_bias[rel_idx]
        attn = jax.nn.softmax(attn, axis=-1)
        out = jnp.einsum('bnhqk,bnhkd->bnhqd', attn, v)
        out = jnp.transpose(out, (0, 1, 3, 2, 4)).reshape(B, nw, WS, C)
        out = jnp.einsum('bnwc,oc->bnwo', out, w_proj) + b_proj
        out = out.reshape(B, padded_L, C)
        if pad_len > 0:
            out = out[:, :L, :]
        return out

    def _L1_ffn_ref(input_embeddings, router_w, w1, b1, w2, b2):
        import jax, jax.numpy as jnp
        import numpy as np
        NUM_EXPERTS = 8
        TOP_K = 2
        B, S, D = (8, 2048, 64)

        def _moe(tokens, router_w, w1, b1, w2, b2):
            N = tokens.shape[0]
            E = router_w.shape[0]
            logits = tokens.astype(jnp.float32) @ router_w.astype(jnp.float32).T
            probs = jax.nn.softmax(logits, axis=-1)
            rw, re = jax.lax.top_k(probs, TOP_K)
            if TOP_K > 1:
                rw = rw / jnp.maximum(rw.sum(-1, keepdims=True), 1e-12)
            rw = rw.astype(tokens.dtype)
            combine = jnp.zeros((N, E), tokens.dtype).at[jnp.arange(N)[:, None], re].set(rw)
            out = tokens
            for e in range(E):
                h = jax.nn.gelu(tokens @ w1[e] + b1[e], approximate=False)
                y = h @ w2[e] + b2[e]
                out = out + combine[:, e:e + 1] * y
            return out
        b, s, d = input_embeddings.shape
        tokens = input_embeddings.reshape(b * s, d)
        return _moe(tokens, router_w, w1, b1, w2, b2).reshape(b, s, d)
    h = _L0_tok_ref(x, L0_tok_W, L0_tok_b, L0_tok_gamma, L0_tok_beta)
    h = h + _L0_attn_ref(_layernorm(h, axis=-1), L0_attn_conv_w, L0_attn_conv_b, L0_attn_sqrt_beta, L0_attn_ln_w, L0_attn_ln_b, L0_attn_q_w, L0_attn_q_b, L0_attn_k_w, L0_attn_k_b, L0_attn_v_w, L0_attn_v_b, L0_attn_out_w, L0_attn_out_b, L0_attn_gammas)
    h = h + _L0_ffn_ref(_layernorm(h, axis=-1), L0_ffn_W_fx, L0_ffn_b_fx, L0_ffn_W_x, L0_ffn_b_x, L0_ffn_W_slice, L0_ffn_b_slice, L0_ffn_W_q, L0_ffn_W_k, L0_ffn_W_v, L0_ffn_W_out, L0_ffn_b_out, L0_ffn_temperature)
    h = h + _L1_attn_ref(_layernorm(h, axis=-1), L1_attn_w_qkv, L1_attn_w_proj, L1_attn_b_proj, L1_attn_rel_bias)
    h = h + _L1_ffn_ref(_layernorm(h, axis=-1), L1_ffn_router_w, L1_ffn_w1, L1_ffn_b1, L1_ffn_w2, L1_ffn_b2)
    return h

_drawn_inputs = setup_inputs


def setup_inputs(seed=0):
    import zlib

    import numpy as np

    out = dict(_drawn_inputs(seed))
    spreads = {'L0_tok_gamma': (1.0, 0.2),
     'L0_tok_beta': (0.0, 0.1),
     'L0_attn_conv_b': (0.0, 0.311),
     'L0_attn_ln_w': (1.0, 0.6),
     'L0_attn_ln_b': (0.0, 0.1),
     'L0_attn_q_b': (0.0, 0.8),
     'L0_attn_k_b': (0.0, 2.0),
     'L0_attn_v_b': (0.0, 0.1),
     'L0_attn_out_b': (0.0, 0.1),
     'L0_ffn_b_fx': (0.0, 0.1),
     'L0_ffn_b_x': (0.0, 0.435),
     'L0_ffn_b_slice': (0.0, 0.434),
     'L0_ffn_b_out': (0.0, 0.1),
     'L0_ffn_temperature': (0.5, 0.6),
     'L1_attn_b_proj': (0.0, 0.1),
     'L1_ffn_b1': (0.0, 0.364),
     'L1_ffn_b2': (0.0, 0.1)}
    factors = {'L0_attn_q_w': 8.0,
     'L0_attn_k_w': 8.0,
     'L0_attn_gammas': 8.0,
     'L0_ffn_W_q': 3.559,
     'L0_ffn_W_k': 3.434,
     'L1_attn_rel_bias': 6.575}
    for name, (base, spread) in spreads.items():
        noise = np.random.default_rng([zlib.crc32(name.encode()), seed]).standard_normal(out[name].shape)
        drawn = base * np.exp(spread * noise) if base else spread * noise
        out[name] = jnp.asarray(drawn.astype(out[name].dtype))
    for name, factor in factors.items():
        out[name] = (out[name] * factor).astype(out[name].dtype)
    return out
```

```python
from contextlib import ExitStack

import concourse.bass as bass
from concourse import mybir

P = 128
B = 16
SEQ, FEAT = 2048, 16
PATCH, STRIDE = 16, 8
CHUNK = STRIDE * FEAT
NCHUNK = SEQ // STRIDE
TOK = NCHUNK - 1
D = 64
H = 8
DK = D // H
TT = 2
ROWS = TT * P
G = 64
INNER = H * D
E = 8
WS = 64
TAPS = 5
STEPS_TO_ABS = 15
NEG = -1e30

F32 = mybir.dt.float32
ALU = mybir.AluOpType
ACT = mybir.ActivationFunctionType
X = mybir.AxisListType.X

QB = P // H
NQ = ROWS // QB
SPAN = [QB * (j + 1) for j in range(NQ)]
BANKS = [[15, 14, 0], [13, 12, 4], [11, 10, 8], [9, 7, 6, 5], [3, 2, 1]]
OFF, BANK_OFF = {}, []
_at = 0
for _bank in BANKS:
    BANK_OFF.append(_at)
    for _j in _bank:
        OFF[_j] = _at
        _at += SPAN[_j]
PACKED = _at
ORDER = [j for bank in BANKS for j in bank]
HALF = NQ // 2
WIDE_OFF = [P * j if j < HALF else P * HALF + 2 * P * (j - HALF) for j in range(NQ)]
WIDE = P * HALF + 2 * P * HALF


def weight_columns():
    sizes = [
        ("tok_w0", P, D), ("tok_w1", P, D), ("tok_b", P, D), ("tok_gamma", P, D), ("tok_beta", P, D),
        ("ident", P, P), ("pad_mask", P, TT), ("head_mask", D, H),
        ("conv", D, TAPS * D), ("conv_b", P, D), ("sqrt_beta", P, D),
        ("ln_w", D, 1), ("ln_b", D, 1), ("ln_b_wide", D, P), ("q_w", D, D), ("k_w", D, D), ("v_w", D, D),
        ("q_b", D, 1), ("k_b", P, 1), ("v_b", P, D), ("out_w", D, D), ("out_b", P, D), ("gammas", P, 1),
        ("fx_w", D + 1, INNER), ("x_w", D, H * D), ("x_b", D, H), ("slice_w", D, G), ("slice_b", D + 1, G),
        ("temp", P, H), ("fq_w", D, D), ("fk_w", D, D), ("fv_w", D, D), ("fout_w", D, H * D), ("fout_b", P, D),
        ("a_q", D, D), ("a_k", D, D), ("a_v", D, D), ("a_proj", D, D), ("a_proj_b", P, D), ("rel", P, WS),
        ("router", D, E), ("w1", D, E * D), ("b1", P, E // 2), ("w2", P, (E // 2) * D), ("b2", E, D),
        ("expand", E, (E // 2) * P), ("last_key", P, QB),
    ]
    cols, at = {}, 0
    for name, rows, width in sizes:
        cols[name] = (at, rows, width)
        at += width
    return cols, at


class Steps:

    def __init__(self, engine, semaphore, per_turn=0, turn=0):
        self.engine, self.semaphore, self.per_turn, self.turn, self.n = engine, semaphore, per_turn, turn, 0

    def step(self, instruction):
        self.n += 1
        instruction.then_inc(self.semaphore, 1)
        return self.n

    def wait(self, n=None):
        n = self.n if n is None else n
        self.engine.wait_ge(self.semaphore, self.turn * self.per_turn + n if self.per_turn else n)

    def link(self, instruction):
        self.step(instruction)
        self.wait()

    def end(self):
        assert not self.per_turn or self.n == self.per_turn, self.n


def bcast(ap, shape):
    return ap.to_broadcast(shape)


def build(nc, x_chunks, weights, packed_tables, out):
    cols, _ = weight_columns()
    top = ExitStack()
    with top:
        def sem(name):
            return top.enter_context(nc.semaphore(name))

        def sb(ctx, name, shape):
            return ctx.enter_context(nc.sbuf_tensor(name, shape, F32))

        W = sb(top, "W", [P, sum(c[2] for c in cols.values())])

        def w(name, rows=None):
            at, r, n = cols[name]
            return W[0:(rows or r), at:at + n]

        h_all = sb(top, "h_all", [P, B * TT, D])
        rstd = sb(top, "rstd", [P, B * TT])
        cen_ctx = ExitStack()
        cen = sb(cen_ctx, "cen_a", [P, B * TT, D])
        psum = top.enter_context(nc.psum_tensor("psum", [P, 8, 512], F32))
        ident = w("ident")

        loaded = sem("weights_loaded")

        def layer_stats(tag, src, cen, eps):
            with ExitStack() as ctx:
                sq = sb(ctx, f"{tag}_sq", [P, B * TT, D])
                mean = sb(ctx, f"{tag}_mean", [P, B * TT])
                var = sb(ctx, f"{tag}_var", [P, B * TT])
                std = sb(ctx, f"{tag}_std", [P, B * TT])
                centred, squared = sem(f"{tag}_centred"), sem(f"{tag}_squared")
                vector_steps, has_var, has_std = sem(f"{tag}_vector_steps"), sem(f"{tag}_has_var"), sem(f"{tag}_has_std")
                nch, per = 4, B * TT // 4
                with nc.Block() as block:
                    @block.vector
                    def _(dve):
                        with dve.Fori(0, nch) as c:
                            rows = bass.ds(c * per, per)
                            st = Steps(dve, vector_steps, 2, c)
                            st.link(nc.vector.tensor_reduce(mean[:, rows], src[:, rows, :], X, ALU.add))
                            st.link(nc.vector.tensor_scalar(mean[:, rows], mean[:, rows], 1.0 / D, None, ALU.mult))
                            nc.vector.tensor_tensor(cen[:, rows, :], src[:, rows, :],
                                                    bcast(mean[:, rows][:, :, None], [P, per, D]),
                                                    ALU.subtract).then_inc(centred, 1)
                            st.end()
                        with dve.Fori(0, nch) as c:
                            rows = bass.ds(c * per, per)
                            dve.wait_ge(squared, c + 1)
                            nc.vector.tensor_reduce(var[:, rows], sq[:, rows, :], X, ALU.add).then_inc(vector_steps, 1)
                        st = Steps(dve, vector_steps)
                        st.n = 3 * nch
                        st.wait()
                        nc.vector.tensor_scalar(var[:], var[:], 1.0 / D, eps, ALU.mult, ALU.add).then_inc(has_var, 1)
                        dve.wait_ge(has_std, 1)
                        st.link(nc.vector.reciprocal(rstd[:], std[:]))
                        st.link(nc.vector.tensor_tensor(
                            rstd[:].rearrange("p (b t) -> p b t", t=TT), rstd[:].rearrange("p (b t) -> p b t", t=TT),
                            bcast(w("pad_mask")[:, None, :], [P, B, TT]), ALU.mult))

                    @block.scalar
                    def _(act):
                        with act.Fori(0, nch) as c:
                            rows = bass.ds(c * per, per)
                            act.wait_ge(centred, c + 1)
                            nc.scalar.activation(sq[:, rows, :], cen[:, rows, :], ACT.Square).then_inc(squared, 1)
                        act.wait_ge(has_var, 1)
                        nc.scalar.activation(std[:], var[:], ACT.Sqrt).then_inc(has_std, 1)

        with ExitStack() as ctx:
            chunks = sb(ctx, "chunks", [P, 2, NCHUNK + 1])
            x_landed = [sem(f"x_landed{u}") for u in range(2)]
            x_used, y_ready, y_used = sem("x_used"), sem("y_ready"), sem("y_used")
            with nc.Block() as block:
                @block.sync
                def _(sp):
                    sp.dma_start(W[:], weights).then_inc(loaded, 16)
                    sp.sem_inc(x_used, 2)
                    with sp.Fori(0, B // 2) as i:
                        for u in range(2):
                            sp.wait_ge(x_used, 2 * i + u + 1)
                            sp.dma_start(chunks[:, u, :], x_chunks[:, bass.ds(2 * i + u, 1), :]
                                         .rearrange("p b c -> p (b c)")).then_inc(x_landed[u], 16)

                @block.tensor
                def _(pe):
                    pe.wait_ge(loaded, 16)
                    pe.sem_inc(y_used, 2)
                    with pe.Fori(0, B // 2) as i:
                        for u in range(2):
                            pe.wait_ge(x_landed[u], i * 16 + 16)
                            pe.wait_ge(y_used, 2 * i + u + 1)
                            for t in range(TT):
                                for half in range(2):
                                    last = nc.tensor.matmul(psum[:, u, t * D:(t + 1) * D],
                                                            chunks[:, u, t * P + half:t * P + half + P],
                                                            w(f"tok_w{half}"), start=(half == 0), stop=(half == 1))
                            last.then_inc(y_ready, 1)
                            pe.wait_ge(y_ready, 2 * i + u + 1)
                            pe.sem_inc(x_used, 1)

                @block.vector
                def _(dve):
                    dve.wait_ge(loaded, 16)
                    with dve.Fori(0, B // 2) as i:
                        for u in range(2):
                            dve.wait_ge(y_ready, 2 * i + u + 1)
                            nc.vector.tensor_tensor(h_all[:, bass.ds((2 * i + u) * TT, TT), :],
                                                    psum[:, u, 0:TT * D].rearrange("p (t d) -> p t d", t=TT),
                                                    bcast(w("tok_b")[:, None, :], [P, TT, D]),
                                                    ALU.add).then_inc(y_used, 1)
        layer_stats("tok_ln", h_all, cen, 1e-5)
        with ExitStack() as ctx:
            scaled = sem("tok_scaled")
            with nc.Block() as block:
                @block.vector
                def _(dve):
                    st = Steps(dve, scaled)
                    full = [P, B * TT, D]
                    st.link(nc.vector.tensor_tensor(h_all[:], cen[:], bcast(rstd[:][:, :, None], full), ALU.mult))
                    st.link(nc.vector.tensor_tensor(h_all[:], h_all[:], bcast(w("tok_gamma")[:, None, :], full), ALU.mult))
                    st.link(nc.vector.tensor_tensor(h_all[:], h_all[:], bcast(w("tok_beta")[:, None, :], full), ALU.add))

        cen_ctx.close()
        conv_x = sb(top, "conv_x", [D, TAPS, D])
        conv_bias = sb(top, "conv_bias", [P, D])
        qkv_x = sb(top, "qkv_x", [D, 3, D])
        q_bias, k_bias = sb(top, "q_bias", [D, 1]), sb(top, "k_bias", [P, 1])
        v_bias = sb(top, "v_bias", [P, D])
        gamma_sq = sb(top, "gamma_sq", [P, 1])
        soft = sb(top, "soft", [P, 4])
        keep_low, keep_high = sb(top, "keep_low", [P, D]), sb(top, "keep_high", [P, D])
        diag_high = sb(top, "diag_high", [D, D])
        w_vector, w_scalar, w_tensor = sem("w_vector"), sem("w_scalar"), sem("w_tensor")
        with nc.Block() as block:
            @block.vector
            def _(dve):
                st = Steps(dve, w_vector)
                v = nc.vector
                st.link(v.tensor_tensor(keep_high[:], w("sqrt_beta"), w("sqrt_beta"), ALU.mult))
                st.link(v.tensor_scalar(keep_low[:], keep_high[:], -1.0, 1.0, ALU.mult, ALU.add))
                st.link(v.tensor_scalar(keep_high[:], keep_high[:], 1.0, None, ALU.add))
                st.step(v.tensor_tensor(conv_bias[:], w("conv_b"), keep_low[:], ALU.mult))
                st.step(v.tensor_tensor(diag_high[:], ident[0:D, 0:D], keep_high[0:D, :], ALU.mult))
                st.step(v.tensor_tensor(conv_x[:], w("conv").rearrange("p (k d) -> p k d", k=TAPS),
                                        bcast(keep_low[0:D, None, :], [D, TAPS, D]), ALU.mult))
                st.wait()
                st.step(v.tensor_tensor(conv_x[:, TAPS - 1, :], conv_x[:, TAPS - 1, :], diag_high[:], ALU.add))
                for n, name in enumerate(("q_w", "k_w", "v_w")):
                    st.step(v.tensor_scalar(qkv_x[:, n, :], w(name), w("ln_w"), None, ALU.mult))
                dve.wait_ge(w_tensor, 3)
                st.step(v.tensor_tensor(q_bias[:], psum[0:D, 0, 0:1], w("q_b"), ALU.add))
                st.step(v.tensor_tensor(k_bias[D:P], psum[D:P, 1, 0:1], w("k_b")[D:P], ALU.add))
                st.step(v.tensor_tensor(v_bias[:], psum[:, 2, 0:D], w("v_b"), ALU.add))
                st.link(v.tensor_scalar(soft[:, 0:1], w("gammas"), -1.0, None, ALU.mult))
                at_abs = st.step(v.tensor_tensor(soft[:, 1:2], soft[:, 0:1], w("gammas"), ALU.min))
                assert at_abs == STEPS_TO_ABS
                st.step(v.tensor_scalar(soft[:, 2:3], w("gammas"), 0.0, None, ALU.max))
                dve.wait_ge(w_scalar, 2)
                st.wait()
                st.link(v.tensor_tensor(soft[:, 2:3], soft[:, 2:3], soft[:, 1:2], ALU.add))
                st.link(v.tensor_tensor(gamma_sq[:], soft[:, 2:3], soft[:, 2:3], ALU.mult))

            @block.scalar
            def _(act):
                act.wait_ge(w_vector, STEPS_TO_ABS)
                nc.scalar.activation(soft[:, 3:4], soft[:, 1:2], ACT.Exp).then_inc(w_scalar, 1)
                act.wait_ge(w_scalar, 1)
                nc.scalar.activation(soft[:, 1:2], soft[:, 3:4], ACT.Ln, bias=1.0).then_inc(w_scalar, 1)

            @block.tensor
            def _(pe):
                nc.tensor.matmul(psum[0:D, 0, 0:1], w("q_w"), w("ln_b"), start=True, stop=True).then_inc(w_tensor, 1)
                nc.tensor.matmul(psum[D:P, 1, 0:1], w("k_w"), w("ln_b"), start=True, stop=True).then_inc(w_tensor, 1)
                nc.tensor.matmul(psum[:, 2, 0:D], w("ln_b_wide"), w("v_w"), start=True, stop=True).then_inc(w_tensor, 1)

        waited_apart = {}

        def wait_apart(engine):
            name = f"waited_apart_{engine.engine.name}"
            if name not in waited_apart:
                waited_apart[name] = sem(name)
            engine.sem_inc(waited_apart[name], 1)

        def seq_rows(ap, b):
            return ap[:, bass.ds(b * TT, TT), :]

        def two_tiles(ap):
            return ap.rearrange("p (t d) -> p t d", t=TT)

        class Signal:

            def __init__(self, name, each=1):
                self.each, self.sem = each, sem(name)

            def done(self, b, n=None, before=0):
                return (b + 2 - before) * self.each + (self.each if n is None else n + 1)

            def event(self, b, n, before):
                return (b + 2) * self.each + n + 1 - before

        def open_signals(sp, signals):
            for s in signals:
                sp.sem_inc(s.sem, 2 * s.each)

        def normed(stage, u, b, cen):
            return nc.vector.tensor_tensor(
                stage[:, u], seq_rows(cen, b),
                bcast(rstd[:, bass.ds(b * TT, TT)][:, :, None], [P, TT, D]), ALU.mult)

        def transposed_rows(bank, stage, u):
            wait_apart(nc.tensor)
            for t in range(TT):
                last = nc.tensor.transpose(psum[0:D, bank, t * P:(t + 1) * P], stage[:, u, t, :], ident)
            return last

        attn_ctx = ExitStack()
        QK = sb(attn_ctx, "QK", [P, B * ROWS])
        QT, KT = QK[0:D], QK[D:P]
        V = sb(attn_ctx, "V", [P, B * TT, D])
        cen_ctx = ExitStack()
        cen = sb(cen_ctx, "cen_b", [P, B * TT, D])

        with ExitStack() as ctx:
            z = sb(ctx, "z", [P, B * TT, D])
            layer_stats("conv_ln", h_all, cen, 1e-5)
            with ExitStack() as inner:
                stage = sb(inner, "conv_stage", [P, 2, TT, D])
                xT = sb(inner, "conv_xT", [D, 2, TAPS - 1 + ROWS])
                xn_ready, xT_ready, xT_copied = Signal("conv_xn_ready"), Signal("conv_xT_ready"), Signal("conv_xT_copied")
                z_ready, z_copied = Signal("conv_z_ready"), Signal("conv_z_copied")
                padded = sem("conv_padded")
                with nc.Block() as block:
                    @block.sync
                    def _(sp):
                        open_signals(sp, [xn_ready, xT_ready, xT_copied, z_ready, z_copied])

                    @block.vector
                    def _(dve):
                        nc.vector.memset(xT[:, :, 0:TAPS - 1], 0.0).then_inc(padded, 1)
                        with dve.Fori(0, B // 2) as i:
                            for u in range(2):
                                b = 2 * i + u
                                dve.wait_ge(xT_ready.sem, xT_ready.done(b, before=2))
                                normed(stage, u, b, cen).then_inc(xn_ready.sem, 1)
                            for u in range(2):
                                b = 2 * i + u
                                dve.wait_ge(z_ready.sem, z_ready.done(b))
                                nc.vector.tensor_tensor(
                                    seq_rows(z, b), two_tiles(psum[:, 2 + u, 0:TT * D]),
                                    bcast(conv_bias[:, None, :], [P, TT, D]), ALU.add).then_inc(z_copied.sem, 1)

                    @block.scalar
                    def _(act):
                        with act.Fori(0, B // 2) as i:
                            for u in range(2):
                                b = 2 * i + u
                                act.wait_ge(xT_ready.sem, xT_ready.done(b))
                                act.wait_ge(z_ready.sem, z_ready.done(b, before=2))
                                nc.scalar.activation(
                                    xT[:, u, TAPS - 1:], psum[0:D, u, 0:ROWS], ACT.Copy).then_inc(xT_copied.sem, 1)

                    @block.tensor
                    def _(pe):
                        pe.wait_ge(padded, 1)
                        with pe.Fori(0, B // 2) as i:
                            for u in range(2):
                                b = 2 * i + u
                                pe.wait_ge(xn_ready.sem, xn_ready.done(b))
                                pe.wait_ge(xT_copied.sem, xT_copied.done(b, before=2))
                                transposed_rows(u, stage, u).then_inc(xT_ready.sem, 1)
                            for u in range(2):
                                b = 2 * i + u
                                pe.wait_ge(xT_copied.sem, xT_copied.done(b))
                                pe.wait_ge(z_copied.sem, z_copied.done(b, before=2))
                                for t in range(TT):
                                    for k in range(TAPS):
                                        last = nc.tensor.matmul(psum[:, 2 + u, t * D:(t + 1) * D],
                                                                xT[:, u, t * P + k:t * P + k + P], conv_x[:, k, :],
                                                                start=(k == 0), stop=(k == TAPS - 1))
                                last.then_inc(z_ready.sem, 1)

            layer_stats("qkv_ln", z, cen, 1e-12)
            with ExitStack() as inner:
                stage = sb(inner, "qkv_stage", [P, 2, TT, D])
                zT = sb(inner, "qkv_zT", [D, 2, ROWS])
                zn_ready, zT_ready, zT_copied = Signal("qkv_zn_ready"), Signal("qkv_zT_ready"), Signal("qkv_zT_copied")
                qkv_ready, qv_copied, k_copied = Signal("qkv_ready"), Signal("qv_copied"), Signal("k_copied")
                with nc.Block() as block:
                    @block.sync
                    def _(sp):
                        open_signals(sp, [zn_ready, zT_ready, zT_copied, qkv_ready, qv_copied, k_copied])

                    @block.vector
                    def _(dve):
                        with dve.Fori(0, B // 2) as i:
                            for u in range(2):
                                b = 2 * i + u
                                dve.wait_ge(zT_ready.sem, zT_ready.done(b, before=2))
                                normed(stage, u, b, cen).then_inc(zn_ready.sem, 1)
                            for u in range(2):
                                b = 2 * i + u
                                dve.wait_ge(qkv_ready.sem, qkv_ready.done(b))
                                nc.vector.tensor_scalar(QT[:, bass.ds(b * ROWS, ROWS)], psum[0:D, 2 + u, 0:ROWS],
                                                        q_bias[:], DK ** -0.5, ALU.add, ALU.mult)
                                nc.vector.tensor_tensor(
                                    seq_rows(V, b), two_tiles(psum[:, 4 + u, 0:TT * D]),
                                    bcast(v_bias[:, None, :], [P, TT, D]), ALU.add).then_inc(qv_copied.sem, 1)

                    @block.scalar
                    def _(act):
                        with act.Fori(0, B // 2) as i:
                            for u in range(2):
                                b = 2 * i + u
                                act.wait_ge(zT_ready.sem, zT_ready.done(b))
                                act.wait_ge(qkv_ready.sem, qkv_ready.done(b, before=2))
                                nc.scalar.activation(zT[:, u], psum[0:D, u, 0:ROWS], ACT.Copy).then_inc(zT_copied.sem, 1)
                            for u in range(2):
                                b = 2 * i + u
                                act.wait_ge(qkv_ready.sem, qkv_ready.done(b))
                                nc.scalar.activation(
                                    KT[:, bass.ds(b * ROWS, ROWS)], psum[D:P, 2 + u, 0:ROWS],
                                    ACT.Identity, bias=k_bias[D:P]).then_inc(k_copied.sem, 1)

                    @block.tensor
                    def _(pe):
                        with pe.Fori(0, B // 2) as i:
                            for u in range(2):
                                b = 2 * i + u
                                pe.wait_ge(zn_ready.sem, zn_ready.done(b))
                                pe.wait_ge(zT_copied.sem, zT_copied.done(b, before=2))
                                transposed_rows(u, stage, u).then_inc(zT_ready.sem, 1)
                            for u in range(2):
                                b = 2 * i + u
                                pe.wait_ge(zT_copied.sem, zT_copied.done(b))
                                pe.wait_ge(qv_copied.sem, qv_copied.done(b, before=2))
                                pe.wait_ge(k_copied.sem, k_copied.done(b, before=2))
                                wait_apart(pe)
                                for n in range(2):
                                    nc.tensor.matmul(psum[n * D:(n + 1) * D, 2 + u, 0:ROWS], qkv_x[:, n, :],
                                                     zT[:, u], start=True, stop=True)
                                for t in range(TT):
                                    last = nc.tensor.matmul(psum[:, 4 + u, t * D:(t + 1) * D],
                                                            zT[:, u, t * P:(t + 1) * P], qkv_x[:, 2, :],
                                                            start=True, stop=True)
                                last.then_inc(qkv_ready.sem, 1)

        cen_ctx.close()
        with ExitStack() as ctx:
            tables = sb(ctx, "tables_sb", [P, 2, PACKED])
            distance, no_reset = tables[:, 0], tables[:, 1]
            causal = sb(ctx, "causal", [P, 2 * P])
            Qd = sb(ctx, "Qd", [D, 2, NQ, H, QB])
            Kb = sb(ctx, "Kb", [D, 2, ROWS])
            VM_COLS = 2 * H * P
            Vm = sb(ctx, "Vm", [P, 2, VM_COLS + P])
            S = sb(ctx, "S", [P, 2, PACKED])
            Ex = sb(ctx, "Ex", [P, 2, PACKED + 1])
            PT = sb(ctx, "PT", [P, 2, WIDE])
            Y = PT[:, :, 0:PACKED]
            S2 = sb(ctx, "S2", [P, 2, WIDE])
            top1, top2 = sb(ctx, "top1", [P, 2, NQ]), sb(ctx, "top2", [P, 2, NQ])
            neg_top, total = sb(ctx, "neg_top", [P, 2, NQ]), sb(ctx, "total", [P, 2, NQ])
            scale = sb(ctx, "scale", [P, 2, NQ])
            inv = sb(ctx, "inv", [D, 2, ROWS])
            oT = sb(ctx, "oT", [D, 2, ROWS])
            k_landed = [sem(f"k_landed{u}") for u in range(2)]
            NB = len(BANKS)
            tables_landed, prepared, pool_prepared = sem("tables_landed"), sem("prepared"), sem("pool_prepared")
            q_ready, v_ready, y_ready1 = Signal("qd_ready"), Signal("vm_ready"), Signal("dist_ready")
            s_ready, top_ready = Signal("s_ready", NB), Signal("top_ready", NB)
            e_ready, scan_ready, root_ready, te_ready = Signal("e_ready"), Signal("scan_ready"), Signal("root_ready"), Signal("te_ready")
            s2_ready, t_ready, p_ready = Signal("s2_ready", 2), Signal("t_ready", 3), Signal("p_ready", 3)
            pv_ready, o_ready, y_done, h_added = Signal("pv_ready"), Signal("o_ready"), Signal("proj_ready"), Signal("h_added")
            DVE_STEPS = 2 * (2 + 2 + 2)
            max_steps = sem("attn_max_steps")
            vector_steps = sem("attn_vector_steps")
            with nc.Block() as block:
                @block.sync
                def _(sp):
                    sp.dma_start(tables[:], packed_tables).then_inc(tables_landed, 16)
                    open_signals(sp, [q_ready, v_ready, y_ready1, s_ready, top_ready, e_ready, scan_ready, root_ready,
                              te_ready, s2_ready, t_ready, p_ready, pv_ready, o_ready, y_done, h_added])
                    with sp.Fori(0, B // 2) as i:
                        for u in range(2):
                            b = 2 * i + u
                            sp.wait_ge(s_ready.sem, s_ready.done(b, before=2))
                            sp.dma_start(Kb[:, u], KT[:, bass.ds(b * ROWS, ROWS)]).then_inc(k_landed[u], 16)

                @block.gpsimd
                def _(pool):
                    g = nc.gpsimd
                    g.memset(Vm[:], 0.0).then_inc(pool_prepared, 1)
                    pool.wait_ge(pool_prepared, 1)
                    for u in range(2):
                        for kb in range(2):
                            at = kb * H * P
                            ones = Vm[:, u, at + D:at + D + H * (P + DK)].rearrange("p (h s) -> p h s", h=H)[:, :, 0:DK]
                            last = g.memset(ones, 1.0)
                    last.then_inc(pool_prepared, 1)
                    pool.wait_ge(pool_prepared, 2)
                    pool.wait_ge(tables_landed, 16)
                    pool.wait_ge(prepared, 1)
                    with pool.Fori(0, B // 2) as i:
                        for u in range(2):
                            b = 2 * i + u
                            pool.wait_ge(s_ready.sem, s_ready.done(b, before=2))
                            qs = QT[:, bass.ds(b * ROWS, ROWS)].rearrange("p (j q) -> p j q", j=NQ)
                            g.tensor_tensor(
                                Qd[:, u], bcast(qs[:, :, None, :], [D, NQ, H, QB]),
                                bcast(w("head_mask")[:, None, :, None], [D, NQ, H, QB]), ALU.mult).then_inc(q_ready.sem, 1)
                            pool.wait_ge(pv_ready.sem, pv_ready.done(b, before=2))
                            for kb in range(2):
                                at = kb * H * P
                                mine = Vm[:, u, at:at + H * (P + DK)].rearrange("p (h s) -> p h s", h=H)[:, :, 0:DK]
                                last = g.tensor_copy(mine, V[:, bass.ds(b * TT + kb, 1), :]
                                                     .rearrange("p t (h d) -> p (t h) d", h=H))
                            last.then_inc(v_ready.sem, 1)
                        for u in range(2):
                            b = 2 * i + u
                            pool.wait_ge(scan_ready.sem, scan_ready.done(b))
                            pool.wait_ge(pv_ready.sem, pv_ready.done(b, before=2))
                            g.tensor_tensor(Y[:, u], Ex[:, u, 1:PACKED + 1], distance, ALU.mult).then_inc(y_ready1.sem, 1)

                @block.tensor
                def _(pe):
                    with pe.Fori(0, B // 2) as i:
                        for u in range(2):
                            b = 2 * i + u
                            pe.wait_ge(q_ready.sem, q_ready.done(b))
                            pe.wait_ge(k_landed[u], 16 * i + 16)
                            for n, bank in enumerate(BANKS):
                                pe.wait_ge(top_ready.sem, top_ready.event(b, n, before=2))
                                for j in bank:
                                    at = OFF[j] - BANK_OFF[n]
                                    last = nc.tensor.matmul(psum[:, (u * NB + n) % 2, at:at + SPAN[j]],
                                                            Qd[:, u, j].rearrange("p h q -> p (h q)"),
                                                            Kb[:, u, 0:SPAN[j]], start=True, stop=True)
                                last.then_inc(s_ready.sem, 1)
                        for u in range(2):
                            b = 2 * i + u
                            for c in range(3):
                                pe.wait_ge(s2_ready.sem, s2_ready.done(b, min(c, 1)))
                                pe.wait_ge(p_ready.sem, p_ready.event(b, c, before=2))
                                for n in range(HALF):
                                    at = P * n if c == 0 else WIDE_OFF[HALF + n] + P * (c - 1)
                                    last = nc.tensor.transpose(
                                        psum[:, 2 + 2 * ((3 * u + c) % 2) + n // 4, (n % 4) * P:(n % 4 + 1) * P],
                                        S2[:, u, at:at + P], ident)
                                last.then_inc(t_ready.sem, 1)
                        for u in range(2):
                            b = 2 * i + u
                            pe.wait_ge(v_ready.sem, v_ready.done(b))
                            pe.wait_ge(p_ready.sem, p_ready.done(b))
                            pe.wait_ge(o_ready.sem, o_ready.done(b, before=1))
                            probs = PT[:, u].rearrange("p (n q) -> p n q", q=P)
                            for h in range(H):
                                vm = [Vm[:, u, (kb * H + h) * P:(kb * H + h + 1) * P] for kb in range(2)]
                                for kb in ((0, 1) if h == 0 else (1, 0)):
                                    mine = (probs[:, 0:NQ] if kb == 0 else probs[:, NQ:])[:, :, h * QB:(h + 1) * QB]
                                    last = nc.tensor.matmul(psum[:, 6, kb * P:ROWS], vm[kb], mine,
                                                            start=(h == 0 and kb == 0), stop=(h == H - 1 and kb == 0),
                                                            skip_group_check=True)
                            last.then_inc(pv_ready.sem, 1)
                            pe.wait_ge(o_ready.sem, o_ready.done(b))
                            pe.wait_ge(h_added.sem, h_added.done(b, before=1))
                            for t in range(TT):
                                last = nc.tensor.matmul(psum[:, 7, t * D:(t + 1) * D], oT[:, u, t * P:(t + 1) * P],
                                                        w("out_w"), start=True, stop=True)
                            last.then_inc(y_done.sem, 1)

                @block.scalar
                def _(act):
                    with act.Fori(0, B // 2) as i:
                        for u in range(2):
                            b = 2 * i + u
                            act.wait_ge(y_ready1.sem, y_ready1.done(b, before=2))
                            for n, bank in enumerate(BANKS):
                                act.wait_ge(top_ready.sem, top_ready.done(b, n))
                                for j in bank:
                                    k = ORDER.index(j)
                                    last = nc.scalar.activation(
                                        Ex[:, u, OFF[j]:OFF[j] + SPAN[j]], S[:, u, OFF[j]:OFF[j] + SPAN[j]], ACT.Exp,
                                        bias=neg_top[:, u, k:k + 1], accum_out=total[:, u, k:k + 1])
                            last.then_inc(e_ready.sem, 1)
                        for u in range(2):
                            b = 2 * i + u
                            act.wait_ge(y_ready1.sem, y_ready1.done(b))
                            for j in ORDER:
                                k = ORDER.index(j)
                                at = Y[:, u, OFF[j]:OFF[j] + SPAN[j]]
                                last = nc.scalar.activation(at, at, ACT.Sqrt, scale=scale[:, u, k:k + 1])
                            last.then_inc(root_ready.sem, 1)
                        for u in range(2):
                            b = 2 * i + u
                            act.wait_ge(root_ready.sem, root_ready.done(b))
                            nc.scalar.activation(Y[:, u], Y[:, u], ACT.Exp, scale=-1.0).then_inc(te_ready.sem, 1)
                        for u in range(2):
                            b = 2 * i + u
                            act.wait_ge(s2_ready.sem, s2_ready.done(b))
                            for c in range(3):
                                act.wait_ge(t_ready.sem, t_ready.done(b, c))
                                bank = 2 + 2 * ((3 * u + c) % 2)
                                nc.scalar.activation(
                                    PT[:, u, c * HALF * P:(c + 1) * HALF * P].rearrange("p (n q) -> p n q", q=P),
                                    psum[:, bank:bank + 2, :].rearrange("p k (n q) -> p (k n) q", q=P), ACT.Exp).then_inc(p_ready.sem, 1)

                @block.vector
                def _(dve):
                    v = nc.vector
                    v.memset(S2[:], NEG)
                    v.memset(oT[:], 0.0)
                    v.memset(Ex[:, :, PACKED:], 0.0)
                    v.memset(causal[:], 0.0).then_inc(prepared, 1)
                    dve.wait_ge(prepared, 1)
                    v.tensor_copy(causal[:, 2 * P - QB:], w("last_key")).then_inc(prepared, 1)
                    dve.wait_ge(prepared, 2)
                    dve.wait_ge(tables_landed, 16)
                    with dve.Fori(0, B // 2) as i:
                        st = Steps(dve, vector_steps, DVE_STEPS, i)
                        for u in range(2):
                            b = 2 * i + u
                            dve.wait_ge(e_ready.sem, e_ready.done(b, before=2))
                            for n, bank in enumerate(BANKS):
                                dve.wait_ge(s_ready.sem, s_ready.done(b, n))
                                wait_apart(dve)
                                for j in bank:
                                    k = ORDER.index(j)
                                    at = OFF[j] - BANK_OFF[n]
                                    last = v.tensor_tensor_reduce(
                                        S[:, u, OFF[j]:OFF[j] + SPAN[j]], psum[:, (u * NB + n) % 2, at:at + SPAN[j]],
                                        causal[:, 2 * P - SPAN[j]:], 1.0, -3e38, ALU.add, ALU.max, top1[:, u, k:k + 1])
                                last.then_inc(max_steps, 1)
                                k0 = ORDER.index(bank[0])
                                dve.wait_ge(max_steps, b * NB + n + 1)
                                v.tensor_scalar(
                                    neg_top[:, u, k0:k0 + len(bank)], top1[:, u, k0:k0 + len(bank)], -1.0, None, ALU.mult).then_inc(top_ready.sem, 1)
                        for u in range(2):
                            b = 2 * i + u
                            dve.wait_ge(e_ready.sem, e_ready.done(b))
                            st.link(v.reciprocal(scale[:, u], total[:, u]))
                            st.step(v.tensor_scalar(scale[:, u], scale[:, u], gamma_sq[:], None, ALU.mult))
                            v.tensor_tensor_scan(
                                Ex[:, u, 0:PACKED][:, ::-1], no_reset[:, ::-1], Ex[:, u, 0:PACKED][:, ::-1],
                                0.0, ALU.mult, ALU.add).then_inc(scan_ready.sem, 1)
                        for u in range(2):
                            b = 2 * i + u
                            dve.wait_ge(te_ready.sem, te_ready.done(b))
                            dve.wait_ge(t_ready.sem, t_ready.done(b, before=2))
                            st.link(v.tensor_scalar(Y[:, u], Y[:, u], 1e-5, 1e5, ALU.max, ALU.min))
                            wait_apart(dve)
                            for j in range(NQ):
                                last = v.tensor_tensor_reduce(
                                    S2[:, u, WIDE_OFF[j]:WIDE_OFF[j] + SPAN[j]], Y[:, u, OFF[j]:OFF[j] + SPAN[j]],
                                    S[:, u, OFF[j]:OFF[j] + SPAN[j]], 1.0, -3e38, ALU.mult, ALU.max, top2[:, u, j:j + 1])
                            st.link(last)
                            for j in range(NQ):
                                at = S2[:, u, WIDE_OFF[j]:WIDE_OFF[j] + SPAN[j]]
                                last = v.tensor_scalar(at, at, top2[:, u, j:j + 1], None, ALU.subtract)
                                if j in (HALF - 1, NQ - 1):
                                    last.then_inc(s2_ready.sem, 1)
                        for u in range(2):
                            b = 2 * i + u
                            dve.wait_ge(pv_ready.sem, pv_ready.done(b))
                            dve.wait_ge(y_done.sem, y_done.done(b, before=2))
                            st.link(v.reciprocal(inv[:, u], psum[D:2 * D, 6, 0:ROWS]))
                            v.tensor_tensor(oT[:, u, 1:], psum[0:D, 6, 1:ROWS], inv[:, u, 1:], ALU.mult).then_inc(o_ready.sem, 1)
                            dve.wait_ge(y_done.sem, y_done.done(b))
                            st.link(v.tensor_tensor(seq_rows(h_all, b), seq_rows(h_all, b),
                                                    two_tiles(psum[:, 7, 0:TT * D]), ALU.add))
                            v.tensor_tensor(seq_rows(h_all, b), seq_rows(h_all, b),
                                                             bcast(w("out_b")[:, None, :], [P, TT, D]), ALU.add).then_inc(h_added.sem, 1)
                        st.end()
        attn_ctx.close()
        cen = sb(top, "cen_c", [P, B * TT, D])
        HP = H // 2
        with ExitStack() as ctx:
            layer_stats("ffn_ln", h_all, cen, 1e-5)
            logit_w = sb(ctx, "logit_w", [D + 1, H, G])
            mix_w = sb(ctx, "mix_w", [D, D])
            vo_w = sb(ctx, "vo_w", [D, H, D])
            inv_temp = sb(ctx, "inv_temp", [P, H])
            fw_tensor, fw_vector = sem("fw_tensor"), sem("fw_vector")
            with nc.Block() as block:
                @block.tensor
                def _(pe):
                    for h in range(H):
                        nc.tensor.matmul(psum[0:D, 0, h * G:(h + 1) * G], w("x_w")[:, h * D:(h + 1) * D], w("slice_w"),
                                         start=True, stop=True)
                    for h in range(H):
                        nc.tensor.matmul(psum[D:D + 1, 3, h * G:(h + 1) * G], w("x_b")[:, h:h + 1], w("slice_w"),
                                         start=True, stop=True)
                    nc.tensor.matmul(psum[0:D, 1, 0:D], w("fq_w"), w("fk_w"), start=True, stop=True)
                    nc.tensor.matmul(psum[0:D, 2, :], w("fv_w"), w("fout_w"), start=True, stop=True).then_inc(fw_tensor, 1)

                @block.vector
                def _(dve):
                    v = nc.vector
                    st = Steps(dve, fw_vector)
                    st.link(v.tensor_scalar(inv_temp[:], w("temp"), 0.1, 5.0, ALU.max, ALU.min))
                    st.link(v.reciprocal(inv_temp[:], inv_temp[:]))
                    dve.wait_ge(fw_tensor, 1)
                    v.tensor_tensor(logit_w[0:D], psum[0:D, 0, :].rearrange("p (h g) -> p h g", h=H),
                                    bcast(inv_temp[0:D, :, None], [D, H, G]), ALU.mult)
                    st.link(v.tensor_tensor(logit_w[D:D + 1], psum[D:D + 1, 3, :].rearrange("p (h g) -> p h g", h=H),
                                            bcast(w("slice_b")[D:D + 1, None, :], [1, H, G]), ALU.add))
                    v.tensor_tensor(logit_w[D:D + 1], logit_w[D:D + 1], bcast(inv_temp[D:D + 1, :, None], [1, H, G]), ALU.mult)
                    v.tensor_copy(mix_w[:], psum[0:D, 1, 0:D])
                    v.tensor_copy(vo_w[:], psum[0:D, 2, :].rearrange("p (h g) -> p h g", h=H))

            stage = sb(ctx, "ffn_stage", [P, 2, TT, D])
            xT = sb(ctx, "ffn_xT", [D + 1, 2, ROWS])
            Wn = sb(ctx, "Wn", [P, 2, TT, H, G])
            WT = sb(ctx, "WT", [P, 2, HP, ROWS])
            Fx = sb(ctx, "Fx", [P, 2, TT, H, D + 1])
            wtop, winv = sb(ctx, "wtop", [P, 2, TT, H]), sb(ctx, "winv", [P, 2, TT, H])
            sinv = sb(ctx, "sinv", [P, 2, HP])
            ST = sb(ctx, "ST", [P, 2, HP, D])
            stT = sb(ctx, "stT", [D, 2, H, G])
            mixT = sb(ctx, "mixT", [D, 2, H, G])
            VO = sb(ctx, "VO", [G, 2, H, D])
            A = sb(ctx, "A", [P, 2, HP, G])
            aT = sb(ctx, "aT", [G, 2, H, G])
            OW = sb(ctx, "OW", [P, 2, HP, D])
            names = ["xn", "xT", "xT_sb", "logits", "fx", "shifted", "exped", "winv", "wn", "fx_sb", "slices", "wT",
                     "wT_sb", "slices_sb", "stT", "stT_sb", "mix_vo", "mixT_sb", "vo_sb", "scores", "sc_shifted",
                     "sc_exped", "attn", "aT", "aT_sb", "ow", "ow_sb", "rows", "h_added"]
            at = {n: Signal(f"ffn_{n}") for n in names}
            steps, ready = sem("ffn_vector_steps"), sem("ffn_prepared")
            FFN_STEPS = 2 * (1 + 2 + 2 + 1 + 2 + 1)
            with nc.Block() as block:
                @block.sync
                def _(sp):
                    open_signals(sp, list(at.values()))

                @block.tensor
                def _(pe):
                    t_ = nc.tensor
                    pe.wait_ge(ready, 1)
                    with pe.Fori(0, B // 2) as i:
                        bu = [(2 * i + u, u, 4 * u) for u in range(2)]
                        for b, u, bank in bu:
                            pe.wait_ge(at["xn"].sem, at["xn"].done(b))
                            pe.wait_ge(at["h_added"].sem, at["h_added"].done(b, before=2))
                            transposed_rows(bank, stage, u).then_inc(at["xT"].sem, 1)
                        for b, u, bank in bu:
                            pe.wait_ge(at["xT_sb"].sem, at["xT_sb"].done(b))
                            for t in range(TT):
                                last = t_.matmul(psum[:, bank + 1 + t, :], xT[:, u, t * P:(t + 1) * P],
                                                 logit_w[:].rearrange("p h g -> p (h g)"), start=True, stop=True)
                            last.then_inc(at["logits"].sem, 1)
                            for t in range(TT):
                                last = t_.matmul(psum[:, bank + 3 * (1 - t), :], xT[:, u, t * P:(t + 1) * P], w("fx_w"),
                                                 start=True, stop=True)
                            last.then_inc(at["fx"].sem, 1)
                        for b, u, bank in bu:
                            pe.wait_ge(at["wn"].sem, at["wn"].done(b))
                            for t in range(TT):
                                for hp in range(HP):
                                    last = t_.transpose(psum[:, bank + 1 + hp // 2, (hp % 2) * ROWS + t * P:(hp % 2) * ROWS + (t + 1) * P],
                                                        Wn[:, u, t, 2 * hp:2 * hp + 2, :].rearrange("p h g -> p (h g)"), ident)
                            last.then_inc(at["wT"].sem, 1)
                            pe.wait_ge(at["fx_sb"].sem, at["fx_sb"].done(b))
                            for h in range(H):
                                for t in range(TT):
                                    last = t_.matmul(psum[(h % 2) * G:(h % 2 + 1) * G, bank, (h // 2) * (D + 1):(h // 2 + 1) * (D + 1)],
                                                     Wn[:, u, t, h, :], Fx[:, u, t, h, :], start=(t == 0), stop=(t == TT - 1))
                            last.then_inc(at["slices"].sem, 1)
                        for b, u, bank in bu:
                            pe.wait_ge(at["slices_sb"].sem, at["slices_sb"].done(b))
                            pe.wait_ge(at["wT_sb"].sem, at["wT_sb"].done(b))
                            wait_apart(pe)
                            for hp in range(HP):
                                last = t_.transpose(psum[0:D, bank + 2, hp * P:(hp + 1) * P], ST[:, u, hp, :], ident)
                            last.then_inc(at["stT"].sem, 1)
                        for b, u, bank in bu:
                            pe.wait_ge(at["stT_sb"].sem, at["stT_sb"].done(b))
                            wait_apart(pe)
                            t_.matmul(psum[0:D, bank, :], mix_w[:], stT[:, u].rearrange("p h g -> p (h g)"), start=True, stop=True)
                            for h in range(H):
                                last = t_.matmul(psum[0:G, bank + 1, h * D:(h + 1) * D], stT[:, u, h, :], vo_w[:, h, :],
                                                 start=True, stop=True)
                            last.then_inc(at["mix_vo"].sem, 1)
                        for b, u, bank in bu:
                            pe.wait_ge(at["mixT_sb"].sem, at["mixT_sb"].done(b))
                            wait_apart(pe)
                            for h in range(H):
                                last = t_.matmul(psum[(h % 2) * G:(h % 2 + 1) * G, bank, (h // 2) * G:(h // 2 + 1) * G],
                                                 mixT[:, u, h, :], stT[:, u, h, :], start=True, stop=True)
                            last.then_inc(at["scores"].sem, 1)
                        for b, u, bank in bu:
                            pe.wait_ge(at["attn"].sem, at["attn"].done(b))
                            pe.wait_ge(at["vo_sb"].sem, at["vo_sb"].done(b))
                            wait_apart(pe)
                            for hp in range(HP):
                                last = t_.transpose(psum[0:G, bank + 1, hp * P:(hp + 1) * P], A[:, u, hp, :], ident)
                            last.then_inc(at["aT"].sem, 1)
                        for b, u, bank in bu:
                            pe.wait_ge(at["aT_sb"].sem, at["aT_sb"].done(b))
                            wait_apart(pe)
                            for h in range(H):
                                last = t_.matmul(psum[(h % 2) * G:(h % 2 + 1) * G, bank, (h // 2) * D:(h // 2 + 1) * D],
                                                 aT[:, u, h, :], VO[:, u, h, :], start=True, stop=True)
                            last.then_inc(at["ow"].sem, 1)
                        for b, u, bank in bu:
                            pe.wait_ge(at["ow_sb"].sem, at["ow_sb"].done(b))
                            for t in range(TT):
                                for hp in range(HP):
                                    last = t_.matmul(psum[:, bank + 2, t * D:(t + 1) * D], WT[:, u, hp, t * P:(t + 1) * P],
                                                     OW[:, u, hp, :], start=(hp == 0), stop=(hp == HP - 1))
                            last.then_inc(at["rows"].sem, 1)

                @block.scalar
                def _(act):
                    a = nc.scalar
                    with act.Fori(0, B // 2) as i:
                        bu = [(2 * i + u, u, 4 * u) for u in range(2)]
                        for b, u, bank in bu:
                            act.wait_ge(at["xT"].sem, at["xT"].done(b))
                            a.activation(xT[0:D, u], psum[0:D, bank, 0:ROWS], ACT.Copy).then_inc(at["xT_sb"].sem, 1)
                        for b, u, bank in bu:
                            act.wait_ge(at["shifted"].sem, at["shifted"].done(b))
                            a.activation(Wn[:, u], Wn[:, u], ACT.Exp).then_inc(at["exped"].sem, 1)
                            act.wait_ge(at["fx"].sem, at["fx"].done(b))
                            for t in range(TT):
                                last = a.activation(Fx[:, u, t, :, 0:D], psum[:, bank + 3 * (1 - t), :]
                                                    .rearrange("p (h d) -> p h d", h=H), ACT.Copy)
                            last.then_inc(at["fx_sb"].sem, 1)
                        for b, u, bank in bu:
                            act.wait_ge(at["wT"].sem, at["wT"].done(b))
                            a.activation(WT[:, u].rearrange("p h n -> p (h n)"),
                                                              psum[:, bank + 1:bank + 3, :].rearrange("p k n -> p (k n)"), ACT.Copy).then_inc(at["wT_sb"].sem, 1)
                        for b, u, bank in bu:
                            act.wait_ge(at["stT"].sem, at["stT"].done(b))
                            a.activation(stT[:, u].rearrange("p h g -> p (h g)"), psum[0:D, bank + 2, :], ACT.Copy).then_inc(at["stT_sb"].sem, 1)
                        for b, u, bank in bu:
                            act.wait_ge(at["mix_vo"].sem, at["mix_vo"].done(b))
                            a.activation(mixT[:, u].rearrange("p h g -> p (h g)"), psum[0:D, bank, :],
                                                                ACT.Copy, scale=D ** -0.5).then_inc(at["mixT_sb"].sem, 1)
                        for b, u, bank in bu:
                            act.wait_ge(at["sc_shifted"].sem, at["sc_shifted"].done(b))
                            a.activation(A[:, u], A[:, u], ACT.Exp).then_inc(at["sc_exped"].sem, 1)
                        for b, u, bank in bu:
                            act.wait_ge(at["aT"].sem, at["aT"].done(b))
                            a.activation(aT[:, u].rearrange("p h g -> p (h g)"), psum[0:G, bank + 1, :], ACT.Copy).then_inc(at["aT_sb"].sem, 1)

                @block.gpsimd
                def _(pool):
                    with pool.Fori(0, B // 2) as i:
                        for u in range(2):
                            b = 2 * i + u
                            pool.wait_ge(at["winv"].sem, at["winv"].done(b))
                            nc.gpsimd.tensor_tensor(
                                Wn[:, u].rearrange("p t h g -> p (t h) g"), Wn[:, u].rearrange("p t h g -> p (t h) g"),
                                bcast(winv[:, u].rearrange("p t h -> p (t h)")[:, :, None], [P, TT * H, G]), ALU.mult).then_inc(at["wn"].sem, 1)

                @block.vector
                def _(dve):
                    v = nc.vector
                    v.memset(xT[D:D + 1], 1.0)
                    v.memset(Fx[:, :, :, :, D:], 1.0).then_inc(ready, 1)
                    with dve.Fori(0, B // 2) as i:
                        bu = [(2 * i + u, u, 4 * u) for u in range(2)]
                        st = Steps(dve, steps, FFN_STEPS, i)
                        for b, u, bank in bu:
                            dve.wait_ge(at["xT"].sem, at["xT"].done(b, before=2))
                            normed(stage, u, b, cen).then_inc(at["xn"].sem, 1)
                        for b, u, bank in bu:
                            dve.wait_ge(at["logits"].sem, at["logits"].done(b))
                            dve.wait_ge(at["slices"].sem, at["slices"].done(b, before=2))
                            lg = psum[:, bank + 1:bank + 3, :].rearrange("p t (h g) -> p (t h) g", g=G)
                            wn = Wn[:, u].rearrange("p t h g -> p (t h) g")
                            wt = wtop[:, u].rearrange("p t h -> p (t h)")
                            st.link(v.tensor_reduce(wt, lg, X, ALU.max))
                            v.tensor_tensor(wn, lg, bcast(wt[:, :, None], [P, TT * H, G]), ALU.subtract).then_inc(at["shifted"].sem, 1)
                        for b, u, bank in bu:
                            dve.wait_ge(at["exped"].sem, at["exped"].done(b))
                            wi = winv[:, u].rearrange("p t h -> p (t h)")
                            st.link(v.tensor_reduce(wi, Wn[:, u].rearrange("p t h g -> p (t h) g"), X, ALU.add))
                            st.link(v.reciprocal(wi, wi))
                            v.tensor_tensor(winv[:, u], winv[:, u], bcast(w("pad_mask")[:, :, None], [P, TT, H]), ALU.mult).then_inc(at["winv"].sem, 1)
                        for b, u, bank in bu:
                            dve.wait_ge(at["slices"].sem, at["slices"].done(b))
                            sl = psum[:, bank, 0:HP * (D + 1)].rearrange("p (h d) -> p h d", h=HP)
                            st.link(v.tensor_scalar(sinv[:, u], sl[:, :, D], 1e-5, None, ALU.add))
                            st.link(v.reciprocal(sinv[:, u], sinv[:, u]))
                            v.tensor_tensor(ST[:, u], sl[:, :, 0:D], bcast(sinv[:, u, :, None], [P, HP, D]), ALU.mult).then_inc(at["slices_sb"].sem, 1)
                        for b, u, bank in bu:
                            dve.wait_ge(at["mix_vo"].sem, at["mix_vo"].done(b))
                            v.tensor_copy(VO[:, u].rearrange("p h g -> p (h g)"), psum[0:G, bank + 1, :]).then_inc(at["vo_sb"].sem, 1)
                        for b, u, bank in bu:
                            dve.wait_ge(at["scores"].sem, at["scores"].done(b))
                            sc = psum[:, bank, 0:HP * G].rearrange("p (h g) -> p h g", h=HP)
                            st.link(v.tensor_reduce(sinv[:, u], sc, X, ALU.max))
                            v.tensor_tensor(A[:, u], sc, bcast(sinv[:, u, :, None], [P, HP, G]), ALU.subtract).then_inc(at["sc_shifted"].sem, 1)
                        for b, u, bank in bu:
                            dve.wait_ge(at["sc_exped"].sem, at["sc_exped"].done(b))
                            st.link(v.tensor_reduce(sinv[:, u], A[:, u], X, ALU.add))
                            st.link(v.reciprocal(sinv[:, u], sinv[:, u]))
                            v.tensor_tensor(A[:, u], A[:, u], bcast(sinv[:, u, :, None], [P, HP, G]), ALU.mult).then_inc(at["attn"].sem, 1)
                        for b, u, bank in bu:
                            dve.wait_ge(at["ow"].sem, at["ow"].done(b))
                            v.tensor_copy(OW[:, u].rearrange("p h g -> p (h g)"), psum[:, bank, 0:HP * D]).then_inc(at["ow_sb"].sem, 1)
                        for b, u, bank in bu:
                            dve.wait_ge(at["rows"].sem, at["rows"].done(b))
                            st.link(v.tensor_tensor(seq_rows(h_all, b), seq_rows(h_all, b),
                                                    bcast(w("fout_b")[:, None, :], [P, TT, D]), ALU.add))
                            v.tensor_tensor(seq_rows(h_all, b), seq_rows(h_all, b),
                                                                   two_tiles(psum[:, bank + 2, 0:TT * D]), ALU.add).then_inc(at["h_added"].sem, 1)
                        st.end()

        with ExitStack() as ctx:
            layer_stats("win_ln", h_all, cen, 1e-5)
            NW = ROWS // WS
            stage = sb(ctx, "win_stage", [P, 2, TT, D])
            xT = sb(ctx, "win_xT", [D, 2, ROWS])
            Qw, Kw = sb(ctx, "Qw", [D, 2, ROWS]), sb(ctx, "Kw", [D, 2, ROWS])
            Kd = sb(ctx, "Kd", [D, 2, NW, H, WS])
            Vd = sb(ctx, "Vd", [P, 2, NW, HP, 2 * DK])
            Aw = sb(ctx, "Aw", [P, 2, TT, H, WS])
            AwT = sb(ctx, "AwT", [P, 2, TT, HP, P])
            wtop, winv = sb(ctx, "win_top", [P, 2, TT, H]), sb(ctx, "win_inv", [P, 2, TT, H])
            On = sb(ctx, "On", [P, 2, TT, D])
            OnT = sb(ctx, "OnT", [D, 2, ROWS])
            names = ["xn", "xT", "xT_sb", "qkv", "q_sb", "k_sb", "v_sb", "kd", "scores", "biased", "top", "shifted", "exped",
                     "aT", "aT_sb", "inv", "heads", "heads_sb", "oT", "oT_sb", "rows", "h_added"]
            at = {n: Signal(f"win_{n}") for n in names}
            steps, ready = sem("win_vector_steps"), sem("win_prepared")
            WIN_STEPS = 2 * (2 + 1)
            with nc.Block() as block:
                @block.sync
                def _(sp):
                    open_signals(sp, list(at.values()))

                @block.tensor
                def _(pe):
                    t_ = nc.tensor
                    with pe.Fori(0, B // 2) as i:
                        bu = [(2 * i + u, u, 4 * u) for u in range(2)]
                        for b, u, bank in bu:
                            pe.wait_ge(at["xn"].sem, at["xn"].done(b))
                            pe.wait_ge(at["h_added"].sem, at["h_added"].done(b, before=2))
                            transposed_rows(bank, stage, u).then_inc(at["xT"].sem, 1)
                        for b, u, bank in bu:
                            pe.wait_ge(at["xT_sb"].sem, at["xT_sb"].done(b))
                            wait_apart(pe)
                            for n, name in enumerate(("a_q", "a_k")):
                                t_.matmul(psum[0:D, bank + 1 + n, 0:ROWS], w(name), xT[:, u], start=True, stop=True)
                            for half in range(2):
                                for n in range(NW):
                                    last = t_.matmul(psum[half * D:(half + 1) * D, bank, n * D:(n + 1) * D],
                                                     xT[:, u, n * WS:(n + 1) * WS], w("a_v"), start=True, stop=True)
                            last.then_inc(at["qkv"].sem, 1)
                        for b, u, bank in bu:
                            pe.wait_ge(at["kd"].sem, at["kd"].done(b))
                            pe.wait_ge(at["q_sb"].sem, at["q_sb"].done(b))
                            wait_apart(pe)
                            for n in range(NW):
                                last = t_.matmul(psum[(n % 2) * WS:(n % 2 + 1) * WS, bank + 2 + n // 2, :],
                                                 Qw[:, u, n * WS:(n + 1) * WS], Kd[:, u, n].rearrange("p h k -> p (h k)"),
                                                 start=True, stop=True)
                            last.then_inc(at["scores"].sem, 1)
                        for b, u, bank in bu:
                            pe.wait_ge(at["exped"].sem, at["exped"].done(b))
                            for t in range(TT):
                                for hp in range(HP):
                                    last = t_.transpose(psum[:, bank + 2 + t, hp * P:(hp + 1) * P],
                                                        Aw[:, u, t, 2 * hp:2 * hp + 2].rearrange("p h k -> p (h k)"), ident)
                            last.then_inc(at["aT"].sem, 1)
                        for b, u, bank in bu:
                            pe.wait_ge(at["aT_sb"].sem, at["aT_sb"].done(b))
                            pe.wait_ge(at["v_sb"].sem, at["v_sb"].done(b))
                            for n in range(NW):
                                for hp in range(HP):
                                    last = t_.matmul(psum[(n % 2) * WS:(n % 2 + 1) * WS, bank,
                                                          (n // 2) * D + hp * 2 * DK:(n // 2) * D + (hp + 1) * 2 * DK],
                                                     AwT[:, u, n // 2, hp, (n % 2) * WS:(n % 2 + 1) * WS],
                                                     Vd[:, u, n, hp, :], start=True, stop=True)
                            last.then_inc(at["heads"].sem, 1)
                        for b, u, bank in bu:
                            pe.wait_ge(at["heads_sb"].sem, at["heads_sb"].done(b))
                            wait_apart(pe)
                            for t in range(TT):
                                last = t_.transpose(psum[0:D, bank + 1, t * P:(t + 1) * P], On[:, u, t, :], ident)
                            last.then_inc(at["oT"].sem, 1)
                        for b, u, bank in bu:
                            pe.wait_ge(at["oT_sb"].sem, at["oT_sb"].done(b))
                            for t in range(TT):
                                last = t_.matmul(psum[:, bank, t * D:(t + 1) * D], OnT[:, u, t * P:(t + 1) * P], w("a_proj"),
                                                 start=True, stop=True)
                            last.then_inc(at["rows"].sem, 1)

                @block.scalar
                def _(act):
                    a = nc.scalar
                    with act.Fori(0, B // 2) as i:
                        bu = [(2 * i + u, u, 4 * u) for u in range(2)]
                        for b, u, bank in bu:
                            act.wait_ge(at["xT"].sem, at["xT"].done(b))
                            a.activation(xT[:, u], psum[0:D, bank, 0:ROWS], ACT.Copy).then_inc(at["xT_sb"].sem, 1)
                        for b, u, bank in bu:
                            act.wait_ge(at["qkv"].sem, at["qkv"].done(b))
                            act.wait_ge(at["kd"].sem, at["kd"].done(b, before=2))
                            a.activation(Kw[:, u], psum[0:D, bank + 2, 0:ROWS], ACT.Copy).then_inc(at["k_sb"].sem, 1)
                        for b, u, bank in bu:
                            act.wait_ge(at["shifted"].sem, at["shifted"].done(b))
                            a.activation(Aw[:, u], Aw[:, u], ACT.Exp).then_inc(at["exped"].sem, 1)
                        for b, u, bank in bu:
                            act.wait_ge(at["aT"].sem, at["aT"].done(b))
                            a.activation(AwT[:, u].rearrange("p t h n -> p t (h n)"),
                                                              psum[:, bank + 2:bank + 4, :], ACT.Copy).then_inc(at["aT_sb"].sem, 1)
                        for b, u, bank in bu:
                            act.wait_ge(at["oT"].sem, at["oT"].done(b))
                            a.activation(OnT[:, u], psum[0:D, bank + 1, 0:ROWS], ACT.Copy).then_inc(at["oT_sb"].sem, 1)

                @block.gpsimd
                def _(pool):
                    g = nc.gpsimd
                    with pool.Fori(0, B // 2) as i:
                        for u in range(2):
                            b = 2 * i + u
                            pool.wait_ge(at["k_sb"].sem, at["k_sb"].done(b))
                            pool.wait_ge(at["scores"].sem, at["scores"].done(b, before=2))
                            ks = Kw[:, u].rearrange("p (n k) -> p n k", n=NW)
                            g.tensor_tensor(Kd[:, u], bcast(ks[:, :, None, :], [D, NW, H, WS]),
                                                              bcast(w("head_mask")[:, None, :, None], [D, NW, H, WS]), ALU.mult).then_inc(at["kd"].sem, 1)
                        for u in range(2):
                            b = 2 * i + u
                            pool.wait_ge(at["top"].sem, at["top"].done(b))
                            aw = Aw[:, u].rearrange("p t h k -> p (t h) k")
                            g.tensor_tensor(
                                aw, aw, bcast(wtop[:, u].rearrange("p t h -> p (t h)")[:, :, None], [P, TT * H, WS]), ALU.subtract).then_inc(at["shifted"].sem, 1)

                @block.vector
                def _(dve):
                    v = nc.vector
                    v.memset(Vd[:], 0.0).then_inc(ready, 1)
                    dve.wait_ge(ready, 1)
                    with dve.Fori(0, B // 2) as i:
                        bu = [(2 * i + u, u, 4 * u) for u in range(2)]
                        st = Steps(dve, steps, WIN_STEPS, i)
                        for b, u, bank in bu:
                            dve.wait_ge(at["xT"].sem, at["xT"].done(b, before=2))
                            normed(stage, u, b, cen).then_inc(at["xn"].sem, 1)
                        for b, u, bank in bu:
                            dve.wait_ge(at["qkv"].sem, at["qkv"].done(b))
                            v.tensor_scalar(Qw[:, u], psum[0:D, bank + 1, 0:ROWS], DK ** -0.5, None, ALU.mult).then_inc(at["q_sb"].sem, 1)
                            for half in range(2):
                                rows_of = slice(half * D, (half + 1) * D)
                                vals = psum[rows_of, bank, 0:NW * D].rearrange("p (n h s d) -> p n h (s d)", n=NW, h=HP, s=2)
                                last = v.tensor_copy(Vd[rows_of, u, :, :, half * DK:(half + 1) * DK],
                                                     vals[:, :, :, half * DK:(half + 1) * DK])
                            last.then_inc(at["v_sb"].sem, 1)
                        for b, u, bank in bu:
                            dve.wait_ge(at["scores"].sem, at["scores"].done(b))
                            dve.wait_ge(at["aT"].sem, at["aT"].done(b, before=2))
                            aw = Aw[:, u].rearrange("p t h k -> p (t h) k")
                            v.tensor_tensor(
                                aw, psum[:, bank + 2:bank + 4, :].rearrange("p t (h k) -> p (t h) k", k=WS),
                                bcast(w("rel")[:, None, :], [P, TT * H, WS]), ALU.add).then_inc(at["biased"].sem, 1)
                            dve.wait_ge(at["biased"].sem, at["biased"].done(b))
                            v.tensor_reduce(wtop[:, u].rearrange("p t h -> p (t h)"), aw, X, ALU.max).then_inc(at["top"].sem, 1)
                        for b, u, bank in bu:
                            dve.wait_ge(at["exped"].sem, at["exped"].done(b))
                            wi = winv[:, u].rearrange("p t h -> p (t h)")
                            st.link(v.tensor_reduce(wi, Aw[:, u].rearrange("p t h k -> p (t h) k"), X, ALU.add))
                            st.link(v.reciprocal(wi, wi))
                        for b, u, bank in bu:
                            dve.wait_ge(at["heads"].sem, at["heads"].done(b))
                            wi = winv[:, u].rearrange("p t h -> p (t h)")
                            v.tensor_tensor(
                                On[:, u].rearrange("p t (h d) -> p (t h) d", d=DK),
                                psum[:, bank, 0:TT * D].rearrange("p (n d) -> p n d", d=DK),
                                bcast(wi[:, :, None], [P, TT * H, DK]), ALU.mult).then_inc(at["heads_sb"].sem, 1)
                        for b, u, bank in bu:
                            dve.wait_ge(at["rows"].sem, at["rows"].done(b))
                            st.link(v.tensor_tensor(seq_rows(h_all, b), seq_rows(h_all, b),
                                                    bcast(w("a_proj_b")[:, None, :], [P, TT, D]), ALU.add))
                            v.tensor_tensor(seq_rows(h_all, b), seq_rows(h_all, b),
                                                                   two_tiles(psum[:, bank, 0:TT * D]), ALU.add).then_inc(at["h_added"].sem, 1)
                        st.end()
        with ExitStack() as ctx:
            layer_stats("moe_ln", h_all, cen, 1e-5)
            EP = E // 2
            XT = sb(ctx, "moe_XT", [D, B * ROWS])
            Pr = sb(ctx, "Pr", [P, B * TT, E])
            with ExitStack() as inner:
                stage = sb(inner, "moe_stage", [P, 2, TT, D])
                xT = sb(inner, "route_xT", [D, 2, ROWS])
                names = ["xn", "xT", "xT_sb", "kept", "logits", "logits_sb"]
                at = {n: Signal(f"route_{n}") for n in names}
                with nc.Block() as block:
                    @block.sync
                    def _(sp):
                        open_signals(sp, list(at.values()))

                    @block.tensor
                    def _(pe):
                        with pe.Fori(0, B // 2) as i:
                            for u in range(2):
                                b = 2 * i + u
                                pe.wait_ge(at["xn"].sem, at["xn"].done(b))
                                pe.wait_ge(at["xT_sb"].sem, at["xT_sb"].done(b, before=2))
                                transposed_rows(u, stage, u).then_inc(at["xT"].sem, 1)
                            for u in range(2):
                                b = 2 * i + u
                                pe.wait_ge(at["xT_sb"].sem, at["xT_sb"].done(b))
                                pe.wait_ge(at["logits_sb"].sem, at["logits_sb"].done(b, before=2))
                                for t in range(TT):
                                    last = nc.tensor.matmul(psum[:, 2 + u, t * E:(t + 1) * E], xT[:, u, t * P:(t + 1) * P],
                                                            w("router"), start=True, stop=True)
                                last.then_inc(at["logits"].sem, 1)

                    @block.scalar
                    def _(act):
                        with act.Fori(0, B // 2) as i:
                            for u in range(2):
                                b = 2 * i + u
                                act.wait_ge(at["xT"].sem, at["xT"].done(b))
                                act.wait_ge(at["logits"].sem, at["logits"].done(b, before=2))
                                act.wait_ge(at["kept"].sem, at["kept"].done(b, before=2))
                                nc.scalar.activation(xT[:, u], psum[0:D, u, 0:ROWS], ACT.Copy).then_inc(at["xT_sb"].sem, 1)

                    @block.gpsimd
                    def _(pool):
                        with pool.Fori(0, B // 2) as i:
                            for u in range(2):
                                b = 2 * i + u
                                pool.wait_ge(at["xT_sb"].sem, at["xT_sb"].done(b))
                                nc.gpsimd.tensor_copy(XT[:, bass.ds(b * ROWS, ROWS)], xT[:, u]).then_inc(at["kept"].sem, 1)

                    @block.vector
                    def _(dve):
                        v = nc.vector
                        with dve.Fori(0, B // 2) as i:
                            for u in range(2):
                                b = 2 * i + u
                                dve.wait_ge(at["xT"].sem, at["xT"].done(b, before=2))
                                normed(stage, u, b, cen).then_inc(at["xn"].sem, 1)
                                dve.wait_ge(at["xn"].sem, at["xn"].done(b))
                                v.tensor_tensor(seq_rows(h_all, b), seq_rows(h_all, b), stage[:, u], ALU.add)
                            for u in range(2):
                                b = 2 * i + u
                                dve.wait_ge(at["logits"].sem, at["logits"].done(b))
                                v.tensor_copy(
                                    seq_rows(Pr, b), psum[:, 2 + u, 0:TT * E].rearrange("p (t e) -> p t e", t=TT)).then_inc(at["logits_sb"].sem, 1)

            Cm = sb(ctx, "Cm", [P, B * TT, E])
            with ExitStack() as inner:
                RB = B * TT
                Left = sb(inner, "Left", [P, RB, E])
                eq, count = sb(inner, "eq", [P, RB, E]), sb(inner, "count", [P, RB, E])
                starts = sb(inner, "starts", [P, RB, E])
                best1, best2 = sb(inner, "best1", [P, RB]), sb(inner, "best2", [P, RB])
                steps, shifted, exped = sem("top_steps"), sem("top_shifted"), sem("top_exped")
                with nc.Block() as block:
                    @block.scalar
                    def _(act):
                        act.wait_ge(shifted, 1)
                        nc.scalar.activation(Pr[:], Pr[:], ACT.Exp).then_inc(exped, 1)

                    @block.vector
                    def _(dve):
                        v = nc.vector
                        st = Steps(dve, steps)
                        wide = [P, RB, E]
                        flat = lambda t: t[:].rearrange("p r e -> p (r e)")
                        over = lambda t: bcast(t[:][:, :, None], wide)
                        st.step(v.memset(starts[:], 1.0))
                        st.link(v.tensor_reduce(best1[:], Pr[:], X, ALU.max))
                        st.step(v.memset(starts[:, :, 0:1], 0.0))
                        v.tensor_tensor(Pr[:], Pr[:], over(best1), ALU.subtract).then_inc(shifted, 1)
                        dve.wait_ge(exped, 1)
                        st.link(v.tensor_reduce(best1[:], Pr[:], X, ALU.add))
                        st.link(v.reciprocal(best1[:], best1[:]))
                        st.link(v.tensor_tensor(Pr[:], Pr[:], over(best1), ALU.mult))

                        def first_of_best(best, source):
                            st.link(v.tensor_reduce(best[:], source[:], X, ALU.max))
                            st.link(v.tensor_tensor(eq[:], source[:], over(best), ALU.is_equal))
                            st.link(v.tensor_tensor_scan(flat(count), flat(starts), flat(eq), 0.0, ALU.mult, ALU.add))
                            st.link(v.scalar_tensor_tensor(flat(count), flat(count), 1.0, flat(eq), ALU.is_equal, ALU.mult))

                        first_of_best(best1, Pr)
                        st.step(v.tensor_tensor(Cm[:], Pr[:], count[:], ALU.mult))
                        st.link(v.scalar_tensor_tensor(flat(Left), flat(count), -2.0, flat(Pr), ALU.mult, ALU.add))
                        first_of_best(best2, Left)
                        st.link(v.tensor_tensor(count[:], Pr[:], count[:], ALU.mult))
                        st.step(v.tensor_tensor(Cm[:], Cm[:], count[:], ALU.add))
                        st.link(v.tensor_tensor(best1[:], best1[:], best2[:], ALU.add))
                        st.link(v.tensor_scalar(best1[:], best1[:], 1e-12, None, ALU.max))
                        st.link(v.reciprocal(best1[:], best1[:]))
                        st.link(v.tensor_tensor(Cm[:], Cm[:], over(best1), ALU.mult))

            xT = sb(ctx, "moe_xT", [D, 2, ROWS])
            Cs = sb(ctx, "Cs", [P, 2, TT, E])
            cT = sb(ctx, "cT", [E, 2, ROWS])
            Hd = sb(ctx, "Hd", [P, 2, EP, ROWS])
            names = ["x_sb", "c_sb", "cT", "cT_sb", "hidden", "gelu", "spread", "weighted", "rows", "h_added"]
            at = {n: Signal(f"moe_{n}") for n in names}
            with nc.Block() as block:
                @block.sync
                def _(sp):
                    open_signals(sp, list(at.values()))

                @block.gpsimd
                def _(pool):
                    with pool.Fori(0, B // 2) as i:
                        for u in range(2):
                            b = 2 * i + u
                            pool.wait_ge(at["hidden"].sem, at["hidden"].done(b, before=2))
                            nc.gpsimd.tensor_copy(xT[:, u], XT[:, bass.ds(b * ROWS, ROWS)]).then_inc(at["x_sb"].sem, 1)
                            pool.wait_ge(at["cT"].sem, at["cT"].done(b, before=2))
                            nc.gpsimd.tensor_copy(Cs[:, u], seq_rows(Cm, b)).then_inc(at["c_sb"].sem, 1)

                @block.tensor
                def _(pe):
                    t_ = nc.tensor
                    with pe.Fori(0, B // 2) as i:
                        bu = [(2 * i + u, u, 4 * u) for u in range(2)]
                        for b, u, bank in bu:
                            pe.wait_ge(at["h_added"].sem, at["h_added"].done(b, before=2))
                            pe.wait_ge(at["weighted"].sem, at["weighted"].done(b, before=2))
                            pe.wait_ge(at["c_sb"].sem, at["c_sb"].done(b))
                            for t in range(TT):
                                last = t_.transpose(psum[0:E, bank + 2, t * P:(t + 1) * P], Cs[:, u, t, :], ident)
                            last.then_inc(at["cT"].sem, 1)
                            pe.wait_ge(at["x_sb"].sem, at["x_sb"].done(b))
                            for c in range(EP):
                                last = t_.matmul(psum[:, bank + c // 2, (c % 2) * ROWS:(c % 2 + 1) * ROWS],
                                                 w("w1")[:, c * P:(c + 1) * P], xT[:, u], start=True, stop=True)
                            last.then_inc(at["hidden"].sem, 1)
                        for b, u, bank in bu:
                            pe.wait_ge(at["cT_sb"].sem, at["cT_sb"].done(b))
                            for c in range(EP):
                                last = t_.matmul(psum[:, bank + 2 + c // 2, (c % 2) * ROWS:(c % 2 + 1) * ROWS],
                                                 w("expand")[:, c * P:(c + 1) * P], cT[:, u], start=True, stop=True)
                            last.then_inc(at["spread"].sem, 1)
                        for b, u, bank in bu:
                            pe.wait_ge(at["weighted"].sem, at["weighted"].done(b))
                            for t in range(TT):
                                for c in range(EP):
                                    t_.matmul(psum[:, bank, t * D:(t + 1) * D], Hd[:, u, c, t * P:(t + 1) * P],
                                              w("w2")[:, c * D:(c + 1) * D], start=(c == 0), stop=False)
                                last = t_.matmul(psum[:, bank, t * D:(t + 1) * D], cT[:, u, t * P:(t + 1) * P], w("b2"),
                                                 start=False, stop=True)
                            last.then_inc(at["rows"].sem, 1)

                @block.scalar
                def _(act):
                    a = nc.scalar
                    with act.Fori(0, B // 2) as i:
                        bu = [(2 * i + u, u, 4 * u) for u in range(2)]
                        for b, u, bank in bu:
                            act.wait_ge(at["cT"].sem, at["cT"].done(b))
                            act.wait_ge(at["rows"].sem, at["rows"].done(b, before=2))
                            a.activation(cT[:, u], psum[0:E, bank + 2, 0:ROWS], ACT.Copy).then_inc(at["cT_sb"].sem, 1)
                            act.wait_ge(at["hidden"].sem, at["hidden"].done(b))
                            for c in range(EP):
                                last = a.activation(Hd[:, u, c], psum[:, bank + c // 2, (c % 2) * ROWS:(c % 2 + 1) * ROWS],
                                                    ACT.Gelu, bias=w("b1")[:, c:c + 1])
                            last.then_inc(at["gelu"].sem, 1)

                @block.vector
                def _(dve):
                    v = nc.vector
                    with dve.Fori(0, B // 2) as i:
                        bu = [(2 * i + u, u, 4 * u) for u in range(2)]
                        for b, u, bank in bu:
                            dve.wait_ge(at["gelu"].sem, at["gelu"].done(b))
                            dve.wait_ge(at["spread"].sem, at["spread"].done(b))
                            hd = Hd[:, u].rearrange("p c n -> p (c n)")
                            v.tensor_tensor(
                                hd, hd, psum[:, bank + 2:bank + 4, :].rearrange("p k n -> p (k n)"), ALU.mult).then_inc(at["weighted"].sem, 1)
                        for b, u, bank in bu:
                            dve.wait_ge(at["rows"].sem, at["rows"].done(b))
                            v.tensor_tensor(seq_rows(h_all, b), seq_rows(h_all, b),
                                                                   two_tiles(psum[:, bank, 0:TT * D]), ALU.add).then_inc(at["h_added"].sem, 1)

        stored = sem("stored")
        with nc.Block() as block:
            @block.sync
            def _(sp):
                sp.dma_start(out, h_all[:]).then_inc(stored, 16)
                sp.wait_ge(stored, 16)


def kernel(**inputs):
    import numpy as np
    import concourse.bacc as _bacc
    from concourse.bass_utils import run_bass_kernel_spmd as _run

    a = {k: np.asarray(v) for k, v in inputs.items()}
    rows = lambda v: np.broadcast_to(np.reshape(v, (1, -1)), (P, np.size(v)))
    x = a["x"].reshape(B, NCHUNK, CHUNK).transpose(2, 0, 1)
    x_chunks = np.zeros((P, B, NCHUNK + 1), np.float32)
    x_chunks[:, :, :NCHUNK] = x

    tok_w = a["L0_tok_W"].T
    rel = a["L1_attn_rel_bias"]
    q_at, k_at = np.meshgrid(np.arange(WS), np.arange(WS), indexing="ij")
    rel_tile = rel[k_at - q_at + WS - 1]
    pad_mask = np.ones((P, TT), np.float32)
    pad_mask[P - 1, TT - 1] = 0
    head_mask = (np.arange(D)[:, None] // DK == np.arange(H)[None, :]).astype(np.float32)
    query = (np.arange(P) % QB)[:, None]
    last_key = np.where(np.arange(QB)[None, :] > query, NEG, 0).astype(np.float32)
    expand = np.zeros((E, E // 2, P), np.float32)
    for e in range(E):
        expand[e, e // 2, (e % 2) * D:(e % 2 + 1) * D] = 1
    qkv = a["L1_attn_w_qkv"]
    pack = {
        "tok_w0": tok_w[:P], "tok_w1": tok_w[P:], "tok_b": rows(a["L0_tok_b"]),
        "tok_gamma": rows(a["L0_tok_gamma"]), "tok_beta": rows(a["L0_tok_beta"]),
        "ident": np.eye(P, dtype=np.float32), "pad_mask": pad_mask, "head_mask": head_mask,
        "conv": a["L0_attn_conv_w"].transpose(1, 2, 0).reshape(D, TAPS * D),
        "conv_b": rows(a["L0_attn_conv_b"]), "sqrt_beta": rows(a["L0_attn_sqrt_beta"]),
        "ln_w": a["L0_attn_ln_w"][:, None], "ln_b": a["L0_attn_ln_b"][:, None],
        "ln_b_wide": np.broadcast_to(a["L0_attn_ln_b"][:, None], (D, P)),
        "q_w": a["L0_attn_q_w"].T, "k_w": a["L0_attn_k_w"].T, "v_w": a["L0_attn_v_w"].T,
        "q_b": a["L0_attn_q_b"][:, None], "k_b": np.tile(a["L0_attn_k_b"], 2)[:, None], "v_b": rows(a["L0_attn_v_b"]),
        "out_w": a["L0_attn_out_w"].T, "out_b": rows(a["L0_attn_out_b"]),
        "gammas": np.repeat(a["L0_attn_gammas"].reshape(H), QB)[:, None],
        "fx_w": np.concatenate([a["L0_ffn_W_fx"], a["L0_ffn_b_fx"][None]]),
        "x_w": a["L0_ffn_W_x"].reshape(D, H, D).transpose(2, 1, 0).reshape(D, H * D),
        "x_b": a["L0_ffn_b_x"].reshape(H, D).T, "slice_w": a["L0_ffn_W_slice"],
        "slice_b": np.broadcast_to(a["L0_ffn_b_slice"][None], (D + 1, G)), "temp": rows(a["L0_ffn_temperature"]),
        "fq_w": a["L0_ffn_W_q"].T, "fk_w": a["L0_ffn_W_k"].T, "fv_w": a["L0_ffn_W_v"].T,
        "fout_w": a["L0_ffn_W_out"].reshape(H, D, D).transpose(1, 0, 2).reshape(D, H * D),
        "fout_b": rows(a["L0_ffn_b_out"]),
        "a_q": qkv[0:D].T, "a_k": qkv[D:2 * D].T, "a_v": qkv[2 * D:].T, "a_proj": a["L1_attn_w_proj"].T,
        "a_proj_b": rows(a["L1_attn_b_proj"]), "rel": np.concatenate([rel_tile, rel_tile]),
        "router": a["L1_ffn_router_w"].T,
        "w1": a["L1_ffn_w1"].transpose(1, 0, 2).reshape(D, E * D),
        "b1": a["L1_ffn_b1"].reshape(E // 2, P).T,
        "w2": a["L1_ffn_w2"].reshape(E // 2, P, D).transpose(1, 0, 2).reshape(P, (E // 2) * D),
        "b2": a["L1_ffn_b2"], "expand": expand.reshape(E, -1), "last_key": last_key,
    }
    cols, total = weight_columns()
    weights = np.zeros((P, total), np.float32)
    for name, (at, r, n) in cols.items():
        weights[:r, at:at + n] = pack[name]
    tables = np.zeros((P, 2, PACKED), np.float32)
    tables[:, 1] = 1
    for j in range(NQ):
        key = np.arange(SPAN[j])[None, :]
        tables[:, 0, OFF[j]:OFF[j] + SPAN[j]] = np.maximum(QB * j + query - key, 0)
        tables[:, 1, OFF[j] + SPAN[j] - 1] = 0

    nc = _bacc.Bacc("TRN2", target_bir_lowering=False, num_devices=1)
    arrays = {"x_chunks": x_chunks, "weights": weights, "tables": tables}
    args = [nc.dram_tensor(k, v.shape, F32, kind="ExternalInput").ap() for k, v in arrays.items()]
    out = nc.dram_tensor("out", (P, B * TT, D), F32, kind="ExternalOutput").ap()
    build(nc, *args, out)
    got = _run(nc, [arrays], core_ids=[0]).results[0]["out"]
    return got.reshape(P, B, TT, D).transpose(1, 2, 0, 3).reshape(B, ROWS, D)[:, :TOK]
```

```python
from contextlib import ExitStack

import concourse.bass as bass
from concourse import mybir

P = 128
B = 16
SEQ, FEAT = 2048, 16
PATCH, STRIDE = 16, 8
CHUNK = STRIDE * FEAT
NCHUNK = SEQ // STRIDE
TOK = NCHUNK - 1
D = 64
H = 8
DK = D // H
TT = 2
ROWS = TT * P
G = 64
INNER = H * D
E = 8
WS = 64
TAPS = 5
STEPS_TO_ABS = 15
NEG = -1e30

F32 = mybir.dt.float32
ALU = mybir.AluOpType
ACT = mybir.ActivationFunctionType
X = mybir.AxisListType.X

QB = P // H
NQ = ROWS // QB
SPAN = [QB * (j + 1) for j in range(NQ)]
BANKS = [[15, 14, 0], [13, 12, 4], [11, 10, 8], [9, 7, 6, 5], [3, 2, 1]]
OFF, BANK_OFF = {}, []
_at = 0
for _bank in BANKS:
    BANK_OFF.append(_at)
    for _j in _bank:
        OFF[_j] = _at
        _at += SPAN[_j]
PACKED = _at
ORDER = [j for bank in BANKS for j in bank]
HALF = NQ // 2
WIDE_OFF = [P * j if j < HALF else P * HALF + 2 * P * (j - HALF) for j in range(NQ)]
WIDE = P * HALF + 2 * P * HALF


def weight_columns():
    sizes = [
        ("tok_w0", P, D), ("tok_w1", P, D), ("tok_b", P, D), ("tok_gamma", P, D), ("tok_beta", P, D),
        ("ident", P, P), ("pad_mask", P, TT), ("head_mask", D, H),
        ("conv", D, TAPS * D), ("conv_b", P, D), ("sqrt_beta", P, D),
        ("ln_w", D, 1), ("ln_b", D, 1), ("ln_b_wide", D, P), ("q_w", D, D), ("k_w", D, D), ("v_w", D, D),
        ("q_b", D, 1), ("k_b", P, 1), ("v_b", P, D), ("out_w", D, D), ("out_b", P, D), ("gammas", P, 1),
        ("fx_wT", D, H * (D + 1)), ("x_w", D, H * D), ("x_b", D, H), ("slice_w", D, G), ("slice_b", D + 1, G),
        ("temp", P, H), ("fq_w", D, D), ("fk_w", D, D), ("fv_w", D, D), ("fout_w", D, H * D), ("fout_b", P, D),
        ("a_q", D, D), ("a_k", D, D), ("a_v", D, D), ("a_proj", D, D), ("a_proj_b", P, D), ("rel", P, WS),
        ("router", D, E), ("w1", D, E * D), ("b1", P, E // 2), ("w2", P, (E // 2) * D), ("b2", E, D),
        ("expand", E, (E // 2) * P), ("last_key", P, QB),
    ]
    cols, at = {}, 0
    for name, rows, width in sizes:
        cols[name] = (at, rows, width)
        at += width
    return cols, at


class Steps:

    def __init__(self, engine, semaphore, per_turn=0, turn=0):
        self.engine, self.semaphore, self.per_turn, self.turn, self.n = engine, semaphore, per_turn, turn, 0

    def step(self, instruction):
        self.n += 1
        instruction.then_inc(self.semaphore, 1)
        return self.n

    def wait(self, n=None):
        n = self.n if n is None else n
        self.engine.wait_ge(self.semaphore, self.turn * self.per_turn + n if self.per_turn else n)

    def link(self, instruction):
        self.step(instruction)
        self.wait()

    def end(self):
        assert not self.per_turn or self.n == self.per_turn, self.n


def bcast(ap, shape):
    return ap.to_broadcast(shape)


def build(nc, x_chunks, weights, packed_tables, out):
    cols, _ = weight_columns()
    top = ExitStack()
    with top:
        def sem(name):
            return top.enter_context(nc.semaphore(name))

        def sb(ctx, name, shape):
            return ctx.enter_context(nc.sbuf_tensor(name, shape, F32))

        W = sb(top, "W", [P, sum(c[2] for c in cols.values())])

        def w(name, rows=None):
            at, r, n = cols[name]
            return W[0:(rows or r), at:at + n]

        h_all = sb(top, "h_all", [P, B * TT, D])
        rstd = sb(top, "rstd", [P, B * TT])
        cen_ctx = ExitStack()
        cen = sb(cen_ctx, "cen_a", [P, B * TT, D])
        psum = top.enter_context(nc.psum_tensor("psum", [P, 8, 512], F32))
        ident = w("ident")

        loaded = sem("weights_loaded")

        centred, squared, ln_steps = sem("ln_centred"), sem("ln_squared"), sem("ln_vector_steps")
        has_var, has_std = sem("ln_has_var"), sem("ln_has_std")
        turns_so_far = []

        def layer_stats(tag, src, cen, eps):
            turn = len(turns_so_far)
            turns_so_far.append(tag)
            with ExitStack() as ctx:
                sq = sb(ctx, f"{tag}_sq", [P, B * TT, D])
                mean = sb(ctx, f"{tag}_mean", [P, B * TT])
                var = sb(ctx, f"{tag}_var", [P, B * TT])
                std = sb(ctx, f"{tag}_std", [P, B * TT])
                nch, per = 4, B * TT // 4
                before = turn * nch
                steps_before = turn * (3 * nch + 2)
                with nc.Block() as block:
                    @block.vector
                    def _(dve):
                        with dve.Fori(0, nch) as c:
                            rows = bass.ds(c * per, per)
                            nc.vector.tensor_reduce(mean[:, rows], src[:, rows, :], X, ALU.add).then_inc(ln_steps, 1)
                            dve.wait_ge(ln_steps, 2 * c + (steps_before + 1))
                            nc.vector.tensor_scalar(mean[:, rows], mean[:, rows], 1.0 / D, None, ALU.mult).then_inc(ln_steps, 1)
                            dve.wait_ge(ln_steps, 2 * c + (steps_before + 2))
                            nc.vector.tensor_tensor(cen[:, rows, :], src[:, rows, :],
                                                    bcast(mean[:, rows][:, :, None], [P, per, D]),
                                                    ALU.subtract).then_inc(centred, 1)
                        with dve.Fori(0, nch) as c:
                            rows = bass.ds(c * per, per)
                            dve.wait_ge(squared, c + (before + 1))
                            nc.vector.tensor_reduce(var[:, rows], sq[:, rows, :], X, ALU.add).then_inc(ln_steps, 1)
                        st = Steps(dve, ln_steps)
                        st.n = steps_before + 3 * nch
                        st.wait()
                        nc.vector.tensor_scalar(var[:], var[:], 1.0 / D, eps, ALU.mult, ALU.add).then_inc(has_var, 1)
                        dve.wait_ge(has_std, turn + 1)
                        st.link(nc.vector.reciprocal(rstd[:], std[:]))
                        st.link(nc.vector.tensor_tensor(
                            rstd[:].rearrange("p (b t) -> p b t", t=TT), rstd[:].rearrange("p (b t) -> p b t", t=TT),
                            bcast(w("pad_mask")[:, None, :], [P, B, TT]), ALU.mult))

                    @block.scalar
                    def _(act):
                        with act.Fori(0, nch) as c:
                            rows = bass.ds(c * per, per)
                            act.wait_ge(centred, c + (before + 1))
                            nc.scalar.activation(sq[:, rows, :], cen[:, rows, :], ACT.Square).then_inc(squared, 1)
                        act.wait_ge(has_var, turn + 1)
                        nc.scalar.activation(std[:], var[:], ACT.Sqrt).then_inc(has_std, 1)

        with ExitStack() as ctx:
            chunks = sb(ctx, "chunks", [P, 2, NCHUNK + 1])
            x_landed = [sem(f"x_landed{u}") for u in range(2)]
            x_used, y_ready, y_used = sem("x_used"), sem("y_ready"), sem("y_used")
            with nc.Block() as block:
                @block.sync
                def _(sp):
                    sp.dma_start(W[:], weights).then_inc(loaded, 16)
                    sp.sem_inc(x_used, 2)
                    with sp.Fori(0, B // 2) as i:
                        for u in range(2):
                            sp.wait_ge(x_used, 2 * i + u + 1)
                            sp.dma_start(chunks[:, u, :], x_chunks[:, bass.ds(2 * i + u, 1), :]
                                         .rearrange("p b c -> p (b c)")).then_inc(x_landed[u], 16)

                @block.tensor
                def _(pe):
                    pe.wait_ge(loaded, 16)
                    pe.sem_inc(y_used, 2)
                    with pe.Fori(0, B // 2) as i:
                        for u in range(2):
                            pe.wait_ge(x_landed[u], i * 16 + 16)
                            pe.wait_ge(y_used, 2 * i + u + 1)
                            for t in range(TT):
                                for half in range(2):
                                    last = nc.tensor.matmul(psum[:, u, t * D:(t + 1) * D],
                                                            chunks[:, u, t * P + half:t * P + half + P],
                                                            w(f"tok_w{half}"), start=(half == 0), stop=(half == 1))
                            last.then_inc(y_ready, 1)
                            pe.wait_ge(y_ready, 2 * i + u + 1)
                            pe.sem_inc(x_used, 1)

                @block.vector
                def _(dve):
                    dve.wait_ge(loaded, 16)
                    with dve.Fori(0, B // 2) as i:
                        for u in range(2):
                            dve.wait_ge(y_ready, 2 * i + u + 1)
                            nc.vector.tensor_tensor(h_all[:, bass.ds((2 * i + u) * TT, TT), :],
                                                    psum[:, u, 0:TT * D].rearrange("p (t d) -> p t d", t=TT),
                                                    bcast(w("tok_b")[:, None, :], [P, TT, D]),
                                                    ALU.add).then_inc(y_used, 1)
        layer_stats("tok_ln", h_all, cen, 1e-5)
        with ExitStack() as ctx:
            scaled = sem("tok_scaled")
            with nc.Block() as block:
                @block.vector
                def _(dve):
                    st = Steps(dve, scaled)
                    full = [P, B * TT, D]
                    st.link(nc.vector.tensor_tensor(h_all[:], cen[:], bcast(rstd[:][:, :, None], full), ALU.mult))
                    st.link(nc.vector.tensor_tensor(h_all[:], h_all[:], bcast(w("tok_gamma")[:, None, :], full), ALU.mult))
                    st.link(nc.vector.tensor_tensor(h_all[:], h_all[:], bcast(w("tok_beta")[:, None, :], full), ALU.add))

        cen_ctx.close()
        conv_x = sb(top, "conv_x", [D, TAPS, D])
        conv_bias = sb(top, "conv_bias", [P, D])
        qkv_x = sb(top, "qkv_x", [D, 3, D])
        q_bias, k_bias = sb(top, "q_bias", [D, 1]), sb(top, "k_bias", [P, 1])
        v_bias = sb(top, "v_bias", [P, D])
        gamma_sq = sb(top, "gamma_sq", [P, 1])
        soft = sb(top, "soft", [P, 4])
        keep_low, keep_high = sb(top, "keep_low", [P, D]), sb(top, "keep_high", [P, D])
        diag_high = sb(top, "diag_high", [D, D])
        w_vector, w_scalar, w_tensor = sem("w_vector"), sem("w_scalar"), sem("w_tensor")
        with nc.Block() as block:
            @block.vector
            def _(dve):
                st = Steps(dve, w_vector)
                v = nc.vector
                st.link(v.tensor_tensor(keep_high[:], w("sqrt_beta"), w("sqrt_beta"), ALU.mult))
                st.link(v.tensor_scalar(keep_low[:], keep_high[:], -1.0, 1.0, ALU.mult, ALU.add))
                st.link(v.tensor_scalar(keep_high[:], keep_high[:], 1.0, None, ALU.add))
                st.step(v.tensor_tensor(conv_bias[:], w("conv_b"), keep_low[:], ALU.mult))
                st.step(v.tensor_tensor(diag_high[:], ident[0:D, 0:D], keep_high[0:D, :], ALU.mult))
                st.step(v.tensor_tensor(conv_x[:], w("conv").rearrange("p (k d) -> p k d", k=TAPS),
                                        bcast(keep_low[0:D, None, :], [D, TAPS, D]), ALU.mult))
                st.wait()
                st.step(v.tensor_tensor(conv_x[:, TAPS - 1, :], conv_x[:, TAPS - 1, :], diag_high[:], ALU.add))
                for n, name in enumerate(("q_w", "k_w", "v_w")):
                    st.step(v.tensor_scalar(qkv_x[:, n, :], w(name), w("ln_w"), None, ALU.mult))
                dve.wait_ge(w_tensor, 3)
                st.step(v.tensor_tensor(q_bias[:], psum[0:D, 0, 0:1], w("q_b"), ALU.add))
                st.step(v.tensor_tensor(k_bias[D:P], psum[D:P, 1, 0:1], w("k_b")[D:P], ALU.add))
                st.step(v.tensor_tensor(v_bias[:], psum[:, 2, 0:D], w("v_b"), ALU.add))
                st.link(v.tensor_scalar(soft[:, 0:1], w("gammas"), -1.0, None, ALU.mult))
                at_abs = st.step(v.tensor_tensor(soft[:, 1:2], soft[:, 0:1], w("gammas"), ALU.min))
                assert at_abs == STEPS_TO_ABS
                st.step(v.tensor_scalar(soft[:, 2:3], w("gammas"), 0.0, None, ALU.max))
                dve.wait_ge(w_scalar, 2)
                st.wait()
                st.link(v.tensor_tensor(soft[:, 2:3], soft[:, 2:3], soft[:, 1:2], ALU.add))
                st.link(v.tensor_tensor(gamma_sq[:], soft[:, 2:3], soft[:, 2:3], ALU.mult))

            @block.scalar
            def _(act):
                act.wait_ge(w_vector, STEPS_TO_ABS)
                nc.scalar.activation(soft[:, 3:4], soft[:, 1:2], ACT.Exp).then_inc(w_scalar, 1)
                act.wait_ge(w_scalar, 1)
                nc.scalar.activation(soft[:, 1:2], soft[:, 3:4], ACT.Ln, bias=1.0).then_inc(w_scalar, 1)

            @block.tensor
            def _(pe):
                nc.tensor.matmul(psum[0:D, 0, 0:1], w("q_w"), w("ln_b"), start=True, stop=True).then_inc(w_tensor, 1)
                nc.tensor.matmul(psum[D:P, 1, 0:1], w("k_w"), w("ln_b"), start=True, stop=True).then_inc(w_tensor, 1)
                nc.tensor.matmul(psum[:, 2, 0:D], w("ln_b_wide"), w("v_w"), start=True, stop=True).then_inc(w_tensor, 1)

        waited_apart = {}

        def wait_apart(engine):
            name = f"waited_apart_{engine.engine.name}"
            if name not in waited_apart:
                waited_apart[name] = sem(name)
            engine.sem_inc(waited_apart[name], 1)

        def seq_rows(ap, b):
            return ap[:, bass.ds(b * TT, TT), :]

        def two_tiles(ap):
            return ap.rearrange("p (t d) -> p t d", t=TT)

        class Signal:

            def __init__(self, name, each=1):
                self.each, self.sem = each, sem(name)

            def done(self, b, n=None, before=0):
                return (b + 2 - before) * self.each + (self.each if n is None else n + 1)

            def event(self, b, n, before):
                return (b + 2) * self.each + n + 1 - before

        def open_signals(sp, signals):
            for s in signals:
                sp.sem_inc(s.sem, 2 * s.each)

        def pipeline(engine, step, ahead, behind):
            def alone(b):
                step(b, b % 2, lambda k: 0 <= b + k < B)
            first, end = (behind + 1) // 2, (B - ahead) // 2
            for b in range(-ahead, 2 * first):
                alone(b)
            with engine.Fori(first, end) as i:
                for u in range(2):
                    step(2 * i + u, u, lambda k: True)
            for b in range(2 * end, B + behind):
                alone(b)

        def normed(stage, u, b, cen):
            return nc.vector.tensor_tensor(
                stage[:, u], seq_rows(cen, b),
                bcast(rstd[:, bass.ds(b * TT, TT)][:, :, None], [P, TT, D]), ALU.mult)

        def transposed_rows(bank, stage, u):
            wait_apart(nc.tensor)
            for t in range(TT):
                last = nc.tensor.transpose(psum[0:D, bank, t * P:(t + 1) * P], stage[:, u, t, :], ident)
            return last

        attn_ctx = ExitStack()
        QK = sb(attn_ctx, "QK", [P, B * ROWS])
        QT, KT = QK[0:D], QK[D:P]
        V = sb(attn_ctx, "V", [P, B * TT, D])
        cen_ctx = ExitStack()
        cen = sb(cen_ctx, "cen_b", [P, B * TT, D])

        with ExitStack() as ctx:
            z = sb(ctx, "z", [P, B * TT, D])
            layer_stats("conv_ln", h_all, cen, 1e-5)
            with ExitStack() as inner:
                stage = sb(inner, "conv_stage", [P, 2, TT, D])
                xT = sb(inner, "conv_xT", [D, 2, TAPS - 1 + ROWS])
                xn_ready, xT_ready, xT_copied = Signal("conv_xn_ready"), Signal("conv_xT_ready"), Signal("conv_xT_copied")
                z_ready, z_copied = Signal("conv_z_ready"), Signal("conv_z_copied")
                padded = sem("conv_padded")
                with nc.Block() as block:
                    @block.sync
                    def _(sp):
                        open_signals(sp, [xn_ready, xT_ready, xT_copied, z_ready, z_copied])

                    @block.vector
                    def _(dve):
                        nc.vector.memset(xT[:, :, 0:TAPS - 1], 0.0).then_inc(padded, 1)
                        with dve.Fori(0, B // 2) as i:
                            for u in range(2):
                                b = 2 * i + u
                                dve.wait_ge(xT_ready.sem, xT_ready.done(b, before=2))
                                normed(stage, u, b, cen).then_inc(xn_ready.sem, 1)
                            for u in range(2):
                                b = 2 * i + u
                                dve.wait_ge(z_ready.sem, z_ready.done(b))
                                nc.vector.tensor_tensor(
                                    seq_rows(z, b), two_tiles(psum[:, 2 + u, 0:TT * D]),
                                    bcast(conv_bias[:, None, :], [P, TT, D]), ALU.add).then_inc(z_copied.sem, 1)

                    @block.scalar
                    def _(act):
                        with act.Fori(0, B // 2) as i:
                            for u in range(2):
                                b = 2 * i + u
                                act.wait_ge(xT_ready.sem, xT_ready.done(b))
                                act.wait_ge(z_ready.sem, z_ready.done(b, before=2))
                                nc.scalar.activation(
                                    xT[:, u, TAPS - 1:], psum[0:D, u, 0:ROWS], ACT.Copy).then_inc(xT_copied.sem, 1)

                    @block.tensor
                    def _(pe):
                        pe.wait_ge(padded, 1)
                        with pe.Fori(0, B // 2) as i:
                            for u in range(2):
                                b = 2 * i + u
                                pe.wait_ge(xn_ready.sem, xn_ready.done(b))
                                pe.wait_ge(xT_copied.sem, xT_copied.done(b, before=2))
                                transposed_rows(u, stage, u).then_inc(xT_ready.sem, 1)
                            for u in range(2):
                                b = 2 * i + u
                                pe.wait_ge(xT_copied.sem, xT_copied.done(b))
                                pe.wait_ge(z_copied.sem, z_copied.done(b, before=2))
                                for t in range(TT):
                                    for k in range(TAPS):
                                        last = nc.tensor.matmul(psum[:, 2 + u, t * D:(t + 1) * D],
                                                                xT[:, u, t * P + k:t * P + k + P], conv_x[:, k, :],
                                                                start=(k == 0), stop=(k == TAPS - 1))
                                last.then_inc(z_ready.sem, 1)

            layer_stats("qkv_ln", z, cen, 1e-12)
            with ExitStack() as inner:
                stage = sb(inner, "qkv_stage", [P, 2, TT, D])
                zT = sb(inner, "qkv_zT", [D, 2, ROWS])
                zn_ready, zT_ready, zT_copied = Signal("qkv_zn_ready"), Signal("qkv_zT_ready"), Signal("qkv_zT_copied")
                qkv_ready, qv_copied, k_copied = Signal("qkv_ready"), Signal("qv_copied"), Signal("k_copied")
                with nc.Block() as block:
                    @block.sync
                    def _(sp):
                        open_signals(sp, [zn_ready, zT_ready, zT_copied, qkv_ready, qv_copied, k_copied])

                    @block.vector
                    def _(dve):
                        with dve.Fori(0, B // 2) as i:
                            for u in range(2):
                                b = 2 * i + u
                                dve.wait_ge(zT_ready.sem, zT_ready.done(b, before=2))
                                normed(stage, u, b, cen).then_inc(zn_ready.sem, 1)
                            for u in range(2):
                                b = 2 * i + u
                                dve.wait_ge(qkv_ready.sem, qkv_ready.done(b))
                                nc.vector.tensor_scalar(QT[:, bass.ds(b * ROWS, ROWS)], psum[0:D, 2 + u, 0:ROWS],
                                                        q_bias[:], DK ** -0.5, ALU.add, ALU.mult)
                                nc.vector.tensor_tensor(
                                    seq_rows(V, b), two_tiles(psum[:, 4 + u, 0:TT * D]),
                                    bcast(v_bias[:, None, :], [P, TT, D]), ALU.add).then_inc(qv_copied.sem, 1)

                    @block.scalar
                    def _(act):
                        with act.Fori(0, B // 2) as i:
                            for u in range(2):
                                b = 2 * i + u
                                act.wait_ge(zT_ready.sem, zT_ready.done(b))
                                act.wait_ge(qkv_ready.sem, qkv_ready.done(b, before=2))
                                nc.scalar.activation(zT[:, u], psum[0:D, u, 0:ROWS], ACT.Copy).then_inc(zT_copied.sem, 1)
                            for u in range(2):
                                b = 2 * i + u
                                act.wait_ge(qkv_ready.sem, qkv_ready.done(b))
                                nc.scalar.activation(
                                    KT[:, bass.ds(b * ROWS, ROWS)], psum[D:P, 2 + u, 0:ROWS],
                                    ACT.Identity, bias=k_bias[D:P]).then_inc(k_copied.sem, 1)

                    @block.tensor
                    def _(pe):
                        with pe.Fori(0, B // 2) as i:
                            for u in range(2):
                                b = 2 * i + u
                                pe.wait_ge(zn_ready.sem, zn_ready.done(b))
                                pe.wait_ge(zT_copied.sem, zT_copied.done(b, before=2))
                                transposed_rows(u, stage, u).then_inc(zT_ready.sem, 1)
                            for u in range(2):
                                b = 2 * i + u
                                pe.wait_ge(zT_copied.sem, zT_copied.done(b))
                                pe.wait_ge(qv_copied.sem, qv_copied.done(b, before=2))
                                pe.wait_ge(k_copied.sem, k_copied.done(b, before=2))
                                wait_apart(pe)
                                for n in range(2):
                                    nc.tensor.matmul(psum[n * D:(n + 1) * D, 2 + u, 0:ROWS], qkv_x[:, n, :],
                                                     zT[:, u], start=True, stop=True)
                                for t in range(TT):
                                    last = nc.tensor.matmul(psum[:, 4 + u, t * D:(t + 1) * D],
                                                            zT[:, u, t * P:(t + 1) * P], qkv_x[:, 2, :],
                                                            start=True, stop=True)
                                last.then_inc(qkv_ready.sem, 1)

        cen_ctx.close()
        with ExitStack() as ctx:
            tables = sb(ctx, "tables_sb", [P, 2, PACKED])
            distance, no_reset = tables[:, 0], tables[:, 1]
            causal = sb(ctx, "causal", [P, 2 * P])
            Qd = sb(ctx, "Qd", [D, 2, NQ, H, QB])
            Kb = sb(ctx, "Kb", [D, 2, ROWS])
            VM_COLS = 2 * H * P
            Vm = sb(ctx, "Vm", [P, 2, VM_COLS + P])
            S = sb(ctx, "S", [P, 2, PACKED])
            Ex = sb(ctx, "Ex", [P, 2, PACKED + 1])
            PT = sb(ctx, "PT", [P, 2, WIDE])
            Y = Ex[:, :, 1:]
            S2 = sb(ctx, "S2", [P, 2, WIDE])
            top1, top2 = sb(ctx, "top1", [P, 2, NQ]), sb(ctx, "top2", [P, 2, NQ])
            neg_top, total = sb(ctx, "neg_top", [P, 2, NQ]), sb(ctx, "total", [P, 2, NQ])
            scale = sb(ctx, "scale", [P, 2, NQ])
            inv = sb(ctx, "inv", [D, 2, ROWS])
            oT = sb(ctx, "oT", [D, 2, ROWS])
            k_landed = [sem(f"k_landed{u}") for u in range(2)]
            NB = len(BANKS)
            PARTS = [slice(0, BANK_OFF[2]), slice(BANK_OFF[2], PACKED)]
            tables_landed, prepared, pool_prepared = sem("tables_landed"), sem("prepared"), sem("pool_prepared")
            q_ready, v_ready, y_ready1 = Signal("qd_ready"), Signal("vm_ready"), Signal("dist_ready")
            s_ready, top_ready = Signal("s_ready", NB), Signal("top_ready", NB)
            e_ready, scan_ready, root_ready, te_ready, y_used = Signal("e_ready"), Signal("scan_ready"), Signal("root_ready"), Signal("te_ready", 2), Signal("effects_used")
            s2_ready, t_ready, p_ready = Signal("s2_ready", 2), Signal("t_ready", 3), Signal("p_ready", 3)
            pv_ready, o_ready, y_done, h_added = Signal("pv_ready"), Signal("o_ready"), Signal("proj_ready"), Signal("h_added")
            max_steps, scale_steps = sem("attn_max_steps"), sem("attn_scale_steps")
            shift_steps, out_steps = sem("attn_shift_steps"), sem("attn_out_steps")

            with nc.Block() as block:
                @block.sync
                def _(sp):
                    sp.dma_start(tables[:], packed_tables).then_inc(tables_landed, 16)
                    open_signals(sp, [q_ready, v_ready, y_ready1, s_ready, top_ready, e_ready, scan_ready, root_ready,
                              te_ready, y_used, s2_ready, t_ready, p_ready, pv_ready, o_ready, y_done, h_added])
                    with sp.Fori(0, B // 2) as i:
                        for u in range(2):
                            b = 2 * i + u
                            sp.wait_ge(s_ready.sem, s_ready.done(b, before=2))
                            sp.dma_start(Kb[:, u], KT[:, bass.ds(b * ROWS, ROWS)]).then_inc(k_landed[u], 16)

                @block.gpsimd
                def _(pool):
                    g = nc.gpsimd
                    g.memset(Vm[:], 0.0).then_inc(pool_prepared, 1)
                    pool.wait_ge(pool_prepared, 1)
                    for u in range(2):
                        for kb in range(2):
                            at = kb * H * P
                            ones = Vm[:, u, at + D:at + D + H * (P + DK)].rearrange("p (h s) -> p h s", h=H)[:, :, 0:DK]
                            last = g.memset(ones, 1.0)
                    last.then_inc(pool_prepared, 1)
                    pool.wait_ge(pool_prepared, 2)
                    pool.wait_ge(tables_landed, 16)
                    pool.wait_ge(prepared, 1)

                    def queries(b, u):
                        pool.wait_ge(s_ready.sem, s_ready.done(b, before=2))
                        qs = QT[:, bass.ds(b * ROWS, ROWS)].rearrange("p (j q) -> p j q", j=NQ)
                        g.tensor_tensor(
                            Qd[:, u], bcast(qs[:, :, None, :], [D, NQ, H, QB]),
                            bcast(w("head_mask")[:, None, :, None], [D, NQ, H, QB]), ALU.mult).then_inc(q_ready.sem, 1)

                    def values(b, u):
                        pool.wait_ge(pv_ready.sem, pv_ready.done(b, before=2))
                        for kb in range(2):
                            at = kb * H * P
                            mine = Vm[:, u, at:at + H * (P + DK)].rearrange("p (h s) -> p h s", h=H)[:, :, 0:DK]
                            last = g.tensor_copy(mine, V[:, bass.ds(b * TT + kb, 1), :]
                                                 .rearrange("p t (h d) -> p (t h) d", h=H))
                        last.then_inc(v_ready.sem, 1)

                    def distances(b, u):
                        pool.wait_ge(scan_ready.sem, scan_ready.done(b))
                        g.tensor_tensor(Y[:, u], Y[:, u], distance, ALU.mult).then_inc(y_ready1.sem, 1)

                    def step(b, u, there):
                        if there(2):
                            queries(b + 2, u)
                        if there(-1):
                            values(b - 1, 1 - u)
                        if there(1):
                            distances(b + 1, 1 - u)
                    pipeline(pool, step, 2, 3)

                @block.tensor
                def _(pe):
                    t_ = nc.tensor

                    def scores(b, u):
                        pe.wait_ge(q_ready.sem, q_ready.done(b))
                        pe.wait_ge(k_landed[u], 8 * (b - u) + 16)
                        for n, bank in enumerate(BANKS):
                            pe.wait_ge(top_ready.sem, top_ready.event(b, n, before=2))
                            for j in bank:
                                at = OFF[j] - BANK_OFF[n]
                                last = t_.matmul(psum[:, (u * NB + n) % 2, at:at + SPAN[j]],
                                                 Qd[:, u, j].rearrange("p h q -> p (h q)"),
                                                 Kb[:, u, 0:SPAN[j]], start=True, stop=True)
                            last.then_inc(s_ready.sem, 1)

                    def transposes(b, u):
                        for c in range(3):
                            pe.wait_ge(s2_ready.sem, s2_ready.done(b, min(c, 1)))
                            pe.wait_ge(p_ready.sem, p_ready.event(b, c, before=2))
                            for n in range(HALF):
                                at = P * n if c == 0 else WIDE_OFF[HALF + n] + P * (c - 1)
                                last = t_.transpose(
                                    psum[:, 2 + 2 * ((3 * u + c) % 2) + n // 4, (n % 4) * P:(n % 4 + 1) * P],
                                    S2[:, u, at:at + P], ident)
                            last.then_inc(t_ready.sem, 1)

                    def weighted_values(b, u):
                        pe.wait_ge(v_ready.sem, v_ready.done(b))
                        pe.wait_ge(p_ready.sem, p_ready.done(b))
                        pe.wait_ge(h_added.sem, h_added.done(b, before=2))
                        probs = PT[:, u].rearrange("p (n q) -> p n q", q=P)
                        for h in range(H):
                            vm = [Vm[:, u, (kb * H + h) * P:(kb * H + h + 1) * P] for kb in range(2)]
                            for kb in ((0, 1) if h == 0 else (1, 0)):
                                mine = (probs[:, 0:NQ] if kb == 0 else probs[:, NQ:])[:, :, h * QB:(h + 1) * QB]
                                last = t_.matmul(psum[:, 6 + u, kb * P:ROWS], vm[kb], mine,
                                                 start=(h == 0 and kb == 0), stop=(h == H - 1 and kb == 0),
                                                 skip_group_check=True)
                        last.then_inc(pv_ready.sem, 1)

                    def projection(b, u):
                        pe.wait_ge(o_ready.sem, o_ready.done(b))
                        for t in range(TT):
                            last = t_.matmul(psum[:, 6 + u, ROWS + t * D:ROWS + (t + 1) * D], oT[:, u, t * P:(t + 1) * P],
                                             w("out_w"), start=True, stop=True)
                        last.then_inc(y_done.sem, 1)

                    def step(b, u, there):
                        if there(1):
                            scores(b + 1, 1 - u)
                        if there(-3):
                            projection(b - 3, 1 - u)
                        if there(-2):
                            weighted_values(b - 2, u)
                        if there(-1):
                            transposes(b - 1, 1 - u)
                    pipeline(pe, step, 2, 3)

                @block.scalar
                def _(act):
                    a = nc.scalar

                    def exponentials(b, u):
                        act.wait_ge(y_used.sem, y_used.done(b, before=2))
                        for n, bank in enumerate(BANKS):
                            act.wait_ge(top_ready.sem, top_ready.done(b, n))
                            for j in bank:
                                k = ORDER.index(j)
                                last = a.activation(
                                    Ex[:, u, OFF[j]:OFF[j] + SPAN[j]], S[:, u, OFF[j]:OFF[j] + SPAN[j]], ACT.Exp,
                                    bias=neg_top[:, u, k:k + 1], accum_out=total[:, u, k:k + 1])
                        last.then_inc(e_ready.sem, 1)

                    def roots(b, u):
                        act.wait_ge(y_ready1.sem, y_ready1.done(b))
                        for k, j in enumerate(ORDER):
                            at = Y[:, u, OFF[j]:OFF[j] + SPAN[j]]
                            last = a.activation(at, at, ACT.Sqrt, scale=scale[:, u, k:k + 1])
                        last.then_inc(root_ready.sem, 1)

                    def effects(b, u):
                        act.wait_ge(root_ready.sem, root_ready.done(b))
                        for part in PARTS:
                            a.activation(Y[:, u, part], Y[:, u, part], ACT.Exp, scale=-1.0).then_inc(te_ready.sem, 1)

                    def probabilities(b, u):
                        act.wait_ge(pv_ready.sem, pv_ready.done(b, before=2))
                        for c in range(3):
                            act.wait_ge(t_ready.sem, t_ready.done(b, c))
                            bank = 2 + 2 * ((3 * u + c) % 2)
                            a.activation(
                                PT[:, u, c * HALF * P:(c + 1) * HALF * P].rearrange("p (n q) -> p n q", q=P),
                                psum[:, bank:bank + 2, :].rearrange("p k (n q) -> p (k n) q", q=P), ACT.Exp).then_inc(p_ready.sem, 1)

                    def step(b, u, there):
                        if there(1):
                            exponentials(b + 1, 1 - u)
                        if there(0):
                            roots(b, u)
                            effects(b, u)
                        if there(-1):
                            probabilities(b - 1, 1 - u)
                    pipeline(act, step, 2, 3)

                @block.vector
                def _(dve):
                    v = nc.vector
                    v.memset(S2[:], NEG)
                    v.memset(oT[:], 0.0)
                    v.memset(Ex[:, :, PACKED:], 0.0)
                    v.memset(causal[:], 0.0).then_inc(prepared, 1)
                    dve.wait_ge(prepared, 1)
                    v.tensor_copy(causal[:, 2 * P - QB:], w("last_key")).then_inc(prepared, 1)
                    dve.wait_ge(prepared, 2)
                    dve.wait_ge(tables_landed, 16)

                    def masked_scores(b, u):
                        dve.wait_ge(e_ready.sem, e_ready.done(b, before=2))
                        dve.wait_ge(y_used.sem, y_used.done(b, before=2))
                        for n, bank in enumerate(BANKS):
                            dve.wait_ge(s_ready.sem, s_ready.done(b, n))
                            wait_apart(dve)
                            for j in bank:
                                k = ORDER.index(j)
                                at = OFF[j] - BANK_OFF[n]
                                last = v.tensor_tensor_reduce(
                                    S[:, u, OFF[j]:OFF[j] + SPAN[j]], psum[:, (u * NB + n) % 2, at:at + SPAN[j]],
                                    causal[:, 2 * P - SPAN[j]:], 1.0, -3e38, ALU.add, ALU.max, top1[:, u, k:k + 1])
                            last.then_inc(max_steps, 1)
                            k0 = ORDER.index(bank[0])
                            dve.wait_ge(max_steps, b * NB + n + 1)
                            v.tensor_scalar(
                                neg_top[:, u, k0:k0 + len(bank)], top1[:, u, k0:k0 + len(bank)], -1.0, None, ALU.mult).then_inc(top_ready.sem, 1)

                    def later_sums(b, u):
                        st = Steps(dve, scale_steps, 2, b)
                        dve.wait_ge(e_ready.sem, e_ready.done(b))
                        dve.wait_ge(root_ready.sem, root_ready.done(b, before=2))
                        st.link(v.reciprocal(scale[:, u], total[:, u]))
                        st.step(v.tensor_scalar(scale[:, u], scale[:, u], gamma_sq[:], None, ALU.mult))
                        v.tensor_tensor_scan(
                            Ex[:, u, 0:PACKED][:, ::-1], no_reset[:, ::-1], Ex[:, u, 0:PACKED][:, ::-1],
                            0.0, ALU.mult, ALU.add).then_inc(scan_ready.sem, 1)
                        st.end()

                    def scaled_scores(b, u):
                        st = Steps(dve, shift_steps, 2, b)
                        dve.wait_ge(t_ready.sem, t_ready.done(b, before=2))
                        for j in ORDER:
                            for n, part in enumerate(PARTS):
                                if OFF[j] == part.start:
                                    dve.wait_ge(te_ready.sem, te_ready.done(b, n))
                                    st.link(v.tensor_scalar(Y[:, u, part], Y[:, u, part], 1e-5, 1e5, ALU.max, ALU.min))
                                    wait_apart(dve)
                            last = v.tensor_tensor_reduce(
                                S2[:, u, WIDE_OFF[j]:WIDE_OFF[j] + SPAN[j]], Y[:, u, OFF[j]:OFF[j] + SPAN[j]],
                                S[:, u, OFF[j]:OFF[j] + SPAN[j]], 1.0, -3e38, ALU.mult, ALU.max, top2[:, u, j:j + 1])
                        last.then_inc(y_used.sem, 1)
                        st.end()

                    def shifted_scores(b, u):
                        dve.wait_ge(y_used.sem, y_used.done(b))
                        for j in range(NQ):
                            at = S2[:, u, WIDE_OFF[j]:WIDE_OFF[j] + SPAN[j]]
                            last = v.tensor_scalar(at, at, top2[:, u, j:j + 1], None, ALU.subtract)
                            if j in (HALF - 1, NQ - 1):
                                last.then_inc(s2_ready.sem, 1)

                    def heads_outputs(b, u):
                        st = Steps(dve, out_steps, 2, b)
                        dve.wait_ge(pv_ready.sem, pv_ready.done(b))
                        dve.wait_ge(y_done.sem, y_done.done(b, before=2))
                        st.link(v.reciprocal(inv[:, u], psum[D:2 * D, 6 + u, 0:ROWS]))
                        v.tensor_tensor(oT[:, u, 1:], psum[0:D, 6 + u, 1:ROWS], inv[:, u, 1:], ALU.mult).then_inc(o_ready.sem, 1)
                        st.link(v.tensor_tensor(seq_rows(h_all, b), seq_rows(h_all, b),
                                                bcast(w("out_b")[:, None, :], [P, TT, D]), ALU.add))
                        st.end()

                    def added(b, u):
                        dve.wait_ge(y_done.sem, y_done.done(b))
                        v.tensor_tensor(seq_rows(h_all, b), seq_rows(h_all, b),
                                        two_tiles(psum[:, 6 + u, ROWS:ROWS + TT * D]), ALU.add).then_inc(h_added.sem, 1)

                    def step(b, u, there):
                        if there(-1):
                            scaled_scores(b - 1, 1 - u)
                        if there(1):
                            masked_scores(b + 1, 1 - u)
                        if there(-3):
                            heads_outputs(b - 3, 1 - u)
                        if there(-1):
                            shifted_scores(b - 1, 1 - u)
                        if there(1):
                            later_sums(b + 1, 1 - u)
                        if there(-3):
                            added(b - 3, 1 - u)
                    pipeline(dve, step, 2, 3)
        attn_ctx.close()
        cen = sb(top, "cen_c", [P, B * TT, D])
        HP = H // 2
        with ExitStack() as ctx:
            layer_stats("ffn_ln", h_all, cen, 1e-5)
            D1 = D + 1
            logit_w = sb(ctx, "logit_w", [D1, H, G])
            mix_w = sb(ctx, "mix_w", [D1, H, D1])
            vo_w = sb(ctx, "vo_w", [D1, H, D])
            inv_temp = sb(ctx, "inv_temp", [P, H])
            fw_tensor, fw_vector = sem("fw_tensor"), sem("fw_vector")
            with ExitStack() as inner, nc.Block() as block:
                kq = sb(inner, "kq", [D, D])
                kq_fx = sb(inner, "kq_fx", [D, H, D1])
                vo = sb(inner, "vo", [D, H, D])
                fx_wT = w("fx_wT").rearrange("p (h c) -> p h c", h=H)
                STEPS_TO_KQ, STEPS_TO_KQ_FX = 2, 4
                @block.tensor
                def _(pe):
                    for h in range(H):
                        nc.tensor.matmul(psum[0:D, 0, h * G:(h + 1) * G], w("x_w")[:, h * D:(h + 1) * D], w("slice_w"),
                                         start=True, stop=True)
                    for h in range(H):
                        nc.tensor.matmul(psum[D:D1, 3, h * G:(h + 1) * G], w("x_b")[:, h:h + 1], w("slice_w"),
                                         start=True, stop=True)
                    nc.tensor.matmul(psum[0:D, 1, 0:D], w("fk_w"), w("fq_w"), start=True, stop=True)
                    nc.tensor.matmul(psum[0:D, 2, :], w("fv_w"), w("fout_w"), start=True, stop=True).then_inc(fw_tensor, 1)
                    pe.wait_ge(fw_vector, STEPS_TO_KQ)
                    for half in range(2):
                        nc.tensor.matmul(psum[0:D, 4 + half, 0:HP * D1], kq[:], fx_wT[:, half * HP:(half + 1) * HP]
                                         .rearrange("p h c -> p (h c)"), start=True, stop=True)
                    for h in range(H):
                        last = nc.tensor.matmul(psum[0:D1, 6, h * D:(h + 1) * D], fx_wT[:, h], vo[:, h], start=True, stop=True)
                    last.then_inc(fw_tensor, 1)
                    pe.wait_ge(fw_vector, STEPS_TO_KQ_FX)
                    for h in range(H):
                        last = nc.tensor.matmul(psum[0:D1, 1 + h // HP, (h % HP) * D1:(h % HP + 1) * D1], fx_wT[:, h],
                                                kq_fx[:, h], start=True, stop=True)
                    last.then_inc(fw_tensor, 1)

                @block.vector
                def _(dve):
                    v = nc.vector
                    st = Steps(dve, fw_vector)
                    dve.wait_ge(fw_tensor, 1)
                    st.step(v.tensor_copy(kq[:], psum[0:D, 1, 0:D]))
                    st.step(v.tensor_copy(vo[:], psum[0:D, 2, :].rearrange("p (h g) -> p h g", h=H)))
                    assert st.n == STEPS_TO_KQ
                    dve.wait_ge(fw_tensor, 2)
                    st.step(v.tensor_copy(kq_fx[:].rearrange("p (k h) c -> p k (h c)", k=2), psum[0:D, 4:6, 0:HP * D1]))
                    st.step(v.tensor_copy(vo_w[:], psum[0:D1, 6, :].rearrange("p (h g) -> p h g", h=H)))
                    assert st.n == STEPS_TO_KQ_FX
                    st.link(v.tensor_scalar(inv_temp[:], w("temp"), 0.1, 5.0, ALU.max, ALU.min))
                    st.link(v.reciprocal(inv_temp[:], inv_temp[:]))
                    v.tensor_tensor(logit_w[0:D], psum[0:D, 0, :].rearrange("p (h g) -> p h g", h=H),
                                    bcast(inv_temp[0:D, :, None], [D, H, G]), ALU.mult)
                    st.link(v.tensor_tensor(logit_w[D:D1], psum[D:D1, 3, :].rearrange("p (h g) -> p h g", h=H),
                                            bcast(w("slice_b")[D:D1, None, :], [1, H, G]), ALU.add))
                    v.tensor_tensor(logit_w[D:D1], logit_w[D:D1], bcast(inv_temp[D:D1, :, None], [1, H, G]), ALU.mult)
                    dve.wait_ge(fw_tensor, 3)
                    v.tensor_copy(mix_w[:].rearrange("p (k h) c -> p k (h c)", k=2), psum[0:D1, 1:3, 0:HP * D1])

            xn = sb(ctx, "ffn_xn", [P, 2, TT, D1])
            xT = sb(ctx, "ffn_xT", [D1, 2, ROWS])
            Wn = sb(ctx, "Wn", [P, 2, TT, H, G])
            WT = sb(ctx, "WT", [P, 2, HP, ROWS])
            wtop, winv = sb(ctx, "wtop", [P, 2, TT, H]), sb(ctx, "winv", [P, 2, TT, H])
            slice_inv, row_stat = sb(ctx, "slice_inv", [P, 2, HP]), sb(ctx, "row_stat", [P, 2, HP])
            ST = sb(ctx, "ST", [P, 2, HP, D1])
            stT = sb(ctx, "stT", [D1, 2, H, G])
            mixT = sb(ctx, "mixT", [D1, 2, H, G])
            VO = sb(ctx, "VO", [G, 2, H, D])
            A = sb(ctx, "A", [P, 2, HP, G])
            aT = sb(ctx, "aT", [G, 2, H, G])
            OW = sb(ctx, "OW", [P, 2, HP, D])
            X_BANK, LOGIT_BANK, W_BANK, SLICE_BANK, SCORE_BANK, ROW_BANK = 0, 1, 3, 5, 6, 7
            ST_BANK, VO_BANK, MIX_BANK = W_BANK, W_BANK + 1, SLICE_BANK
            names = ["xn", "xT", "xT_sb", "logits", "shifted", "exped", "winv", "wn", "slices", "wT",
                     "wT_sb", "slices_sb", "stT", "stT_sb", "mix_vo", "mixT_sb", "vo_sb", "scores", "sc_shifted",
                     "sc_exped", "attn", "aT", "aT_sb", "ow", "ow_sb", "rows", "h_added"]
            at = {n: Signal(f"ffn_{n}") for n in names}
            top_steps, sum_steps, mean_steps = sem("ffn_top_steps"), sem("ffn_sum_steps"), sem("ffn_mean_steps")
            score_steps, attn_steps, row_steps = sem("ffn_score_steps"), sem("ffn_attn_steps"), sem("ffn_row_steps")
            ready = sem("ffn_prepared")

            def after(engine, name, b, before=0):
                engine.wait_ge(at[name].sem, at[name].done(b, before=before))

            with nc.Block() as block:
                @block.sync
                def _(sp):
                    open_signals(sp, list(at.values()))

                @block.tensor
                def _(pe):
                    t_ = nc.tensor

                    def transpose_x(b, u):
                        after(pe, "xn", b)
                        after(pe, "xT_sb", b, 1)
                        wait_apart(pe)
                        for t in range(TT):
                            last = t_.transpose(psum[0:D, X_BANK, t * P:(t + 1) * P], xn[:, u, t, 0:D], ident)
                        last.then_inc(at["xT"].sem, 1)

                    def logits(b, u):
                        after(pe, "xT_sb", b)
                        after(pe, "shifted", b, 1)
                        for t in range(TT):
                            last = t_.matmul(psum[:, LOGIT_BANK + t, :], xT[:, u, t * P:(t + 1) * P],
                                             logit_w[:].rearrange("p h g -> p (h g)"), start=True, stop=True)
                        last.then_inc(at["logits"].sem, 1)

                    def slices(b, u):
                        after(pe, "wn", b)
                        after(pe, "stT_sb", b, 1)
                        after(pe, "vo_sb", b, 1)
                        for t in range(TT):
                            for hp in range(HP):
                                last = t_.transpose(psum[:, W_BANK + hp // 2, (hp % 2) * ROWS + t * P:(hp % 2) * ROWS + (t + 1) * P],
                                                    Wn[:, u, t, 2 * hp:2 * hp + 2, :].rearrange("p h g -> p (h g)"), ident)
                        last.then_inc(at["wT"].sem, 1)
                        after(pe, "mixT_sb", b, 1)
                        for hp in range(HP):
                            for t in range(TT):
                                last = t_.matmul(psum[:, SLICE_BANK, hp * D1:(hp + 1) * D1],
                                                 Wn[:, u, t, 2 * hp:2 * hp + 2, :].rearrange("p h g -> p (h g)"),
                                                 xn[:, u, t, :], start=(t == 0), stop=(t == TT - 1))
                        last.then_inc(at["slices"].sem, 1)

                    def transpose_slices(b, u):
                        after(pe, "slices_sb", b)
                        after(pe, "wT_sb", b)
                        wait_apart(pe)
                        for hp in range(HP):
                            last = t_.transpose(psum[0:D1, ST_BANK, hp * P:(hp + 1) * P], ST[:, u, hp, :], ident)
                        last.then_inc(at["stT"].sem, 1)

                    def mix(b, u):
                        after(pe, "stT_sb", b)
                        wait_apart(pe)
                        for h in range(H):
                            t_.matmul(psum[0:D1, MIX_BANK, h * G:(h + 1) * G], mix_w[:, h], stT[:, u, h, :], start=True, stop=True)
                        for h in range(H):
                            last = t_.matmul(psum[0:G, VO_BANK, h * D:(h + 1) * D], stT[:, u, h, :], vo_w[:, h, :],
                                             start=True, stop=True)
                        last.then_inc(at["mix_vo"].sem, 1)

                    def scores(b, u):
                        after(pe, "mixT_sb", b)
                        after(pe, "ow_sb", b, 1)
                        wait_apart(pe)
                        for h in range(H):
                            last = t_.matmul(psum[(h % 2) * G:(h % 2 + 1) * G, SCORE_BANK, (h // 2) * G:(h // 2 + 1) * G],
                                             mixT[:, u, h, :], stT[:, u, h, :], start=True, stop=True)
                        last.then_inc(at["scores"].sem, 1)

                    def transpose_attention(b, u):
                        after(pe, "attn", b)
                        after(pe, "h_added", b, 1)
                        wait_apart(pe)
                        for hp in range(HP):
                            last = t_.transpose(psum[0:G, ROW_BANK, hp * P:(hp + 1) * P], A[:, u, hp, :], ident)
                        last.then_inc(at["aT"].sem, 1)

                    def attended(b, u):
                        after(pe, "aT_sb", b)
                        after(pe, "vo_sb", b)
                        wait_apart(pe)
                        for h in range(H):
                            last = t_.matmul(psum[(h % 2) * G:(h % 2 + 1) * G, SCORE_BANK, (h // 2) * D:(h // 2 + 1) * D],
                                             aT[:, u, h, :], VO[:, u, h, :], start=True, stop=True)
                        last.then_inc(at["ow"].sem, 1)

                    def rows_out(b, u):
                        after(pe, "ow_sb", b)
                        for t in range(TT):
                            for hp in range(HP):
                                last = t_.matmul(psum[:, ROW_BANK, t * D:(t + 1) * D], WT[:, u, hp, t * P:(t + 1) * P],
                                                 OW[:, u, hp, :], start=(hp == 0), stop=(hp == HP - 1))
                        last.then_inc(at["rows"].sem, 1)

                    def step(b, u, there):
                        if there(1):
                            transpose_x(b + 1, 1 - u)
                        if there(-1):
                            scores(b - 1, 1 - u)
                        if there(1):
                            logits(b + 1, 1 - u)
                        if there(-1):
                            transpose_attention(b - 1, 1 - u)
                        if there(0):
                            slices(b, u)
                        if there(-1):
                            attended(b - 1, 1 - u)
                        if there(0):
                            transpose_slices(b, u)
                        if there(-1):
                            rows_out(b - 1, 1 - u)
                        if there(0):
                            mix(b, u)

                    pe.wait_ge(ready, 1)
                    pipeline(pe, step, 2, 1)

                @block.scalar
                def _(act):
                    a = nc.scalar

                    def step(b, u, there):
                        x, y = 1 - u, 1 - u
                        if there(1):
                            after(act, "xT", b + 1)
                            after(act, "logits", b + 1, 2)
                            a.activation(xT[0:D, x], psum[0:D, X_BANK, 0:ROWS], ACT.Copy).then_inc(at["xT_sb"].sem, 1)
                        if there(-1):
                            after(act, "sc_shifted", b - 1)
                            a.activation(A[:, y], A[:, y], ACT.Exp).then_inc(at["sc_exped"].sem, 1)
                            after(act, "aT", b - 1)
                            after(act, "ow", b - 1, 2)
                            a.activation(aT[:, y].rearrange("p h g -> p (h g)"), psum[0:G, ROW_BANK, :],
                                         ACT.Copy).then_inc(at["aT_sb"].sem, 1)
                        if there(1):
                            after(act, "shifted", b + 1)
                            a.activation(Wn[:, x], Wn[:, x], ACT.Exp).then_inc(at["exped"].sem, 1)
                        if there(0):
                            after(act, "wT", b)
                            after(act, "rows", b, 2)
                            a.activation(WT[:, u].rearrange("p h n -> p (h n)"),
                                         psum[:, W_BANK:W_BANK + 2, :].rearrange("p k n -> p (k n)"),
                                         ACT.Copy).then_inc(at["wT_sb"].sem, 1)
                            after(act, "stT", b)
                            after(act, "scores", b, 2)
                            a.activation(stT[:, u].rearrange("p h g -> p (h g)"), psum[0:D1, ST_BANK, :],
                                         ACT.Copy).then_inc(at["stT_sb"].sem, 1)
                            after(act, "mix_vo", b)
                            a.activation(mixT[:, u].rearrange("p h g -> p (h g)"), psum[0:D1, MIX_BANK, :],
                                         ACT.Copy, scale=D ** -0.5).then_inc(at["mixT_sb"].sem, 1)
                    pipeline(act, step, 2, 1)

                @block.gpsimd
                def _(pool):
                    def step(b, u, there):
                        if there(1):
                            after(pool, "winv", b + 1)
                            wn = Wn[:, 1 - u].rearrange("p t h g -> p (t h) g")
                            nc.gpsimd.tensor_tensor(
                                wn, wn, bcast(winv[:, 1 - u].rearrange("p t h -> p (t h)")[:, :, None], [P, TT * H, G]),
                                ALU.mult).then_inc(at["wn"].sem, 1)
                    pipeline(pool, step, 2, 1)

                @block.vector
                def _(dve):
                    v = nc.vector
                    v.memset(xT[D:D1], 1.0)
                    v.memset(xn[:, :, :, D:], 1.0).then_inc(ready, 1)

                    def normalised(b, u):
                        after(dve, "slices", b, 2)
                        v.tensor_tensor(xn[:, u, :, 0:D], seq_rows(cen, b),
                                        bcast(rstd[:, bass.ds(b * TT, TT)][:, :, None], [P, TT, D]),
                                        ALU.mult).then_inc(at["xn"].sem, 1)

                    def less_top(b, u):
                        st = Steps(dve, top_steps, 1, b)
                        after(dve, "logits", b)
                        after(dve, "slices", b, 2)
                        lg = psum[:, LOGIT_BANK:LOGIT_BANK + 2, :].rearrange("p t (h g) -> p (t h) g", g=G)
                        wt = wtop[:, u].rearrange("p t h -> p (t h)")
                        st.link(v.tensor_reduce(wt, lg, X, ALU.max))
                        v.tensor_tensor(Wn[:, u].rearrange("p t h g -> p (t h) g"), lg,
                                        bcast(wt[:, :, None], [P, TT * H, G]), ALU.subtract).then_inc(at["shifted"].sem, 1)

                    def weight_sums(b, u):
                        st = Steps(dve, sum_steps, 2, b)
                        after(dve, "exped", b)
                        wi = winv[:, u].rearrange("p t h -> p (t h)")
                        st.link(v.tensor_reduce(wi, Wn[:, u].rearrange("p t h g -> p (t h) g"), X, ALU.add))
                        st.link(v.reciprocal(wi, wi))
                        v.tensor_tensor(winv[:, u], winv[:, u], bcast(w("pad_mask")[:, :, None], [P, TT, H]),
                                        ALU.mult).then_inc(at["winv"].sem, 1)

                    def slice_means(b, u):
                        st = Steps(dve, mean_steps, 2, b)
                        after(dve, "slices", b)
                        after(dve, "stT", b, 2)
                        sl = psum[:, SLICE_BANK, 0:HP * D1].rearrange("p (h d) -> p h d", h=HP)
                        st.link(v.tensor_scalar(slice_inv[:, u], sl[:, :, D], 1e-5, None, ALU.add))
                        st.link(v.reciprocal(slice_inv[:, u], slice_inv[:, u]))
                        v.tensor_tensor(ST[:, u], sl, bcast(slice_inv[:, u, :, None], [P, HP, D1]),
                                        ALU.mult).then_inc(at["slices_sb"].sem, 1)

                    def keep_vo(b, u):
                        after(dve, "mix_vo", b)
                        after(dve, "ow", b, 2)
                        v.tensor_copy(VO[:, u].rearrange("p h g -> p (h g)"), psum[0:G, VO_BANK, :]).then_inc(at["vo_sb"].sem, 1)

                    def attention(b, u):
                        st = Steps(dve, score_steps, 1, b)
                        after(dve, "scores", b)
                        after(dve, "aT", b, 2)
                        sc = psum[:, SCORE_BANK, 0:HP * G].rearrange("p (h g) -> p h g", h=HP)
                        st.link(v.tensor_reduce(row_stat[:, u], sc, X, ALU.max))
                        v.tensor_tensor(A[:, u], sc, bcast(row_stat[:, u, :, None], [P, HP, G]),
                                        ALU.subtract).then_inc(at["sc_shifted"].sem, 1)
                        st = Steps(dve, attn_steps, 2, b)
                        after(dve, "sc_exped", b)
                        st.link(v.tensor_reduce(row_stat[:, u], A[:, u], X, ALU.add))
                        st.link(v.reciprocal(row_stat[:, u], row_stat[:, u]))
                        v.tensor_tensor(A[:, u], A[:, u], bcast(row_stat[:, u, :, None], [P, HP, G]),
                                        ALU.mult).then_inc(at["attn"].sem, 1)

                    def keep_ow(b, u):
                        after(dve, "ow", b)
                        after(dve, "rows", b, 2)
                        v.tensor_copy(OW[:, u].rearrange("p h g -> p (h g)"), psum[:, SCORE_BANK, 0:HP * D]).then_inc(at["ow_sb"].sem, 1)

                    def added(b, u):
                        st = Steps(dve, row_steps, 1, b)
                        st.link(v.tensor_tensor(seq_rows(h_all, b), seq_rows(h_all, b),
                                                bcast(w("fout_b")[:, None, :], [P, TT, D]), ALU.add))
                        after(dve, "rows", b)
                        v.tensor_tensor(seq_rows(h_all, b), seq_rows(h_all, b),
                                        two_tiles(psum[:, ROW_BANK, 0:TT * D]), ALU.add).then_inc(at["h_added"].sem, 1)

                    def step(b, u, there):
                        if there(-1):
                            attention(b - 1, 1 - u)
                        if there(1):
                            less_top(b + 1, 1 - u)
                        if there(0):
                            slice_means(b, u)
                        if there(-1):
                            keep_ow(b - 1, 1 - u)
                        if there(1):
                            weight_sums(b + 1, 1 - u)
                        if there(2):
                            normalised(b + 2, u)
                        if there(-1):
                            added(b - 1, 1 - u)
                        if there(0):
                            keep_vo(b, u)
                    pipeline(dve, step, 2, 1)

        with ExitStack() as ctx:
            layer_stats("win_ln", h_all, cen, 1e-5)
            NW = ROWS // WS
            xn = sb(ctx, "win_xn", [P, 2, TT, D])
            xT = sb(ctx, "win_xT", [D, 2, ROWS])
            Qw, Kw = sb(ctx, "Qw", [D, 2, ROWS]), sb(ctx, "Kw", [D, 2, ROWS])
            Kd = sb(ctx, "Kd", [D, 2, NW, H, WS])
            Vd = sb(ctx, "Vd", [P, 2, NW, HP, 2 * DK])
            Aw = sb(ctx, "Aw", [P, 2, TT, H, WS])
            AwT = sb(ctx, "AwT", [P, 2, TT, HP, P])
            wtop, winv = sb(ctx, "win_top", [P, 2, TT, H]), sb(ctx, "win_inv", [P, 2, TT, H])
            On = sb(ctx, "On", [P, 2, TT, D])
            OnT = sb(ctx, "OnT", [D, 2, ROWS])
            XK_BANK, QV_BANK, SCORE_BANK, AT_BANK, HEAD_BANK, ROW_BANK = 0, 1, 2, 4, 6, 7
            names = ["xn", "xT", "xT_sb", "qkv", "q_sb", "k_sb", "v_sb", "kd", "scores", "biased", "top", "shifted", "exped",
                     "aT", "aT_sb", "inv", "heads", "heads_sb", "oT", "oT_sb", "rows", "h_added"]
            at = {n: Signal(f"win_{n}") for n in names}
            sum_steps, row_steps, ready = sem("win_sum_steps"), sem("win_row_steps"), sem("win_prepared")

            def after(engine, name, b, before=0):
                engine.wait_ge(at[name].sem, at[name].done(b, before=before))

            with nc.Block() as block:
                @block.sync
                def _(sp):
                    open_signals(sp, list(at.values()))

                @block.tensor
                def _(pe):
                    t_ = nc.tensor

                    def transpose_x(b, u):
                        after(pe, "xn", b)
                        after(pe, "k_sb", b, 1)
                        wait_apart(pe)
                        for t in range(TT):
                            last = t_.transpose(psum[0:D, XK_BANK, t * P:(t + 1) * P], xn[:, u, t, :], ident)
                        last.then_inc(at["xT"].sem, 1)

                    def qkv(b, u):
                        after(pe, "xT_sb", b)
                        after(pe, "q_sb", b, 1)
                        after(pe, "v_sb", b, 1)
                        wait_apart(pe)
                        t_.matmul(psum[0:D, XK_BANK, ROWS:2 * ROWS], w("a_k"), xT[:, u], start=True, stop=True)
                        t_.matmul(psum[0:D, QV_BANK, 0:ROWS], w("a_q"), xT[:, u], start=True, stop=True)
                        for half in range(2):
                            for n in range(NW):
                                last = t_.matmul(psum[half * D:(half + 1) * D, QV_BANK, ROWS + n * D:ROWS + (n + 1) * D],
                                                 xT[:, u, n * WS:(n + 1) * WS], w("a_v"), start=True, stop=True)
                        last.then_inc(at["qkv"].sem, 1)

                    def scores(b, u):
                        after(pe, "kd", b)
                        after(pe, "q_sb", b)
                        after(pe, "biased", b, 1)
                        wait_apart(pe)
                        for n in range(NW):
                            last = t_.matmul(psum[(n % 2) * WS:(n % 2 + 1) * WS, SCORE_BANK + n // 2, :],
                                             Qw[:, u, n * WS:(n + 1) * WS], Kd[:, u, n].rearrange("p h k -> p (h k)"),
                                             start=True, stop=True)
                        last.then_inc(at["scores"].sem, 1)

                    def transpose_attention(b, u):
                        after(pe, "exped", b)
                        after(pe, "aT_sb", b, 1)
                        for t in range(TT):
                            for hp in range(HP):
                                last = t_.transpose(psum[:, AT_BANK + t, hp * P:(hp + 1) * P],
                                                    Aw[:, u, t, 2 * hp:2 * hp + 2].rearrange("p h k -> p (h k)"), ident)
                        last.then_inc(at["aT"].sem, 1)

                    def heads(b, u):
                        after(pe, "aT_sb", b)
                        after(pe, "v_sb", b)
                        after(pe, "heads_sb", b, 1)
                        for n in range(NW):
                            for hp in range(HP):
                                last = t_.matmul(psum[(n % 2) * WS:(n % 2 + 1) * WS, HEAD_BANK,
                                                      (n // 2) * D + hp * 2 * DK:(n // 2) * D + (hp + 1) * 2 * DK],
                                                 AwT[:, u, n // 2, hp, (n % 2) * WS:(n % 2 + 1) * WS],
                                                 Vd[:, u, n, hp, :], start=True, stop=True)
                        last.then_inc(at["heads"].sem, 1)

                    def transpose_heads(b, u):
                        after(pe, "heads_sb", b)
                        after(pe, "h_added", b, 1)
                        wait_apart(pe)
                        for t in range(TT):
                            last = t_.transpose(psum[0:D, ROW_BANK, t * P:(t + 1) * P], On[:, u, t, :], ident)
                        last.then_inc(at["oT"].sem, 1)

                    def rows_out(b, u):
                        after(pe, "oT_sb", b)
                        for t in range(TT):
                            last = t_.matmul(psum[:, ROW_BANK, ROWS + t * D:ROWS + (t + 1) * D], OnT[:, u, t * P:(t + 1) * P],
                                             w("a_proj"), start=True, stop=True)
                        last.then_inc(at["rows"].sem, 1)

                    def step(b, u, there):
                        if there(1):
                            qkv(b + 1, 1 - u)
                        if there(-2):
                            rows_out(b - 2, u)
                        if there(-1):
                            transpose_attention(b - 1, 1 - u)
                        if there(0):
                            scores(b, u)
                        if there(-1):
                            heads(b - 1, 1 - u)
                        if there(2):
                            transpose_x(b + 2, u)
                        if there(-1):
                            transpose_heads(b - 1, 1 - u)
                    pipeline(pe, step, 3, 2)

                @block.scalar
                def _(act):
                    a = nc.scalar

                    def step(b, u, there):
                        if there(1):
                            after(act, "qkv", b + 1)
                            after(act, "kd", b + 1, 2)
                            a.activation(Kw[:, 1 - u], psum[0:D, XK_BANK, ROWS:2 * ROWS], ACT.Copy).then_inc(at["k_sb"].sem, 1)
                        if there(-1):
                            after(act, "aT", b - 1)
                            after(act, "heads", b - 1, 2)
                            a.activation(AwT[:, 1 - u].rearrange("p t h n -> p t (h n)"),
                                         psum[:, AT_BANK:AT_BANK + 2, :], ACT.Copy).then_inc(at["aT_sb"].sem, 1)
                        if there(2):
                            after(act, "xT", b + 2)
                            after(act, "qkv", b + 2, 2)
                            a.activation(xT[:, u], psum[0:D, XK_BANK, 0:ROWS], ACT.Copy).then_inc(at["xT_sb"].sem, 1)
                        if there(-1):
                            after(act, "oT", b - 1)
                            after(act, "rows", b - 1, 2)
                            a.activation(OnT[:, 1 - u], psum[0:D, ROW_BANK, 0:ROWS], ACT.Copy).then_inc(at["oT_sb"].sem, 1)
                        if there(0):
                            after(act, "shifted", b)
                            a.activation(Aw[:, u], Aw[:, u], ACT.Exp).then_inc(at["exped"].sem, 1)
                    pipeline(act, step, 3, 2)

                @block.gpsimd
                def _(pool):
                    g = nc.gpsimd

                    def step(b, u, there):
                        if there(1):
                            after(pool, "k_sb", b + 1)
                            after(pool, "scores", b + 1, 2)
                            ks = Kw[:, 1 - u].rearrange("p (n k) -> p n k", n=NW)
                            g.tensor_tensor(Kd[:, 1 - u], bcast(ks[:, :, None, :], [D, NW, H, WS]),
                                            bcast(w("head_mask")[:, None, :, None], [D, NW, H, WS]), ALU.mult).then_inc(at["kd"].sem, 1)
                        if there(0):
                            after(pool, "top", b)
                            aw = Aw[:, u].rearrange("p t h k -> p (t h) k")
                            g.tensor_tensor(aw, aw, bcast(wtop[:, u].rearrange("p t h -> p (t h)")[:, :, None], [P, TT * H, WS]),
                                            ALU.subtract).then_inc(at["shifted"].sem, 1)
                    pipeline(pool, step, 3, 2)

                @block.vector
                def _(dve):
                    v = nc.vector
                    v.memset(Vd[:], 0.0).then_inc(ready, 1)
                    dve.wait_ge(ready, 1)

                    def normalised(b, u):
                        after(dve, "xT", b, 2)
                        normed(xn, u, b, cen).then_inc(at["xn"].sem, 1)

                    def keep_q(b, u):
                        after(dve, "qkv", b)
                        after(dve, "scores", b, 2)
                        v.tensor_scalar(Qw[:, u], psum[0:D, QV_BANK, 0:ROWS], DK ** -0.5, None, ALU.mult).then_inc(at["q_sb"].sem, 1)

                    def keep_v(b, u):
                        after(dve, "heads", b, 2)
                        for half in range(2):
                            rows_of = slice(half * D, (half + 1) * D)
                            vals = psum[rows_of, QV_BANK, ROWS:ROWS + NW * D].rearrange("p (n h s d) -> p n h (s d)", n=NW, h=HP, s=2)
                            last = v.tensor_copy(Vd[rows_of, u, :, :, half * DK:(half + 1) * DK],
                                                 vals[:, :, :, half * DK:(half + 1) * DK])
                        last.then_inc(at["v_sb"].sem, 1)

                    def biased(b, u):
                        after(dve, "scores", b)
                        after(dve, "aT", b, 2)
                        after(dve, "inv", b, 2)
                        aw = Aw[:, u].rearrange("p t h k -> p (t h) k")
                        v.tensor_tensor(
                            aw, psum[:, SCORE_BANK:SCORE_BANK + 2, :].rearrange("p t (h k) -> p (t h) k", k=WS),
                            bcast(w("rel")[:, None, :], [P, TT * H, WS]), ALU.add).then_inc(at["biased"].sem, 1)
                        after(dve, "biased", b)
                        v.tensor_reduce(wtop[:, u].rearrange("p t h -> p (t h)"), aw, X, ALU.max).then_inc(at["top"].sem, 1)

                    def sums(b, u):
                        after(dve, "exped", b)
                        wi = winv[:, u].rearrange("p t h -> p (t h)")
                        st = Steps(dve, sum_steps, 1, b)
                        st.link(v.tensor_reduce(wi, Aw[:, u].rearrange("p t h k -> p (t h) k"), X, ALU.add))
                        v.reciprocal(wi, wi).then_inc(at["inv"].sem, 1)

                    def scaled_heads(b, u):
                        after(dve, "heads", b)
                        after(dve, "inv", b)
                        after(dve, "oT", b, 2)
                        wi = winv[:, u].rearrange("p t h -> p (t h)")
                        v.tensor_tensor(On[:, u].rearrange("p t (h d) -> p (t h) d", d=DK),
                                        psum[:, HEAD_BANK, 0:TT * D].rearrange("p (n d) -> p n d", d=DK),
                                        bcast(wi[:, :, None], [P, TT * H, DK]), ALU.mult).then_inc(at["heads_sb"].sem, 1)

                    def added(b, u):
                        st = Steps(dve, row_steps, 1, b)
                        st.link(v.tensor_tensor(seq_rows(h_all, b), seq_rows(h_all, b),
                                                bcast(w("a_proj_b")[:, None, :], [P, TT, D]), ALU.add))
                        after(dve, "rows", b)
                        v.tensor_tensor(seq_rows(h_all, b), seq_rows(h_all, b),
                                        two_tiles(psum[:, ROW_BANK, ROWS:ROWS + TT * D]), ALU.add).then_inc(at["h_added"].sem, 1)

                    def step(b, u, there):
                        if there(1):
                            keep_q(b + 1, 1 - u)
                        if there(-1):
                            sums(b - 1, 1 - u)
                        if there(0):
                            biased(b, u)
                        if there(-1):
                            scaled_heads(b - 1, 1 - u)
                        if there(1):
                            keep_v(b + 1, 1 - u)
                        if there(3):
                            normalised(b + 3, 1 - u)
                        if there(-2):
                            added(b - 2, u)
                    pipeline(dve, step, 3, 2)
        with ExitStack() as ctx:
            layer_stats("moe_ln", h_all, cen, 1e-5)
            EP = E // 2
            XT = sb(ctx, "moe_XT", [D, B * ROWS])
            Pr = sb(ctx, "Pr", [P, B * TT, E])
            with ExitStack() as inner:
                stage = sb(inner, "moe_stage", [P, 2, TT, D])
                xT = sb(inner, "route_xT", [D, 2, ROWS])
                names = ["xn", "xT", "xT_sb", "kept", "logits", "logits_sb"]
                at = {n: Signal(f"route_{n}") for n in names}
                with nc.Block() as block:
                    @block.sync
                    def _(sp):
                        open_signals(sp, list(at.values()))

                    @block.tensor
                    def _(pe):
                        with pe.Fori(0, B // 2) as i:
                            for u in range(2):
                                b = 2 * i + u
                                pe.wait_ge(at["xn"].sem, at["xn"].done(b))
                                pe.wait_ge(at["xT_sb"].sem, at["xT_sb"].done(b, before=2))
                                transposed_rows(u, stage, u).then_inc(at["xT"].sem, 1)
                            for u in range(2):
                                b = 2 * i + u
                                pe.wait_ge(at["xT_sb"].sem, at["xT_sb"].done(b))
                                pe.wait_ge(at["logits_sb"].sem, at["logits_sb"].done(b, before=2))
                                for t in range(TT):
                                    last = nc.tensor.matmul(psum[:, 2 + u, t * E:(t + 1) * E], xT[:, u, t * P:(t + 1) * P],
                                                            w("router"), start=True, stop=True)
                                last.then_inc(at["logits"].sem, 1)

                    @block.scalar
                    def _(act):
                        with act.Fori(0, B // 2) as i:
                            for u in range(2):
                                b = 2 * i + u
                                act.wait_ge(at["xT"].sem, at["xT"].done(b))
                                act.wait_ge(at["logits"].sem, at["logits"].done(b, before=2))
                                act.wait_ge(at["kept"].sem, at["kept"].done(b, before=2))
                                nc.scalar.activation(xT[:, u], psum[0:D, u, 0:ROWS], ACT.Copy).then_inc(at["xT_sb"].sem, 1)

                    @block.gpsimd
                    def _(pool):
                        with pool.Fori(0, B // 2) as i:
                            for u in range(2):
                                b = 2 * i + u
                                pool.wait_ge(at["xT_sb"].sem, at["xT_sb"].done(b))
                                nc.gpsimd.tensor_copy(XT[:, bass.ds(b * ROWS, ROWS)], xT[:, u]).then_inc(at["kept"].sem, 1)

                    @block.vector
                    def _(dve):
                        v = nc.vector
                        with dve.Fori(0, B // 2) as i:
                            for u in range(2):
                                b = 2 * i + u
                                dve.wait_ge(at["xT"].sem, at["xT"].done(b, before=2))
                                normed(stage, u, b, cen).then_inc(at["xn"].sem, 1)
                                dve.wait_ge(at["xn"].sem, at["xn"].done(b))
                                v.tensor_tensor(seq_rows(h_all, b), seq_rows(h_all, b), stage[:, u], ALU.add)
                            for u in range(2):
                                b = 2 * i + u
                                dve.wait_ge(at["logits"].sem, at["logits"].done(b))
                                v.tensor_copy(
                                    seq_rows(Pr, b), psum[:, 2 + u, 0:TT * E].rearrange("p (t e) -> p t e", t=TT)).then_inc(at["logits_sb"].sem, 1)

            Cm = sb(ctx, "Cm", [P, B * TT, E])
            with ExitStack() as inner:
                RB = B * TT
                Left = sb(inner, "Left", [P, RB, E])
                eq, count = sb(inner, "eq", [P, RB, E]), sb(inner, "count", [P, RB, E])
                starts = sb(inner, "starts", [P, RB, E])
                best1, best2 = sb(inner, "best1", [P, RB]), sb(inner, "best2", [P, RB])
                steps, shifted, exped = sem("top_steps"), sem("top_shifted"), sem("top_exped")
                with nc.Block() as block:
                    @block.scalar
                    def _(act):
                        act.wait_ge(shifted, 1)
                        nc.scalar.activation(Pr[:], Pr[:], ACT.Exp).then_inc(exped, 1)

                    @block.vector
                    def _(dve):
                        v = nc.vector
                        st = Steps(dve, steps)
                        wide = [P, RB, E]
                        flat = lambda t: t[:].rearrange("p r e -> p (r e)")
                        over = lambda t: bcast(t[:][:, :, None], wide)
                        st.step(v.memset(starts[:], 1.0))
                        st.link(v.tensor_reduce(best1[:], Pr[:], X, ALU.max))
                        st.step(v.memset(starts[:, :, 0:1], 0.0))
                        v.tensor_tensor(Pr[:], Pr[:], over(best1), ALU.subtract).then_inc(shifted, 1)
                        dve.wait_ge(exped, 1)
                        st.link(v.tensor_reduce(best1[:], Pr[:], X, ALU.add))
                        st.link(v.reciprocal(best1[:], best1[:]))
                        st.link(v.tensor_tensor(Pr[:], Pr[:], over(best1), ALU.mult))

                        def first_of_best(best, source):
                            st.link(v.tensor_reduce(best[:], source[:], X, ALU.max))
                            st.link(v.tensor_tensor(eq[:], source[:], over(best), ALU.is_equal))
                            st.link(v.tensor_tensor_scan(flat(count), flat(starts), flat(eq), 0.0, ALU.mult, ALU.add))
                            st.link(v.scalar_tensor_tensor(flat(count), flat(count), 1.0, flat(eq), ALU.is_equal, ALU.mult))

                        first_of_best(best1, Pr)
                        st.step(v.tensor_tensor(Cm[:], Pr[:], count[:], ALU.mult))
                        st.link(v.scalar_tensor_tensor(flat(Left), flat(count), -2.0, flat(Pr), ALU.mult, ALU.add))
                        first_of_best(best2, Left)
                        st.link(v.tensor_tensor(count[:], Pr[:], count[:], ALU.mult))
                        st.step(v.tensor_tensor(Cm[:], Cm[:], count[:], ALU.add))
                        st.link(v.tensor_tensor(best1[:], best1[:], best2[:], ALU.add))
                        st.link(v.tensor_scalar(best1[:], best1[:], 1e-12, None, ALU.max))
                        st.link(v.reciprocal(best1[:], best1[:]))
                        st.link(v.tensor_tensor(Cm[:], Cm[:], over(best1), ALU.mult))

            xT = sb(ctx, "moe_xT", [D, 2, ROWS])
            Cs = sb(ctx, "Cs", [P, 2, TT, E])
            cT = sb(ctx, "cT", [E, 2, ROWS])
            Hd = sb(ctx, "Hd", [P, 2, EP, ROWS])
            names = ["x_sb", "c_sb", "cT", "cT_sb", "hidden", "gelu", "spread", "weighted", "rows", "h_added"]
            at = {n: Signal(f"moe_{n}") for n in names}
            with nc.Block() as block:
                @block.sync
                def _(sp):
                    open_signals(sp, list(at.values()))

                @block.gpsimd
                def _(pool):
                    with pool.Fori(0, B // 2) as i:
                        for u in range(2):
                            b = 2 * i + u
                            pool.wait_ge(at["hidden"].sem, at["hidden"].done(b, before=2))
                            nc.gpsimd.tensor_copy(xT[:, u], XT[:, bass.ds(b * ROWS, ROWS)]).then_inc(at["x_sb"].sem, 1)
                            pool.wait_ge(at["cT"].sem, at["cT"].done(b, before=2))
                            nc.gpsimd.tensor_copy(Cs[:, u], seq_rows(Cm, b)).then_inc(at["c_sb"].sem, 1)

                @block.tensor
                def _(pe):
                    t_ = nc.tensor
                    with pe.Fori(0, B // 2) as i:
                        bu = [(2 * i + u, u, 4 * u) for u in range(2)]
                        for b, u, bank in bu:
                            pe.wait_ge(at["h_added"].sem, at["h_added"].done(b, before=2))
                            pe.wait_ge(at["weighted"].sem, at["weighted"].done(b, before=2))
                            pe.wait_ge(at["c_sb"].sem, at["c_sb"].done(b))
                            for t in range(TT):
                                last = t_.transpose(psum[0:E, bank + 2, t * P:(t + 1) * P], Cs[:, u, t, :], ident)
                            last.then_inc(at["cT"].sem, 1)
                            pe.wait_ge(at["x_sb"].sem, at["x_sb"].done(b))
                            for c in range(EP):
                                last = t_.matmul(psum[:, bank + c // 2, (c % 2) * ROWS:(c % 2 + 1) * ROWS],
                                                 w("w1")[:, c * P:(c + 1) * P], xT[:, u], start=True, stop=True)
                            last.then_inc(at["hidden"].sem, 1)
                        for b, u, bank in bu:
                            pe.wait_ge(at["cT_sb"].sem, at["cT_sb"].done(b))
                            for c in range(EP):
                                last = t_.matmul(psum[:, bank + 2 + c // 2, (c % 2) * ROWS:(c % 2 + 1) * ROWS],
                                                 w("expand")[:, c * P:(c + 1) * P], cT[:, u], start=True, stop=True)
                            last.then_inc(at["spread"].sem, 1)
                        for b, u, bank in bu:
                            pe.wait_ge(at["weighted"].sem, at["weighted"].done(b))
                            for t in range(TT):
                                for c in range(EP):
                                    t_.matmul(psum[:, bank, t * D:(t + 1) * D], Hd[:, u, c, t * P:(t + 1) * P],
                                              w("w2")[:, c * D:(c + 1) * D], start=(c == 0), stop=False)
                                last = t_.matmul(psum[:, bank, t * D:(t + 1) * D], cT[:, u, t * P:(t + 1) * P], w("b2"),
                                                 start=False, stop=True)
                            last.then_inc(at["rows"].sem, 1)

                @block.scalar
                def _(act):
                    a = nc.scalar
                    with act.Fori(0, B // 2) as i:
                        bu = [(2 * i + u, u, 4 * u) for u in range(2)]
                        for b, u, bank in bu:
                            act.wait_ge(at["cT"].sem, at["cT"].done(b))
                            act.wait_ge(at["rows"].sem, at["rows"].done(b, before=2))
                            a.activation(cT[:, u], psum[0:E, bank + 2, 0:ROWS], ACT.Copy).then_inc(at["cT_sb"].sem, 1)
                            act.wait_ge(at["hidden"].sem, at["hidden"].done(b))
                            for c in range(EP):
                                last = a.activation(Hd[:, u, c], psum[:, bank + c // 2, (c % 2) * ROWS:(c % 2 + 1) * ROWS],
                                                    ACT.Gelu, bias=w("b1")[:, c:c + 1])
                            last.then_inc(at["gelu"].sem, 1)

                @block.vector
                def _(dve):
                    v = nc.vector
                    with dve.Fori(0, B // 2) as i:
                        bu = [(2 * i + u, u, 4 * u) for u in range(2)]
                        for b, u, bank in bu:
                            dve.wait_ge(at["gelu"].sem, at["gelu"].done(b))
                            dve.wait_ge(at["spread"].sem, at["spread"].done(b))
                            hd = Hd[:, u].rearrange("p c n -> p (c n)")
                            v.tensor_tensor(
                                hd, hd, psum[:, bank + 2:bank + 4, :].rearrange("p k n -> p (k n)"), ALU.mult).then_inc(at["weighted"].sem, 1)
                        for b, u, bank in bu:
                            dve.wait_ge(at["rows"].sem, at["rows"].done(b))
                            v.tensor_tensor(seq_rows(h_all, b), seq_rows(h_all, b),
                                                                   two_tiles(psum[:, bank, 0:TT * D]), ALU.add).then_inc(at["h_added"].sem, 1)

        stored = sem("stored")
        with nc.Block() as block:
            @block.sync
            def _(sp):
                sp.dma_start(out, h_all[:]).then_inc(stored, 16)
                sp.wait_ge(stored, 16)


def kernel(**inputs):
    import numpy as np
    import concourse.bacc as _bacc
    from concourse.bass_utils import run_bass_kernel_spmd as _run

    a = {k: np.asarray(v) for k, v in inputs.items()}
    rows = lambda v: np.broadcast_to(np.reshape(v, (1, -1)), (P, np.size(v)))
    x = a["x"].reshape(B, NCHUNK, CHUNK).transpose(2, 0, 1)
    x_chunks = np.zeros((P, B, NCHUNK + 1), np.float32)
    x_chunks[:, :, :NCHUNK] = x

    tok_w = a["L0_tok_W"].T
    rel = a["L1_attn_rel_bias"]
    q_at, k_at = np.meshgrid(np.arange(WS), np.arange(WS), indexing="ij")
    rel_tile = rel[k_at - q_at + WS - 1]
    pad_mask = np.ones((P, TT), np.float32)
    pad_mask[P - 1, TT - 1] = 0
    head_mask = (np.arange(D)[:, None] // DK == np.arange(H)[None, :]).astype(np.float32)
    query = (np.arange(P) % QB)[:, None]
    last_key = np.where(np.arange(QB)[None, :] > query, NEG, 0).astype(np.float32)
    expand = np.zeros((E, E // 2, P), np.float32)
    for e in range(E):
        expand[e, e // 2, (e % 2) * D:(e % 2 + 1) * D] = 1
    qkv = a["L1_attn_w_qkv"]
    pack = {
        "tok_w0": tok_w[:P], "tok_w1": tok_w[P:], "tok_b": rows(a["L0_tok_b"]),
        "tok_gamma": rows(a["L0_tok_gamma"]), "tok_beta": rows(a["L0_tok_beta"]),
        "ident": np.eye(P, dtype=np.float32), "pad_mask": pad_mask, "head_mask": head_mask,
        "conv": a["L0_attn_conv_w"].transpose(1, 2, 0).reshape(D, TAPS * D),
        "conv_b": rows(a["L0_attn_conv_b"]), "sqrt_beta": rows(a["L0_attn_sqrt_beta"]),
        "ln_w": a["L0_attn_ln_w"][:, None], "ln_b": a["L0_attn_ln_b"][:, None],
        "ln_b_wide": np.broadcast_to(a["L0_attn_ln_b"][:, None], (D, P)),
        "q_w": a["L0_attn_q_w"].T, "k_w": a["L0_attn_k_w"].T, "v_w": a["L0_attn_v_w"].T,
        "q_b": a["L0_attn_q_b"][:, None], "k_b": np.tile(a["L0_attn_k_b"], 2)[:, None], "v_b": rows(a["L0_attn_v_b"]),
        "out_w": a["L0_attn_out_w"].T, "out_b": rows(a["L0_attn_out_b"]),
        "gammas": np.repeat(a["L0_attn_gammas"].reshape(H), QB)[:, None],
        "fx_wT": np.concatenate([a["L0_ffn_W_fx"], a["L0_ffn_b_fx"][None]]).reshape(D + 1, H, D)
        .transpose(2, 1, 0).reshape(D, H * (D + 1)),
        "x_w": a["L0_ffn_W_x"].reshape(D, H, D).transpose(2, 1, 0).reshape(D, H * D),
        "x_b": a["L0_ffn_b_x"].reshape(H, D).T, "slice_w": a["L0_ffn_W_slice"],
        "slice_b": np.broadcast_to(a["L0_ffn_b_slice"][None], (D + 1, G)), "temp": rows(a["L0_ffn_temperature"]),
        "fq_w": a["L0_ffn_W_q"].T, "fk_w": a["L0_ffn_W_k"].T, "fv_w": a["L0_ffn_W_v"].T,
        "fout_w": a["L0_ffn_W_out"].reshape(H, D, D).transpose(1, 0, 2).reshape(D, H * D),
        "fout_b": rows(a["L0_ffn_b_out"]),
        "a_q": qkv[0:D].T, "a_k": qkv[D:2 * D].T, "a_v": qkv[2 * D:].T, "a_proj": a["L1_attn_w_proj"].T,
        "a_proj_b": rows(a["L1_attn_b_proj"]), "rel": np.concatenate([rel_tile, rel_tile]),
        "router": a["L1_ffn_router_w"].T,
        "w1": a["L1_ffn_w1"].transpose(1, 0, 2).reshape(D, E * D),
        "b1": a["L1_ffn_b1"].reshape(E // 2, P).T,
        "w2": a["L1_ffn_w2"].reshape(E // 2, P, D).transpose(1, 0, 2).reshape(P, (E // 2) * D),
        "b2": a["L1_ffn_b2"], "expand": expand.reshape(E, -1), "last_key": last_key,
    }
    cols, total = weight_columns()
    weights = np.zeros((P, total), np.float32)
    for name, (at, r, n) in cols.items():
        weights[:r, at:at + n] = pack[name]
    tables = np.zeros((P, 2, PACKED), np.float32)
    tables[:, 1] = 1
    for j in range(NQ):
        key = np.arange(SPAN[j])[None, :]
        tables[:, 0, OFF[j]:OFF[j] + SPAN[j]] = np.maximum(QB * j + query - key, 0)
        tables[:, 1, OFF[j] + SPAN[j] - 1] = 0

    nc = _bacc.Bacc("TRN2", target_bir_lowering=False, num_devices=1)
    arrays = {"x_chunks": x_chunks, "weights": weights, "tables": tables}
    args = [nc.dram_tensor(k, v.shape, F32, kind="ExternalInput").ap() for k, v in arrays.items()]
    out = nc.dram_tensor("out", (P, B * TT, D), F32, kind="ExternalOutput").ap()
    build(nc, *args, out)
    got = _run(nc, [arrays], core_ids=[0]).results[0]["out"]
    return got.reshape(P, B, TT, D).transpose(1, 2, 0, 3).reshape(B, ROWS, D)[:, :TOK]
```

```python
from contextlib import ExitStack

import concourse.bass as bass
from concourse import mybir

P = 128
B = 16
SEQ, FEAT = 2048, 16
PATCH, STRIDE = 16, 8
CHUNK = STRIDE * FEAT
NCHUNK = SEQ // STRIDE
TOK = NCHUNK - 1
D = 64
H = 8
DK = D // H
TT = 2
ROWS = TT * P
G = 64
INNER = H * D
E = 8
PARTS_OF_C = 3
WS = 64
TAPS = 5
TAP_PAIRS = (TAPS + 1) // 2
STEPS_TO_ABS = 15
NEG = -1e30

F32 = mybir.dt.float32
BF16 = mybir.dt.bfloat16
ALU = mybir.AluOpType
ACT = mybir.ActivationFunctionType
X = mybir.AxisListType.X

QB = P // H
NQ = ROWS // QB
SPAN = [QB * (j + 1) for j in range(NQ)]
BANKS = [[15, 14, 0], [13, 12, 4], [11, 10, 8], [9, 7, 6, 5], [3, 2, 1]]
IN_BANK = {j: sum(SPAN[k] for k in bank[:bank.index(j)]) for bank in BANKS for j in bank}
ORDER = [j for bank in BANKS for j in bank]
PAIR = SPAN[0] + SPAN[NQ - 1]
PACKED = PAIR * (NQ // 2)
OFF = {}
for _n in range(NQ // 2):
    OFF[NQ - 1 - _n] = PAIR * _n
    OFF[_n] = PAIR * _n + SPAN[NQ - 1 - _n]
SB_ORDER = sorted(OFF, key=OFF.get)
HALF = NQ // 2
WIDE_OFF = [P * j if j < HALF else P * HALF + 2 * P * (j - HALF) for j in range(NQ)]
WIDE = P * HALF + 2 * P * HALF


def weight_columns():
    sizes = [
        ("tok_w0", P, D), ("tok_w1", P, D), ("tok_b", P, D), ("tok_gamma", P, D), ("tok_beta", P, D),
        ("ident", P, P), ("pad_mask", P, TT), ("head_mask", P, H),
        ("conv", P, TAP_PAIRS * D), ("conv_b", P, D), ("sqrt_beta", P, D),
        ("ln_w", D, 1), ("ln_b", D, 1), ("ln_b_wide", D, P), ("q_w", D, D), ("k_w", D, D), ("v_w", D, D),
        ("q_b", D, 1), ("k_b", P, 1), ("v_b", P, D), ("out_w", D, D), ("out_b", P, D), ("gammas", P, 1),
        ("last_key", P, QB),
        ("fx_wT", D, H * (D + 1)), ("x_w", D, H * D), ("x_b", D, H), ("slice_w", D, G), ("slice_b", D + 1, G),
        ("temp", P, H), ("fq_w", D, D), ("fk_w", D, D), ("fv_w", D, D), ("fout_w", D, H * D), ("fout_b", P, D),
        ("a_qk", D, 2 * D), ("a_v", D, D), ("a_proj", D, D), ("a_proj_b", P, D), ("rel", P, WS),
        ("router", D, E), ("w1", D, E * D), ("b1", P, E // 2), ("w2", P, (E // 2) * D), ("b2", PARTS_OF_C * E, D),
        ("expand", PARTS_OF_C * E, (E // 2) * P),
    ]
    cols, at = {}, 0
    for name, rows, width in sizes:
        cols[name] = (at, rows, width)
        at += width
    return cols, at


class Steps:

    def __init__(self, engine, semaphore, per_turn=0, turn=0):
        self.engine, self.semaphore, self.per_turn, self.turn, self.n = engine, semaphore, per_turn, turn, 0

    def step(self, instruction):
        self.n += 1
        instruction.then_inc(self.semaphore, 1)
        return self.n

    def wait(self, n=None):
        n = self.n if n is None else n
        self.engine.wait_ge(self.semaphore, self.turn * self.per_turn + n if self.per_turn else n)

    def link(self, instruction):
        self.step(instruction)
        self.wait()

    def end(self):
        assert not self.per_turn or self.n == self.per_turn, self.n


def bcast(ap, shape):
    return ap.to_broadcast(shape)


def build(nc, x_chunks, weights, packed_tables, out):
    cols, _ = weight_columns()
    top = ExitStack()
    with top:
        def sem(name):
            return top.enter_context(nc.semaphore(name))

        def sb(ctx, name, shape, dtype=F32):
            return ctx.enter_context(nc.sbuf_tensor(name, shape, dtype))

        W = sb(top, "W", [P, sum(c[2] for c in cols.values())])
        LATE = cols["fx_wT"][0]

        def w(name, rows=None):
            at, r, n = cols[name]
            return W[0:(rows or r), at:at + n]

        h_all = sb(top, "h_all", [P, B * TT, D])
        rstd = sb(top, "rstd", [P, B * TT])
        moments = sb(top, "moments", [P, B * TT, 2])
        psum = top.enter_context(nc.psum_tensor("psum", [P, 8, 512], F32))
        ident = w("ident")

        loaded, loaded_late = sem("weights_loaded"), sem("late_weights_loaded")

        waited_apart = {}

        def wait_apart(engine):
            name = f"waited_apart_{engine.engine.name}"
            if name not in waited_apart:
                waited_apart[name] = sem(name)
            engine.sem_inc(waited_apart[name], 1)

        ln_steps, has_var, has_std, normed_steps = sem("ln_steps"), sem("ln_has_var"), sem("ln_has_std"), sem("normed_steps")
        layernorms = []

        def row_moments(dve, turn, b, u, parts, small, added):
            st = Steps(dve, moment_steps, 2, turn * B + b)
            dve.wait_ge(added.sem, added.done(b))
            wait_apart(dve)
            for t in range(TT):
                last = nc.vector.bn_stats(parts[:, u, t, :], h_all[:, bass.ds(b * TT + t, 1), :].rearrange("p t d -> p (t d)"))
            st.link(last)
            wait_apart(dve)
            for t in range(TT):
                last = nc.vector.bn_aggr(small[:, u, t, :], parts[:, u, t, :])
            st.link(last)
            nc.vector.tensor_copy(moments[:, bass.ds(b * TT, TT), :], small[:, u]).then_inc(kept_moments, 1)

        moment_steps, kept_moments = sem("moment_steps"), sem("kept_moments")
        measured_before = []

        def layer_stats(tag, eps, on_the_way=False):
            turn = len(layernorms)
            layernorms.append(on_the_way)
            with ExitStack() as ctx:
                parts = sb(ctx, f"{tag}_parts", [P, B * TT, 6])
                var, std = sb(ctx, f"{tag}_var", [P, B * TT]), sb(ctx, f"{tag}_std", [P, B * TT])
                nch, per = 4, B * TT // 4
                steps_before = sum(2 if m else 2 * nch + 2 for m in layernorms[:-1])
                if on_the_way:
                    measured_before.append(tag)
                with nc.Block() as block:
                    @block.vector
                    def _(dve):
                        v = nc.vector
                        st = Steps(dve, ln_steps)
                        st.n = steps_before
                        if on_the_way:
                            dve.wait_ge(kept_moments, B * len(measured_before))
                        else:
                            chunks = [range(c * per, (c + 1) * per) for c in range(nch)]
                            for row in chunks[0]:
                                last = v.bn_stats(parts[:, row, :], h_all[:, row, :])
                            measured = st.step(last)
                            for c in range(nch):
                                for_this = measured
                                if c + 1 < nch:
                                    for row in chunks[c + 1]:
                                        last = v.bn_stats(parts[:, row, :], h_all[:, row, :])
                                    measured = st.step(last)
                                st.wait(for_this)
                                for row in chunks[c]:
                                    last = v.bn_aggr(moments[:, row, :], parts[:, row, :])
                                st.step(last)
                            st.wait()
                        v.tensor_scalar(var[:], moments[:, :, 1], eps, None, ALU.add).then_inc(has_var, 1)
                        dve.wait_ge(has_std, turn + 1)
                        st.link(v.reciprocal(rstd[:], std[:]))
                        st.link(v.tensor_tensor(
                            rstd[:].rearrange("p (b t) -> p b t", t=TT), rstd[:].rearrange("p (b t) -> p b t", t=TT),
                            bcast(w("pad_mask")[:, None, :], [P, B, TT]), ALU.mult))

                    @block.scalar
                    def _(act):
                        act.wait_ge(has_var, turn + 1)
                        nc.scalar.activation(std[:], var[:], ACT.Sqrt).then_inc(has_std, 1)

        conv_x = sb(top, "conv_x", [P, TAP_PAIRS, D])
        conv_bias = sb(top, "conv_bias", [P, D])
        qkv_x = sb(top, "qkv_x", [D, 3, D])
        q_bias, k_bias = sb(top, "q_bias", [D, 1]), sb(top, "k_bias", [P, 1])
        v_bias = sb(top, "v_bias", [P, D])
        gamma_sq = sb(top, "gamma_sq", [P, 1])
        soft = sb(top, "soft", [P, 4])
        keep_low, keep_high = sb(top, "keep_low", [P, D]), sb(top, "keep_high", [P, D])
        diag_high = sb(top, "diag_high", [D, D])
        w_vector, w_scalar, w_tensor = sem("w_vector"), sem("w_scalar"), sem("w_tensor")
        with nc.Block() as block:
            @block.sync
            def _(sp):
                sp.dma_start(W[:, :LATE], weights[:, :LATE]).then_inc(loaded, 16)

            @block.vector
            def _(dve):
                dve.wait_ge(loaded, 16)
                st = Steps(dve, w_vector)
                v = nc.vector
                st.link(v.tensor_tensor(keep_high[:], w("sqrt_beta"), w("sqrt_beta"), ALU.mult))
                st.link(v.tensor_scalar(keep_low[:], keep_high[:], -1.0, 1.0, ALU.mult, ALU.add))
                st.link(v.tensor_scalar(keep_high[:], keep_high[:], 1.0, None, ALU.add))
                st.step(v.tensor_tensor(conv_bias[:], w("conv_b"), keep_low[:], ALU.mult))
                st.step(v.tensor_tensor(diag_high[:], ident[0:D, 0:D], keep_high[0:D, :], ALU.mult))
                st.step(v.tensor_tensor(conv_x[:], w("conv").rearrange("p (k d) -> p k d", k=TAP_PAIRS),
                                        bcast(keep_low[:, None, :], [P, TAP_PAIRS, D]), ALU.mult))
                st.wait()
                st.step(v.tensor_tensor(conv_x[0:D, TAP_PAIRS - 1, :], conv_x[0:D, TAP_PAIRS - 1, :], diag_high[:], ALU.add))
                for n, name in enumerate(("q_w", "k_w", "v_w")):
                    st.step(v.tensor_scalar(qkv_x[:, n, :], w(name), w("ln_w"), None, ALU.mult))
                dve.wait_ge(w_tensor, 3)
                st.step(v.tensor_tensor(q_bias[:], psum[0:D, 0, 0:1], w("q_b"), ALU.add))
                st.step(v.tensor_tensor(k_bias[D:P], psum[D:P, 1, 0:1], w("k_b")[D:P], ALU.add))
                st.step(v.tensor_tensor(v_bias[:], psum[:, 2, 0:D], w("v_b"), ALU.add))
                st.link(v.tensor_scalar(soft[:, 0:1], w("gammas"), -1.0, None, ALU.mult))
                at_abs = st.step(v.tensor_tensor(soft[:, 1:2], soft[:, 0:1], w("gammas"), ALU.min))
                assert at_abs == STEPS_TO_ABS
                st.step(v.tensor_scalar(soft[:, 2:3], w("gammas"), 0.0, None, ALU.max))
                dve.wait_ge(w_scalar, 2)
                st.wait()
                st.link(v.tensor_tensor(soft[:, 2:3], soft[:, 2:3], soft[:, 1:2], ALU.add))
                st.link(v.tensor_tensor(gamma_sq[:], soft[:, 2:3], soft[:, 2:3], ALU.mult))

            @block.scalar
            def _(act):
                act.wait_ge(w_vector, STEPS_TO_ABS)
                nc.scalar.activation(soft[:, 3:4], soft[:, 1:2], ACT.Exp).then_inc(w_scalar, 1)
                act.wait_ge(w_scalar, 1)
                nc.scalar.activation(soft[:, 1:2], soft[:, 3:4], ACT.Ln, bias=1.0).then_inc(w_scalar, 1)

            @block.tensor
            def _(pe):
                pe.wait_ge(loaded, 16)
                nc.tensor.matmul(psum[0:D, 0, 0:1], w("q_w"), w("ln_b"), start=True, stop=True).then_inc(w_tensor, 1)
                nc.tensor.matmul(psum[D:P, 1, 0:1], w("k_w"), w("ln_b"), start=True, stop=True).then_inc(w_tensor, 1)
                nc.tensor.matmul(psum[:, 2, 0:D], w("ln_b_wide"), w("v_w"), start=True, stop=True).then_inc(w_tensor, 1)

        def seq_rows(ap, b):
            return ap[:, bass.ds(b * TT, TT), :]

        def two_tiles(ap):
            return ap.rearrange("p (t d) -> p t d", t=TT)

        class Signal:

            def __init__(self, name, each=1):
                self.each, self.sem = each, sem(name)

            def done(self, b, n=None, before=0):
                return (b + 2 - before) * self.each + (self.each if n is None else n + 1)

            def event(self, b, n, before):
                return (b + 2) * self.each + n + 1 - before

        def open_signals(sp, signals):
            for s in signals:
                sp.sem_inc(s.sem, 2 * s.each)

        def pipeline(engine, step, ahead, behind):
            def alone(b):
                step(b, b % 2, lambda k: 0 <= b + k < B)
            first, end = (behind + 1) // 2, (B - ahead) // 2
            for b in range(-ahead, 2 * first):
                alone(b)
            with engine.Fori(first, end) as i:
                for u in range(2):
                    step(2 * i + u, u, lambda k: True)
            for b in range(2 * end, B + behind):
                alone(b)

        def normed(dve, turn, into, b, signal):
            wide = [P, TT, D]
            nc.vector.tensor_tensor(into, seq_rows(h_all, b), bcast(seq_rows(moments, b)[:, :, 0:1], wide),
                                    ALU.subtract).then_inc(normed_steps, 1)
            dve.wait_ge(normed_steps, b + (turn * B + 1))
            nc.vector.tensor_tensor(into, into, bcast(rstd[:, bass.ds(b * TT, TT)][:, :, None], wide),
                                    ALU.mult).then_inc(signal, 1)

        attn_ctx = ExitStack()
        QK = sb(attn_ctx, "QK", [P, B * ROWS])
        QT, KT = QK[0:D], QK[D:P]
        V = sb(attn_ctx, "V", [P, B * TT, D])
        with ExitStack() as ctx:
            chunks = sb(ctx, "chunks", [P, 2, NCHUNK + 1])
            xn, zn = sb(ctx, "xn", [P, 2, TT, D]), sb(ctx, "zn", [P, 2, TT, D])
            xT = sb(ctx, "conv_xT", [P, 2, TAPS - 1 + ROWS])
            z = sb(ctx, "z", [P, 2, TT, D])
            zT = sb(ctx, "zT", [D, 2, ROWS])
            names = ["tok", "tok_copied", "tok_normed", "scaled", "xn", "xT", "xT_sb", "conv", "z", "zn", "zT", "zT_sb",
                     "qkv", "q_sb", "k_sb", "v_sb"]
            at = {n: Signal(f"front_{n}") for n in names}
            x_landed = [sem(f"x_landed{u}") for u in range(2)]
            padded = sem("conv_padded")
            TOK_BANK, X_BANK, CONV_BANK, Z_BANK, QK_BANK, V_BANK = range(6)

            def after(engine, name, b, before=0):
                engine.wait_ge(at[name].sem, at[name].done(b, before=before))

            def row_norm(name, eps, masked):
                return {
                    "eps": eps, "masked": masked,
                    "parts": sb(ctx, f"{name}_parts", [P, 2, TT, 6]), "moments": sb(ctx, f"{name}_moments", [P, 2, TT, 2]),
                    "var": sb(ctx, f"{name}_var", [P, 2, TT]), "std": sb(ctx, f"{name}_std", [P, 2, TT]),
                    "rstd": sb(ctx, f"{name}_rstd", [P, 2, TT]),
                    "has_var": Signal(f"{name}_has_var"), "has_std": Signal(f"{name}_has_std"),
                    "moment_steps": sem(f"{name}_moment_steps"), "apply_steps": sem(f"{name}_apply_steps"),
                }

            def norm_moments(dve, norm, b, u, rows):
                st = Steps(dve, norm["moment_steps"], 2, b)
                wait_apart(dve)
                for t in range(TT):
                    last = nc.vector.bn_stats(norm["parts"][:, u, t, :], rows[t])
                st.link(last)
                wait_apart(dve)
                for t in range(TT):
                    last = nc.vector.bn_aggr(norm["moments"][:, u, t, :], norm["parts"][:, u, t, :])
                st.link(last)
                nc.vector.tensor_scalar(norm["var"][:, u], norm["moments"][:, u, :, 1], norm["eps"], None,
                                        ALU.add).then_inc(norm["has_var"].sem, 1)

            def norm_roots(act, norm, b, u):
                act.wait_ge(norm["has_var"].sem, norm["has_var"].done(b))
                nc.scalar.activation(norm["std"][:, u], norm["var"][:, u], ACT.Sqrt).then_inc(norm["has_std"].sem, 1)

            def norm_apply(dve, norm, b, u, rows, into, signal):
                st = Steps(dve, norm["apply_steps"], 1 + norm["masked"], b)
                dve.wait_ge(norm["has_std"].sem, norm["has_std"].done(b))
                st.link(nc.vector.reciprocal(norm["rstd"][:, u], norm["std"][:, u]))
                if norm["masked"]:
                    st.link(nc.vector.tensor_tensor(norm["rstd"][:, u], norm["rstd"][:, u], w("pad_mask"), ALU.mult))
                for t in range(TT):
                    last = nc.vector.tensor_scalar(into[t], rows[t], norm["moments"][:, u, t, 0:1],
                                                   norm["rstd"][:, u, t:t + 1], ALU.subtract, ALU.mult)
                last.then_inc(signal, 1)

            tok_norm, conv_norm = row_norm("tok_ln", 1e-5, False), row_norm("conv_ln", 1e-5, True)
            qkv_norm = row_norm("qkv_ln", 1e-12, True)
            norms = [tok_norm, conv_norm, qkv_norm]

            def tiles(ap, b):
                return [ap[:, bass.ds(b * TT + t, 1), :].rearrange("p t d -> p (t d)") for t in range(TT)]

            def buffer_tiles(ap, u):
                return [ap[:, u, t, :] for t in range(TT)]

            AHEAD, BEHIND = 4, 2
            with nc.Block() as block:
                @block.sync
                def _(sp):
                    open_signals(sp, list(at.values()) + [n["has_var"] for n in norms] + [n["has_std"] for n in norms])
                    with sp.Fori(0, B // 2) as i:
                        for u in range(2):
                            after(sp, "tok", 2 * i + u, 2)
                            sp.dma_start(chunks[:, u, :], x_chunks[:, bass.ds(2 * i + u, 1), :]
                                         .rearrange("p b c -> p (b c)")).then_inc(x_landed[u], 16)
                    sp.dma_start(W[:, LATE:], weights[:, LATE:]).then_inc(loaded_late, 16)
                    sp.wait_ge(loaded_late, 16)

                @block.tensor
                def _(pe):
                    t_ = nc.tensor

                    def tokens(b, u):
                        pe.wait_ge(x_landed[u], 8 * (b - u) + 16)
                        after(pe, "tok_copied", b, 1)
                        for t in range(TT):
                            for half in range(2):
                                last = t_.matmul(psum[:, TOK_BANK, t * D:(t + 1) * D],
                                                 chunks[:, u, t * P + half:t * P + half + P],
                                                 w(f"tok_w{half}"), start=(half == 0), stop=(half == 1))
                        last.then_inc(at["tok"].sem, 1)

                    def transpose_rows(b, u, rows, bank, ready, left, signal):
                        after(pe, ready, b)
                        after(pe, left, b, 1)
                        wait_apart(pe)
                        for t in range(TT):
                            last = t_.transpose(psum[0:D, bank, t * P:(t + 1) * P], rows[:, u, t, :], ident)
                        last.then_inc(at[signal].sem, 1)

                    def convolution(b, u):
                        after(pe, "xT_sb", b)
                        after(pe, "z", b, 1)
                        for t in range(TT):
                            for k in range(TAP_PAIRS):
                                both = slice(0, P if 2 * k + 1 < TAPS else D)
                                last = t_.matmul(psum[:, CONV_BANK, t * D:(t + 1) * D],
                                                 xT[both, u, t * P + 2 * k:t * P + 2 * k + P], conv_x[both, k, :],
                                                 start=(k == 0), stop=(k == TAP_PAIRS - 1))
                        last.then_inc(at["conv"].sem, 1)

                    def qkv(b, u):
                        after(pe, "zT_sb", b)
                        after(pe, "q_sb", b, 1)
                        after(pe, "k_sb", b, 1)
                        after(pe, "v_sb", b, 1)
                        t_.matmul(psum[:, QK_BANK, 0:ROWS], qkv_x[:, 0:2, :].rearrange("p n d -> p (n d)"),
                                  zT[:, u], start=True, stop=True)
                        for t in range(TT):
                            last = t_.matmul(psum[:, V_BANK, t * D:(t + 1) * D], zT[:, u, t * P:(t + 1) * P],
                                             qkv_x[:, 2, :], start=True, stop=True)
                        last.then_inc(at["qkv"].sem, 1)

                    def step(b, u, there):
                        if there(-2):
                            qkv(b - 2, u)
                        if there(0):
                            convolution(b, u)
                        if there(1):
                            transpose_rows(b + 1, 1 - u, xn, X_BANK, "xn", "xT_sb", "xT")
                        if there(-1):
                            transpose_rows(b - 1, 1 - u, zn, Z_BANK, "zn", "zT_sb", "zT")
                        if there(4):
                            tokens(b + 4, u)

                    pe.wait_ge(padded, 1)
                    pipeline(pe, step, AHEAD, BEHIND)

                @block.scalar
                def _(act):
                    a = nc.scalar

                    def step(b, u, there):
                        if there(-2):
                            after(act, "qkv", b - 2)
                            a.activation(KT[:, bass.ds((b - 2) * ROWS, ROWS)], psum[D:P, QK_BANK, 0:ROWS],
                                         ACT.Identity, bias=k_bias[D:P]).then_inc(at["k_sb"].sem, 1)
                        if there(1):
                            after(act, "xT", b + 1)
                            after(act, "conv", b + 1, 2)
                            a.activation(xT[0:D, 1 - u, TAPS - 1:], psum[0:D, X_BANK, 0:ROWS], ACT.Copy)
                            a.activation(xT[D:P, 1 - u, TAPS - 2:TAPS - 2 + ROWS], psum[0:D, X_BANK, 0:ROWS],
                                         ACT.Copy).then_inc(at["xT_sb"].sem, 1)
                        if there(-1):
                            after(act, "zT", b - 1)
                            after(act, "qkv", b - 1, 2)
                            a.activation(zT[:, 1 - u], psum[0:D, Z_BANK, 0:ROWS], ACT.Copy).then_inc(at["zT_sb"].sem, 1)
                        if there(0):
                            norm_roots(act, qkv_norm, b, u)
                        if there(2):
                            norm_roots(act, conv_norm, b + 2, u)
                        if there(4):
                            norm_roots(act, tok_norm, b + 4, u)
                    pipeline(act, step, AHEAD, BEHIND)

                @block.gpsimd
                def _(pool):
                    g = nc.gpsimd
                    tok_scaled = sem("tok_scaled")

                    def step(b, u, there):
                        if there(3):
                            rows = seq_rows(h_all, b + 3)
                            after(pool, "tok_normed", b + 3)
                            g.tensor_tensor(rows, rows, bcast(w("tok_gamma")[:, None, :], [P, TT, D]),
                                            ALU.mult).then_inc(tok_scaled, 1)
                            pool.wait_ge(tok_scaled, b + 4)
                            wait_apart(pool)
                            g.tensor_tensor(rows, rows, bcast(w("tok_beta")[:, None, :], [P, TT, D]),
                                            ALU.add).then_inc(at["scaled"].sem, 1)
                    pipeline(pool, step, AHEAD, BEHIND)

                @block.vector
                def _(dve):
                    v = nc.vector

                    def keep_tokens(b, u):
                        after(dve, "tok", b)
                        v.tensor_tensor(seq_rows(h_all, b), psum[:, TOK_BANK, 0:TT * D].rearrange("p (t d) -> p t d", t=TT),
                                        bcast(w("tok_b")[:, None, :], [P, TT, D]), ALU.add).then_inc(at["tok_copied"].sem, 1)
                        after(dve, "tok_copied", b)
                        after(dve, "tok_normed", b, 2)
                        norm_moments(dve, tok_norm, b, u, tiles(h_all, b))

                    def keep_z(b, u):
                        after(dve, "conv", b)
                        after(dve, "zn", b, 2)
                        v.tensor_tensor(z[:, u], two_tiles(psum[:, CONV_BANK, 0:TT * D]),
                                        bcast(conv_bias[:, None, :], [P, TT, D]), ALU.add).then_inc(at["z"].sem, 1)
                        after(dve, "z", b)
                        norm_moments(dve, qkv_norm, b, u, buffer_tiles(z, u))

                    def keep_q(b, u):
                        after(dve, "qkv", b)
                        v.tensor_scalar(QT[:, bass.ds(b * ROWS, ROWS)], psum[0:D, QK_BANK, 0:ROWS],
                                        q_bias[:], DK ** -0.5, ALU.add, ALU.mult).then_inc(at["q_sb"].sem, 1)
                        v.tensor_tensor(seq_rows(V, b), two_tiles(psum[:, V_BANK, 0:TT * D]),
                                        bcast(v_bias[:, None, :], [P, TT, D]), ALU.add).then_inc(at["v_sb"].sem, 1)

                    def step(b, u, there):
                        if there(1):
                            after(dve, "xT", b + 1, 2)
                            norm_apply(dve, conv_norm, b + 1, 1 - u, tiles(h_all, b + 1), buffer_tiles(xn, 1 - u), at["xn"].sem)
                        if there(-1):
                            after(dve, "zT", b - 1, 2)
                            norm_apply(dve, qkv_norm, b - 1, 1 - u, buffer_tiles(z, 1 - u), buffer_tiles(zn, 1 - u), at["zn"].sem)
                        if there(-2):
                            keep_q(b - 2, u)
                        if there(0):
                            keep_z(b, u)
                        if there(3):
                            rows = tiles(h_all, b + 3)
                            norm_apply(dve, tok_norm, b + 3, 1 - u, rows, rows, at["tok_normed"].sem)
                        if there(2):
                            after(dve, "scaled", b + 2)
                            after(dve, "xn", b + 2, 2)
                            norm_moments(dve, conv_norm, b + 2, u, tiles(h_all, b + 2))
                        if there(4):
                            keep_tokens(b + 4, u)

                    v.memset(xT[0:D, :, 0:TAPS - 1], 0.0)
                    v.memset(xT[D:P, :, 0:TAPS - 2], 0.0).then_inc(padded, 1)
                    pipeline(dve, step, AHEAD, BEHIND)

        with ExitStack() as ctx:
            tables = sb(ctx, "tables_sb", [P, 2, PACKED])
            distance, no_reset = tables[:, 0], tables[:, 1]
            causal = sb(ctx, "causal", [P, 2 * P])
            Qd = sb(ctx, "Qd", [D, 2, NQ, H, QB])
            Kb = sb(ctx, "Kb", [D, 2, ROWS])
            VM_COLS = 2 * H * P
            Vm = sb(ctx, "Vm", [P, 2, VM_COLS + P])
            S = sb(ctx, "S", [P, 2, PACKED])
            Ex = sb(ctx, "Ex", [P, 2, PACKED + 1])
            PT = sb(ctx, "PT", [P, 2, WIDE])
            Y = Ex[:, :, 1:]
            S2 = sb(ctx, "S2", [P, 2, WIDE])
            top1, top2 = sb(ctx, "top1", [P, 2, NQ]), sb(ctx, "top2", [P, 2, NQ])
            neg_top = sb(ctx, "neg_top", [P, 2, NQ])
            scale = sb(ctx, "scale", [P, 2, NQ])
            inv = sb(ctx, "inv", [D, 2, ROWS])
            oT = sb(ctx, "oT", [D, 2, ROWS])
            k_landed = [sem(f"k_landed{u}") for u in range(2)]
            NB = len(BANKS)
            PARTS = [slice(0, PACKED // 2), slice(PACKED // 2, PACKED)]
            SLOT = {j: NQ - 1 - j if j >= HALF else HALF + j for j in range(NQ)}
            tables_landed, prepared, pool_prepared = sem("tables_landed"), sem("prepared"), sem("pool_prepared")
            q_ready, v_ready, y_ready1 = Signal("qd_ready"), Signal("vm_ready"), Signal("dist_ready")
            s_ready, top_ready = Signal("s_ready", NB), Signal("top_ready", NB)
            e_ready, scan_ready, root_ready, te_ready, y_used = Signal("e_ready"), Signal("scan_ready"), Signal("root_ready"), Signal("te_ready", 2), Signal("effects_used")
            s2_ready, t_ready, p_ready = Signal("s2_ready", 2), Signal("t_ready", 3), Signal("p_ready", 3)
            pv_ready, o_ready, y_done, h_added = Signal("pv_ready"), Signal("o_ready"), Signal("proj_ready"), Signal("h_added")
            max_steps, scale_steps = sem("attn_max_steps"), sem("attn_scale_steps")
            shift_steps, out_steps = sem("attn_shift_steps"), sem("attn_out_steps")

            with nc.Block() as block:
                @block.sync
                def _(sp):
                    sp.dma_start(tables[:], packed_tables).then_inc(tables_landed, 16)
                    open_signals(sp, [q_ready, v_ready, y_ready1, s_ready, top_ready, e_ready, scan_ready, root_ready,
                              te_ready, y_used, s2_ready, t_ready, p_ready, pv_ready, o_ready, y_done, h_added])
                    with sp.Fori(0, B // 2) as i:
                        for u in range(2):
                            b = 2 * i + u
                            sp.wait_ge(s_ready.sem, s_ready.done(b, before=2))
                            sp.dma_start(Kb[:, u], KT[:, bass.ds(b * ROWS, ROWS)]).then_inc(k_landed[u], 16)

                @block.gpsimd
                def _(pool):
                    g = nc.gpsimd

                    def prepare():
                        g.memset(S2[:], NEG)
                        g.memset(Vm[:], 0.0).then_inc(pool_prepared, 1)
                        pool.wait_ge(pool_prepared, 1)
                        for u in range(2):
                            for kb in range(2):
                                at = kb * H * P
                                ones = Vm[:, u, at + D:at + D + H * (P + DK)].rearrange("p (h s) -> p h s", h=H)[:, :, 0:DK]
                                last = g.memset(ones, 1.0)
                        last.then_inc(pool_prepared, 1)
                        pool.wait_ge(pool_prepared, 2)
                        pool.wait_ge(tables_landed, 16)

                    def queries(b, u):
                        pool.wait_ge(s_ready.sem, s_ready.done(b, before=2))
                        qs = QT[:, bass.ds(b * ROWS, ROWS)].rearrange("p (j q) -> p j q", j=NQ)
                        g.tensor_tensor(
                            Qd[:, u], bcast(qs[:, :, None, :], [D, NQ, H, QB]),
                            bcast(w("head_mask", D)[:, None, :, None], [D, NQ, H, QB]), ALU.mult).then_inc(q_ready.sem, 1)

                    def values(b, u):
                        pool.wait_ge(pv_ready.sem, pv_ready.done(b, before=2))
                        for kb in range(2):
                            at = kb * H * P
                            mine = Vm[:, u, at:at + H * (P + DK)].rearrange("p (h s) -> p h s", h=H)[:, :, 0:DK]
                            last = g.tensor_copy(mine, V[:, bass.ds(b * TT + kb, 1), :]
                                                 .rearrange("p t (h d) -> p (t h) d", h=H))
                        last.then_inc(v_ready.sem, 1)

                    def distances(b, u):
                        pool.wait_ge(scan_ready.sem, scan_ready.done(b))
                        g.tensor_tensor(Y[:, u], Y[:, u], distance, ALU.mult).then_inc(y_ready1.sem, 1)

                    def step(b, u, there):
                        if there(2):
                            queries(b + 2, u)
                        if there(1) and not there(0):
                            prepare()
                        if there(-1):
                            values(b - 1, 1 - u)
                        if there(1):
                            distances(b + 1, 1 - u)
                    pipeline(pool, step, 2, 3)

                @block.tensor
                def _(pe):
                    t_ = nc.tensor

                    def scores(b, u):
                        pe.wait_ge(q_ready.sem, q_ready.done(b))
                        pe.wait_ge(k_landed[u], 8 * (b - u) + 16)
                        for n, bank in enumerate(BANKS):
                            pe.wait_ge(top_ready.sem, top_ready.event(b, n, before=2))
                            for j in bank:
                                at = IN_BANK[j]
                                last = t_.matmul(psum[:, (u * NB + n) % 2, at:at + SPAN[j]],
                                                 Qd[:, u, j].rearrange("p h q -> p (h q)"),
                                                 Kb[:, u, 0:SPAN[j]], start=True, stop=True)
                            last.then_inc(s_ready.sem, 1)

                    def transposes(b, u, thirds):
                        for c in thirds:
                            pe.wait_ge(s2_ready.sem, s2_ready.done(b, min(c, 1)))
                            pe.wait_ge(p_ready.sem, p_ready.event(b, c, before=2))
                            for n in range(HALF):
                                at = P * n if c == 0 else WIDE_OFF[HALF + n] + P * (c - 1)
                                last = t_.transpose(
                                    psum[:, 2 + 2 * ((3 * u + c) % 2) + n // 4, (n % 4) * P:(n % 4 + 1) * P],
                                    S2[:, u, at:at + P], ident)
                            last.then_inc(t_ready.sem, 1)

                    def weighted_values(b, u, heads):
                        if 0 in heads:
                            pe.wait_ge(v_ready.sem, v_ready.done(b))
                            pe.wait_ge(p_ready.sem, p_ready.done(b))
                            pe.wait_ge(h_added.sem, h_added.done(b, before=2))
                        probs = PT[:, u].rearrange("p (n q) -> p n q", q=P)
                        for h in heads:
                            vm = [Vm[:, u, (kb * H + h) * P:(kb * H + h + 1) * P] for kb in range(2)]
                            for kb in ((0, 1) if h == 0 else (1, 0)):
                                mine = (probs[:, 0:NQ] if kb == 0 else probs[:, NQ:])[:, :, h * QB:(h + 1) * QB]
                                last = t_.matmul(psum[:, 6 + u, kb * P:ROWS], vm[kb], mine,
                                                 start=(h == 0 and kb == 0), stop=(h == H - 1 and kb == 0),
                                                 skip_group_check=True)
                        if H - 1 in heads:
                            last.then_inc(pv_ready.sem, 1)

                    def projection(b, u):
                        pe.wait_ge(o_ready.sem, o_ready.done(b))
                        for t in range(TT):
                            last = t_.matmul(psum[:, 6 + u, ROWS + t * D:ROWS + (t + 1) * D], oT[:, u, t * P:(t + 1) * P],
                                             w("out_w"), start=True, stop=True)
                        last.then_inc(y_done.sem, 1)

                    def step(b, u, there):
                        if there(1):
                            scores(b + 1, 1 - u)
                        if there(-2):
                            weighted_values(b - 2, u, range(0, H // 2))
                        if there(-1):
                            transposes(b - 1, 1 - u, (0,))
                        if there(-2):
                            weighted_values(b - 2, u, range(H // 2, H))
                        if there(-3):
                            projection(b - 3, 1 - u)
                        if there(-1):
                            transposes(b - 1, 1 - u, (1, 2))
                    pipeline(pe, step, 2, 3)

                @block.scalar
                def _(act):
                    a = nc.scalar

                    def exponentials(b, u):
                        act.wait_ge(y_used.sem, y_used.done(b, before=2))
                        for n, bank in enumerate(BANKS):
                            act.wait_ge(top_ready.sem, top_ready.done(b, n))
                            for j in bank:
                                k = ORDER.index(j)
                                last = a.activation(
                                    Ex[:, u, OFF[j]:OFF[j] + SPAN[j]], S[:, u, OFF[j]:OFF[j] + SPAN[j]], ACT.Exp,
                                    bias=neg_top[:, u, k:k + 1])
                        last.then_inc(e_ready.sem, 1)

                    def roots(b, u):
                        act.wait_ge(y_ready1.sem, y_ready1.done(b))
                        for j in SB_ORDER:
                            k = SLOT[j]
                            at = Y[:, u, OFF[j]:OFF[j] + SPAN[j]]
                            last = a.activation(at, at, ACT.Sqrt, scale=scale[:, u, k:k + 1])
                        last.then_inc(root_ready.sem, 1)

                    def effects(b, u):
                        act.wait_ge(root_ready.sem, root_ready.done(b))
                        for part in PARTS:
                            a.activation(Y[:, u, part], Y[:, u, part], ACT.Exp, scale=-1.0).then_inc(te_ready.sem, 1)

                    def probabilities(b, u):
                        act.wait_ge(pv_ready.sem, pv_ready.done(b, before=2))
                        for c in range(3):
                            act.wait_ge(t_ready.sem, t_ready.done(b, c))
                            bank = 2 + 2 * ((3 * u + c) % 2)
                            a.activation(
                                PT[:, u, c * HALF * P:(c + 1) * HALF * P].rearrange("p (n q) -> p n q", q=P),
                                psum[:, bank:bank + 2, :].rearrange("p k (n q) -> p (k n) q", q=P), ACT.Exp).then_inc(p_ready.sem, 1)

                    def step(b, u, there):
                        if there(0):
                            roots(b, u)
                        if there(1):
                            exponentials(b + 1, 1 - u)
                        if there(0):
                            effects(b, u)
                        if there(-1):
                            probabilities(b - 1, 1 - u)
                    pipeline(act, step, 2, 3)

                @block.vector
                def _(dve):
                    v = nc.vector
                    v.memset(oT[:], 0.0)
                    v.memset(Ex[:, :, PACKED:], 0.0)
                    v.memset(causal[:], 0.0).then_inc(prepared, 1)
                    dve.wait_ge(prepared, 1)
                    v.tensor_copy(causal[:, 2 * P - QB:], w("last_key")).then_inc(prepared, 1)
                    dve.wait_ge(prepared, 2)
                    dve.wait_ge(tables_landed, 16)

                    def masked_scores(b, u):
                        dve.wait_ge(e_ready.sem, e_ready.done(b, before=2))
                        dve.wait_ge(y_used.sem, y_used.done(b, before=2))
                        for n, bank in enumerate(BANKS):
                            dve.wait_ge(s_ready.sem, s_ready.done(b, n))
                            wait_apart(dve)
                            for j in bank:
                                k = ORDER.index(j)
                                at = IN_BANK[j]
                                last = v.tensor_tensor_reduce(
                                    S[:, u, OFF[j]:OFF[j] + SPAN[j]], psum[:, (u * NB + n) % 2, at:at + SPAN[j]],
                                    causal[:, 2 * P - SPAN[j]:], 1.0, -3e38, ALU.add, ALU.max, top1[:, u, k:k + 1])
                            last.then_inc(max_steps, 1)
                            k0 = ORDER.index(bank[0])
                            dve.wait_ge(max_steps, b * NB + n + 1)
                            v.tensor_scalar(
                                neg_top[:, u, k0:k0 + len(bank)], top1[:, u, k0:k0 + len(bank)], -1.0, None, ALU.mult).then_inc(top_ready.sem, 1)

                    def later_sums(b, u):
                        st = Steps(dve, scale_steps, 2, b)
                        dve.wait_ge(e_ready.sem, e_ready.done(b))
                        dve.wait_ge(root_ready.sem, root_ready.done(b, before=2))
                        st.link(v.tensor_tensor_scan(
                            Ex[:, u, 0:PACKED][:, ::-1], no_reset[:, ::-1], Ex[:, u, 0:PACKED][:, ::-1],
                            0.0, ALU.mult, ALU.add))
                        v.reciprocal(scale[:, u, 0:HALF], Ex[:, u, 0:OFF[HALF] + 1:PAIR])
                        st.link(v.reciprocal(scale[:, u, HALF:], Ex[:, u, OFF[0]:OFF[HALF - 1] + 1:OFF[0]]))
                        v.tensor_scalar(scale[:, u], scale[:, u], gamma_sq[:], None, ALU.mult).then_inc(scan_ready.sem, 1)
                        st.end()

                    def scaled_scores(b, u):
                        st = Steps(dve, shift_steps, 2, b)
                        dve.wait_ge(t_ready.sem, t_ready.done(b, before=2))
                        dve.wait_ge(pool_prepared, 2)
                        for j in SB_ORDER:
                            for n, part in enumerate(PARTS):
                                if OFF[j] == part.start:
                                    dve.wait_ge(te_ready.sem, te_ready.done(b, n))
                                    st.link(v.tensor_scalar(Y[:, u, part], Y[:, u, part], 1e-5, 1e5, ALU.max, ALU.min))
                                    wait_apart(dve)
                            last = v.tensor_tensor_reduce(
                                S2[:, u, WIDE_OFF[j]:WIDE_OFF[j] + SPAN[j]], Y[:, u, OFF[j]:OFF[j] + SPAN[j]],
                                S[:, u, OFF[j]:OFF[j] + SPAN[j]], 1.0, -3e38, ALU.mult, ALU.max, top2[:, u, j:j + 1])
                        last.then_inc(y_used.sem, 1)
                        st.end()

                    def shifted_scores(b, u):
                        dve.wait_ge(y_used.sem, y_used.done(b))
                        for j in range(NQ):
                            at = S2[:, u, WIDE_OFF[j]:WIDE_OFF[j] + SPAN[j]]
                            last = v.tensor_scalar(at, at, top2[:, u, j:j + 1], None, ALU.subtract)
                            if j in (HALF - 1, NQ - 1):
                                last.then_inc(s2_ready.sem, 1)

                    def heads_outputs(b, u):
                        st = Steps(dve, out_steps, 2, b)
                        dve.wait_ge(pv_ready.sem, pv_ready.done(b))
                        dve.wait_ge(y_done.sem, y_done.done(b, before=2))
                        st.link(v.reciprocal(inv[:, u], psum[D:2 * D, 6 + u, 0:ROWS]))
                        v.tensor_tensor(oT[:, u, 1:], psum[0:D, 6 + u, 1:ROWS], inv[:, u, 1:], ALU.mult).then_inc(o_ready.sem, 1)
                        st.link(v.tensor_tensor(seq_rows(h_all, b), seq_rows(h_all, b),
                                                bcast(w("out_b")[:, None, :], [P, TT, D]), ALU.add))
                        st.end()

                    def added(b, u):
                        dve.wait_ge(y_done.sem, y_done.done(b))
                        v.tensor_tensor(seq_rows(h_all, b), seq_rows(h_all, b),
                                        two_tiles(psum[:, 6 + u, ROWS:ROWS + TT * D]), ALU.add).then_inc(h_added.sem, 1)

                    def step(b, u, there):
                        if there(-1):
                            scaled_scores(b - 1, 1 - u)
                        if there(1):
                            masked_scores(b + 1, 1 - u)
                        if there(-1):
                            shifted_scores(b - 1, 1 - u)
                        if there(-3):
                            heads_outputs(b - 3, 1 - u)
                        if there(1):
                            later_sums(b + 1, 1 - u)
                        if there(-3):
                            added(b - 3, 1 - u)
                    pipeline(dve, step, 2, 3)
        attn_ctx.close()
        HP = H // 2
        with ExitStack() as ctx:
            layer_stats("ffn_ln", 1e-5)
            D1 = D + 1
            logit_w = sb(ctx, "logit_w", [D1, H, G])
            mix_w = sb(ctx, "mix_w", [D1, H, D1])
            vo_w = sb(ctx, "vo_w", [D1, H, D])
            inv_temp = sb(ctx, "inv_temp", [P, H])
            fw_tensor, fw_vector = sem("fw_tensor"), sem("fw_vector")
            with ExitStack() as inner, nc.Block() as block:
                kq = sb(inner, "kq", [D, D])
                kq_fx = sb(inner, "kq_fx", [D, H, D1])
                vo = sb(inner, "vo", [D, H, D])
                fx_wT = w("fx_wT").rearrange("p (h c) -> p h c", h=H)
                STEPS_TO_KQ, STEPS_TO_KQ_FX = 2, 4
                @block.tensor
                def _(pe):
                    for h in range(H):
                        nc.tensor.matmul(psum[0:D, 0, h * G:(h + 1) * G], w("x_w")[:, h * D:(h + 1) * D], w("slice_w"),
                                         start=True, stop=True)
                    for h in range(H):
                        nc.tensor.matmul(psum[D:D1, 3, h * G:(h + 1) * G], w("x_b")[:, h:h + 1], w("slice_w"),
                                         start=True, stop=True)
                    nc.tensor.matmul(psum[0:D, 1, 0:D], w("fk_w"), w("fq_w"), start=True, stop=True)
                    nc.tensor.matmul(psum[0:D, 2, :], w("fv_w"), w("fout_w"), start=True, stop=True).then_inc(fw_tensor, 1)
                    pe.wait_ge(fw_vector, STEPS_TO_KQ)
                    for half in range(2):
                        nc.tensor.matmul(psum[0:D, 4 + half, 0:HP * D1], kq[:], fx_wT[:, half * HP:(half + 1) * HP]
                                         .rearrange("p h c -> p (h c)"), start=True, stop=True)
                    for h in range(H):
                        last = nc.tensor.matmul(psum[0:D1, 6, h * D:(h + 1) * D], fx_wT[:, h], vo[:, h], start=True, stop=True)
                    last.then_inc(fw_tensor, 1)
                    pe.wait_ge(fw_vector, STEPS_TO_KQ_FX)
                    for h in range(H):
                        last = nc.tensor.matmul(psum[0:D1, 1 + h // HP, (h % HP) * D1:(h % HP + 1) * D1], fx_wT[:, h],
                                                kq_fx[:, h], start=True, stop=True)
                    last.then_inc(fw_tensor, 1)

                @block.vector
                def _(dve):
                    v = nc.vector
                    st = Steps(dve, fw_vector)
                    dve.wait_ge(fw_tensor, 1)
                    st.step(v.tensor_copy(kq[:], psum[0:D, 1, 0:D]))
                    st.step(v.tensor_copy(vo[:], psum[0:D, 2, :].rearrange("p (h g) -> p h g", h=H)))
                    assert st.n == STEPS_TO_KQ
                    dve.wait_ge(fw_tensor, 2)
                    st.step(v.tensor_copy(kq_fx[:].rearrange("p (k h) c -> p k (h c)", k=2), psum[0:D, 4:6, 0:HP * D1]))
                    st.step(v.tensor_copy(vo_w[:], psum[0:D1, 6, :].rearrange("p (h g) -> p h g", h=H)))
                    assert st.n == STEPS_TO_KQ_FX
                    st.link(v.tensor_scalar(inv_temp[:], w("temp"), 0.1, 5.0, ALU.max, ALU.min))
                    st.link(v.reciprocal(inv_temp[:], inv_temp[:]))
                    v.tensor_tensor(logit_w[0:D], psum[0:D, 0, :].rearrange("p (h g) -> p h g", h=H),
                                    bcast(inv_temp[0:D, :, None], [D, H, G]), ALU.mult)
                    st.link(v.tensor_tensor(logit_w[D:D1], psum[D:D1, 3, :].rearrange("p (h g) -> p h g", h=H),
                                            bcast(w("slice_b")[D:D1, None, :], [1, H, G]), ALU.add))
                    v.tensor_tensor(logit_w[D:D1], logit_w[D:D1], bcast(inv_temp[D:D1, :, None], [1, H, G]), ALU.mult)
                    dve.wait_ge(fw_tensor, 3)
                    v.tensor_copy(mix_w[:].rearrange("p (k h) c -> p k (h c)", k=2), psum[0:D1, 1:3, 0:HP * D1])

            parts, small = sb(ctx, "ffn_parts", [P, 2, TT, 6]), sb(ctx, "ffn_small", [P, 2, TT, 2])
            xn = sb(ctx, "ffn_xn", [P, 2, TT, D1])
            xT = sb(ctx, "ffn_xT", [D1, 2, ROWS])
            Wn = sb(ctx, "Wn", [P, 2, TT, H, G])
            WT = sb(ctx, "WT", [P, 2, HP, ROWS])
            wtop, winv = sb(ctx, "wtop", [P, 2, TT, H]), sb(ctx, "winv", [P, 2, TT, H])
            slice_inv, row_stat = sb(ctx, "slice_inv", [P, 2, HP]), sb(ctx, "row_stat", [P, 2, HP])
            ST = sb(ctx, "ST", [P, 2, HP, D1])
            stT = sb(ctx, "stT", [D1, 2, H, G])
            mixT = sb(ctx, "mixT", [D1, 2, H, G])
            VO = sb(ctx, "VO", [G, 2, H, D])
            A = sb(ctx, "A", [P, 2, HP, G])
            aT = sb(ctx, "aT", [G, 2, H, G])
            OW = sb(ctx, "OW", [P, 2, HP, D])
            X_BANK, LOGIT_BANK, W_BANK, SLICE_BANK, SCORE_BANK, ROW_BANK = 0, 1, 3, 5, 6, 7
            ST_BANK, VO_BANK, MIX_BANK = W_BANK, W_BANK + 1, SLICE_BANK
            names = ["xn", "xT", "xT_sb", "logits", "shifted", "exped", "winv", "wn", "slices", "wT",
                     "wT_sb", "slices_sb", "stT", "stT_sb", "mix", "vo", "mixT_sb", "vo_sb", "scores", "sc_shifted",
                     "sc_exped", "attn", "aT", "aT_sb", "ow", "ow_sb", "rows", "h_added"]
            at = {n: Signal(f"ffn_{n}") for n in names}
            top_steps, sum_steps, mean_steps = sem("ffn_top_steps"), sem("ffn_sum_steps"), sem("ffn_mean_steps")
            score_steps, attn_steps, row_steps = sem("ffn_score_steps"), sem("ffn_attn_steps"), sem("ffn_row_steps")
            ready = sem("ffn_prepared")

            def after(engine, name, b, before=0):
                engine.wait_ge(at[name].sem, at[name].done(b, before=before))

            with nc.Block() as block:
                @block.sync
                def _(sp):
                    open_signals(sp, list(at.values()))

                @block.tensor
                def _(pe):
                    t_ = nc.tensor

                    def transpose_x(b, u):
                        after(pe, "xn", b)
                        after(pe, "xT_sb", b, 1)
                        wait_apart(pe)
                        for t in range(TT):
                            last = t_.transpose(psum[0:D, X_BANK, t * P:(t + 1) * P], xn[:, u, t, 0:D], ident)
                        last.then_inc(at["xT"].sem, 1)

                    def logits(b, u):
                        after(pe, "xT_sb", b)
                        after(pe, "shifted", b, 1)
                        for t in range(TT):
                            last = t_.matmul(psum[:, LOGIT_BANK + t, :], xT[:, u, t * P:(t + 1) * P],
                                             logit_w[:].rearrange("p h g -> p (h g)"), start=True, stop=True)
                        last.then_inc(at["logits"].sem, 1)

                    def slices(b, u):
                        after(pe, "wn", b)
                        after(pe, "stT_sb", b, 1)
                        after(pe, "vo_sb", b, 1)
                        for t in range(TT):
                            for hp in range(HP):
                                last = t_.transpose(psum[:, W_BANK + hp // 2, (hp % 2) * ROWS + t * P:(hp % 2) * ROWS + (t + 1) * P],
                                                    Wn[:, u, t, 2 * hp:2 * hp + 2, :].rearrange("p h g -> p (h g)"), ident)
                        last.then_inc(at["wT"].sem, 1)
                        after(pe, "mixT_sb", b, 1)
                        for hp in range(HP):
                            for t in range(TT):
                                last = t_.matmul(psum[:, SLICE_BANK, hp * D1:(hp + 1) * D1],
                                                 Wn[:, u, t, 2 * hp:2 * hp + 2, :].rearrange("p h g -> p (h g)"),
                                                 xn[:, u, t, :], start=(t == 0), stop=(t == TT - 1))
                        last.then_inc(at["slices"].sem, 1)

                    def transpose_slices(b, u):
                        after(pe, "slices_sb", b)
                        after(pe, "wT_sb", b)
                        wait_apart(pe)
                        for hp in range(HP):
                            last = t_.transpose(psum[0:D1, ST_BANK, hp * P:(hp + 1) * P], ST[:, u, hp, :], ident)
                        last.then_inc(at["stT"].sem, 1)

                    def mix(b, u):
                        after(pe, "stT_sb", b)
                        wait_apart(pe)
                        for h in range(H):
                            last = t_.matmul(psum[0:D1, MIX_BANK, h * G:(h + 1) * G], mix_w[:, h], stT[:, u, h, :],
                                             start=True, stop=True)
                        last.then_inc(at["mix"].sem, 1)
                        for h in range(H):
                            last = t_.matmul(psum[0:G, VO_BANK, h * D:(h + 1) * D], stT[:, u, h, :], vo_w[:, h, :],
                                             start=True, stop=True)
                        last.then_inc(at["vo"].sem, 1)

                    def scores(b, u):
                        after(pe, "mixT_sb", b)
                        after(pe, "ow_sb", b, 1)
                        wait_apart(pe)
                        for h in range(H):
                            last = t_.matmul(psum[(h % 2) * G:(h % 2 + 1) * G, SCORE_BANK, (h // 2) * G:(h // 2 + 1) * G],
                                             mixT[:, u, h, :], stT[:, u, h, :], start=True, stop=True)
                        last.then_inc(at["scores"].sem, 1)

                    def transpose_attention(b, u):
                        after(pe, "attn", b)
                        after(pe, "h_added", b, 1)
                        wait_apart(pe)
                        for hp in range(HP):
                            last = t_.transpose(psum[0:G, ROW_BANK, hp * P:(hp + 1) * P], A[:, u, hp, :], ident)
                        last.then_inc(at["aT"].sem, 1)

                    def attended(b, u):
                        after(pe, "aT_sb", b)
                        after(pe, "vo_sb", b)
                        wait_apart(pe)
                        for h in range(H):
                            last = t_.matmul(psum[(h % 2) * G:(h % 2 + 1) * G, SCORE_BANK, (h // 2) * D:(h // 2 + 1) * D],
                                             aT[:, u, h, :], VO[:, u, h, :], start=True, stop=True)
                        last.then_inc(at["ow"].sem, 1)

                    def rows_out(b, u):
                        after(pe, "ow_sb", b)
                        for t in range(TT):
                            for hp in range(HP):
                                last = t_.matmul(psum[:, ROW_BANK, t * D:(t + 1) * D], WT[:, u, hp, t * P:(t + 1) * P],
                                                 OW[:, u, hp, :], start=(hp == 0), stop=(hp == HP - 1))
                        last.then_inc(at["rows"].sem, 1)

                    def step(b, u, there):
                        if there(1):
                            transpose_x(b + 1, 1 - u)
                        if there(-1):
                            scores(b - 1, 1 - u)
                        if there(1):
                            logits(b + 1, 1 - u)
                        if there(0):
                            slices(b, u)
                        if there(-1):
                            transpose_attention(b - 1, 1 - u)
                        if there(-1):
                            attended(b - 1, 1 - u)
                        if there(0):
                            transpose_slices(b, u)
                        if there(-1):
                            rows_out(b - 1, 1 - u)
                        if there(0):
                            mix(b, u)

                    pe.wait_ge(ready, 1)
                    pipeline(pe, step, 2, 1)

                @block.scalar
                def _(act):
                    a = nc.scalar

                    def step(b, u, there):
                        x, y = 1 - u, 1 - u
                        if there(1):
                            after(act, "xT", b + 1)
                            after(act, "logits", b + 1, 2)
                            a.activation(xT[0:D, x], psum[0:D, X_BANK, 0:ROWS], ACT.Copy).then_inc(at["xT_sb"].sem, 1)
                        if there(-1):
                            after(act, "sc_shifted", b - 1)
                            a.activation(A[:, y], A[:, y], ACT.Exp).then_inc(at["sc_exped"].sem, 1)
                        if there(0):
                            after(act, "wT", b)
                            after(act, "rows", b, 2)
                            a.activation(WT[:, u].rearrange("p h n -> p (h n)"),
                                         psum[:, W_BANK:W_BANK + 2, :].rearrange("p k n -> p (k n)"),
                                         ACT.Copy).then_inc(at["wT_sb"].sem, 1)
                        if there(-1):
                            after(act, "aT", b - 1)
                            after(act, "ow", b - 1, 2)
                            a.activation(aT[:, y].rearrange("p h g -> p (h g)"), psum[0:G, ROW_BANK, :],
                                         ACT.Copy).then_inc(at["aT_sb"].sem, 1)
                        if there(1):
                            after(act, "shifted", b + 1)
                            a.activation(Wn[:, x], Wn[:, x], ACT.Exp).then_inc(at["exped"].sem, 1)
                        if there(0):
                            after(act, "stT", b)
                            after(act, "scores", b, 2)
                            a.activation(stT[:, u].rearrange("p h g -> p (h g)"), psum[0:D1, ST_BANK, :],
                                         ACT.Copy).then_inc(at["stT_sb"].sem, 1)
                        if there(0):
                            after(act, "mix", b)
                            a.activation(mixT[:, u].rearrange("p h g -> p (h g)"), psum[0:D1, MIX_BANK, :],
                                         ACT.Copy, scale=D ** -0.5).then_inc(at["mixT_sb"].sem, 1)
                    pipeline(act, step, 2, 1)

                @block.gpsimd
                def _(pool):
                    def step(b, u, there):
                        if there(1):
                            after(pool, "winv", b + 1)
                            wn = Wn[:, 1 - u].rearrange("p t h g -> p (t h) g")
                            nc.gpsimd.tensor_tensor(
                                wn, wn, bcast(winv[:, 1 - u].rearrange("p t h -> p (t h)")[:, :, None], [P, TT * H, G]),
                                ALU.mult).then_inc(at["wn"].sem, 1)
                    pipeline(pool, step, 2, 1)

                @block.vector
                def _(dve):
                    v = nc.vector
                    v.memset(xT[D:D1], 1.0)
                    v.memset(xn[:, :, :, D:], 1.0).then_inc(ready, 1)

                    def normalised(b, u):
                        after(dve, "slices", b, 2)
                        normed(dve, 0, xn[:, u, :, 0:D], b, at["xn"].sem)

                    def less_top(b, u):
                        st = Steps(dve, top_steps, 1, b)
                        after(dve, "logits", b)
                        after(dve, "slices", b, 2)
                        lg = psum[:, LOGIT_BANK:LOGIT_BANK + 2, :].rearrange("p t (h g) -> p (t h) g", g=G)
                        wt = wtop[:, u].rearrange("p t h -> p (t h)")
                        st.link(v.tensor_reduce(wt, lg, X, ALU.max))
                        v.tensor_tensor(Wn[:, u].rearrange("p t h g -> p (t h) g"), lg,
                                        bcast(wt[:, :, None], [P, TT * H, G]), ALU.subtract).then_inc(at["shifted"].sem, 1)

                    def weight_sums(b, u):
                        st = Steps(dve, sum_steps, 2, b)
                        after(dve, "exped", b)
                        wi = winv[:, u].rearrange("p t h -> p (t h)")
                        st.link(v.tensor_reduce(wi, Wn[:, u].rearrange("p t h g -> p (t h) g"), X, ALU.add))
                        st.link(v.reciprocal(wi, wi))
                        v.tensor_tensor(winv[:, u], winv[:, u], bcast(w("pad_mask")[:, :, None], [P, TT, H]),
                                        ALU.mult).then_inc(at["winv"].sem, 1)

                    def slice_means(b, u):
                        st = Steps(dve, mean_steps, 2, b)
                        after(dve, "slices", b)
                        after(dve, "stT", b, 2)
                        sl = psum[:, SLICE_BANK, 0:HP * D1].rearrange("p (h d) -> p h d", h=HP)
                        st.link(v.tensor_scalar(slice_inv[:, u], sl[:, :, D], 1e-5, None, ALU.add))
                        st.link(v.reciprocal(slice_inv[:, u], slice_inv[:, u]))
                        v.tensor_tensor(ST[:, u], sl, bcast(slice_inv[:, u, :, None], [P, HP, D1]),
                                        ALU.mult).then_inc(at["slices_sb"].sem, 1)

                    def keep_vo(b, u):
                        after(dve, "vo", b)
                        after(dve, "ow", b, 2)
                        v.tensor_copy(VO[:, u].rearrange("p h g -> p (h g)"), psum[0:G, VO_BANK, :]).then_inc(at["vo_sb"].sem, 1)

                    def attention(b, u):
                        st = Steps(dve, score_steps, 1, b)
                        after(dve, "scores", b)
                        after(dve, "aT", b, 2)
                        sc = psum[:, SCORE_BANK, 0:HP * G].rearrange("p (h g) -> p h g", h=HP)
                        st.link(v.tensor_reduce(row_stat[:, u], sc, X, ALU.max))
                        v.tensor_tensor(A[:, u], sc, bcast(row_stat[:, u, :, None], [P, HP, G]),
                                        ALU.subtract).then_inc(at["sc_shifted"].sem, 1)
                        st = Steps(dve, attn_steps, 2, b)
                        after(dve, "sc_exped", b)
                        st.link(v.tensor_reduce(row_stat[:, u], A[:, u], X, ALU.add))
                        st.link(v.reciprocal(row_stat[:, u], row_stat[:, u]))
                        v.tensor_tensor(A[:, u], A[:, u], bcast(row_stat[:, u, :, None], [P, HP, G]),
                                        ALU.mult).then_inc(at["attn"].sem, 1)

                    def keep_ow(b, u):
                        after(dve, "ow", b)
                        after(dve, "rows", b, 2)
                        v.tensor_copy(OW[:, u].rearrange("p h g -> p (h g)"), psum[:, SCORE_BANK, 0:HP * D]).then_inc(at["ow_sb"].sem, 1)

                    def added(b, u):
                        st = Steps(dve, row_steps, 1, b)
                        st.link(v.tensor_tensor(seq_rows(h_all, b), seq_rows(h_all, b),
                                                bcast(w("fout_b")[:, None, :], [P, TT, D]), ALU.add))
                        after(dve, "rows", b)
                        v.tensor_tensor(seq_rows(h_all, b), seq_rows(h_all, b),
                                        two_tiles(psum[:, ROW_BANK, 0:TT * D]), ALU.add).then_inc(at["h_added"].sem, 1)

                    def measured(b, u):
                        row_moments(dve, 0, b, u, parts, small, at["h_added"])

                    def step(b, u, there):
                        if there(-1):
                            attention(b - 1, 1 - u)
                        if there(1):
                            less_top(b + 1, 1 - u)
                        if there(0):
                            slice_means(b, u)
                        if there(-1):
                            keep_ow(b - 1, 1 - u)
                        if there(1):
                            weight_sums(b + 1, 1 - u)
                        if there(2):
                            normalised(b + 2, u)
                        if there(-1):
                            added(b - 1, 1 - u)
                        if there(-1):
                            measured(b - 1, 1 - u)
                        if there(0):
                            keep_vo(b, u)
                    pipeline(dve, step, 2, 1)

        with ExitStack() as ctx:
            layer_stats("win_ln", 1e-5, on_the_way=True)
            NW = ROWS // WS
            parts, small = sb(ctx, "win_parts", [P, 2, TT, 6]), sb(ctx, "win_small", [P, 2, TT, 2])
            xn = sb(ctx, "win_xn", [P, 2, TT, D])
            xT = sb(ctx, "win_xT", [D, 2, ROWS])
            Qw = sb(ctx, "Qw", [P, 2, TT, 2, WS])
            Kw = sb(ctx, "Kw", [P, 2, TT, WS])
            Kd = sb(ctx, "Kd", [P, 2, TT, H, WS])
            Vd = sb(ctx, "Vd", [P, 2, NW, HP, 2 * DK])
            Aw = sb(ctx, "Aw", [P, 2, TT, H, WS])
            AwT = sb(ctx, "AwT", [P, 2, TT, HP, P])
            wtop, winv = sb(ctx, "win_top", [P, 2, TT, H]), sb(ctx, "win_inv", [P, 2, TT, H])
            On = sb(ctx, "On", [P, 2, TT, D])
            OnT = sb(ctx, "OnT", [D, 2, ROWS])
            V_BANK, QK_BANK, SCORE_BANK, AT_BANK, HEAD_BANK, ROW_BANK = 0, 1, 2, 4, 6, 7
            X_BANK, X_AT = HEAD_BANK, TT * D
            names = ["xn", "xT", "xT_sb", "qkv", "q_sb", "k_sb", "v_sb", "kd", "scores", "biased", "top", "shifted", "exped",
                     "aT", "aT_sb", "inv", "heads", "heads_sb", "oT", "oT_sb", "rows", "h_added"]
            at = {n: Signal(f"win_{n}") for n in names}
            sum_steps, row_steps, ready = sem("win_sum_steps"), sem("win_row_steps"), sem("win_prepared")

            def after(engine, name, b, before=0):
                engine.wait_ge(at[name].sem, at[name].done(b, before=before))

            with nc.Block() as block:
                @block.sync
                def _(sp):
                    open_signals(sp, list(at.values()))

                @block.tensor
                def _(pe):
                    t_ = nc.tensor

                    def transpose_x(b, u, heads_before):
                        after(pe, "xn", b)
                        after(pe, "xT_sb", b, 1)
                        if heads_before:
                            after(pe, "heads_sb", b, 4)
                        wait_apart(pe)
                        for t in range(TT):
                            last = t_.transpose(psum[0:D, X_BANK, X_AT + t * P:X_AT + (t + 1) * P], xn[:, u, t, :], ident)
                        last.then_inc(at["xT"].sem, 1)

                    def qkv(b, u):
                        after(pe, "xT_sb", b)
                        after(pe, "q_sb", b, 1)
                        after(pe, "k_sb", b, 1)
                        after(pe, "v_sb", b, 1)
                        wait_apart(pe)
                        t_.matmul(psum[:, QK_BANK, 0:ROWS], w("a_qk"), xT[:, u], start=True, stop=True)
                        for t in range(TT):
                            last = t_.matmul(psum[:, V_BANK, t * D:(t + 1) * D],
                                             xT[:, u, t * P:(t + 1) * P], w("a_v"), start=True, stop=True)
                        last.then_inc(at["qkv"].sem, 1)

                    def scores(b, u):
                        after(pe, "kd", b)
                        after(pe, "q_sb", b)
                        after(pe, "biased", b, 1)
                        wait_apart(pe)
                        for t in range(TT):
                            last = t_.matmul(psum[:, SCORE_BANK + t, :], Qw[:, u, t].rearrange("p n q -> p (n q)"),
                                             Kd[:, u, t].rearrange("p h k -> p (h k)"), start=True, stop=True)
                        last.then_inc(at["scores"].sem, 1)

                    def transpose_attention(b, u):
                        after(pe, "exped", b)
                        after(pe, "aT_sb", b, 1)
                        for t in range(TT):
                            for hp in range(HP):
                                last = t_.transpose(psum[:, AT_BANK + t, hp * P:(hp + 1) * P],
                                                    Aw[:, u, t, 2 * hp:2 * hp + 2].rearrange("p h k -> p (h k)"), ident)
                        last.then_inc(at["aT"].sem, 1)

                    def heads(b, u, rows_ahead):
                        after(pe, "aT_sb", b)
                        after(pe, "v_sb", b)
                        after(pe, "heads_sb", b, 1)
                        if rows_ahead:
                            after(pe, "xT_sb", b + 3)
                        for n in range(NW):
                            for hp in range(HP):
                                last = t_.matmul(psum[(n % 2) * WS:(n % 2 + 1) * WS, HEAD_BANK,
                                                      (n // 2) * D + hp * 2 * DK:(n // 2) * D + (hp + 1) * 2 * DK],
                                                 AwT[:, u, n // 2, hp, (n % 2) * WS:(n % 2 + 1) * WS],
                                                 Vd[:, u, n, hp, :], start=True, stop=True)
                        last.then_inc(at["heads"].sem, 1)

                    def transpose_heads(b, u):
                        after(pe, "heads_sb", b)
                        after(pe, "h_added", b, 1)
                        wait_apart(pe)
                        for t in range(TT):
                            last = t_.transpose(psum[0:D, ROW_BANK, t * P:(t + 1) * P], On[:, u, t, :], ident)
                        last.then_inc(at["oT"].sem, 1)

                    def rows_out(b, u):
                        after(pe, "oT_sb", b)
                        for t in range(TT):
                            last = t_.matmul(psum[:, ROW_BANK, ROWS + t * D:ROWS + (t + 1) * D], OnT[:, u, t * P:(t + 1) * P],
                                             w("a_proj"), start=True, stop=True)
                        last.then_inc(at["rows"].sem, 1)

                    def step(b, u, there):
                        if there(0):
                            scores(b, u)
                        if there(1):
                            qkv(b + 1, 1 - u)
                        if there(-2):
                            transpose_heads(b - 2, u)
                        if there(2):
                            transpose_x(b + 2, u, there(-2))
                        if there(-1):
                            transpose_attention(b - 1, 1 - u)
                        if there(-2):
                            rows_out(b - 2, u)
                        if there(-1):
                            heads(b - 1, 1 - u, there(2))
                    pipeline(pe, step, 3, 2)

                @block.scalar
                def _(act):
                    a = nc.scalar

                    def step(b, u, there):
                        if there(1):
                            after(act, "qkv", b + 1)
                            after(act, "kd", b + 1, 2)
                            for odd in range(2):
                                last = a.activation(Kw[odd * D:(odd + 1) * D, 1 - u], psum[D:P, QK_BANK, 0:ROWS]
                                                    .rearrange("p (t n k) -> p t n k", t=TT, n=2)[:, :, odd, :], ACT.Copy)
                            last.then_inc(at["k_sb"].sem, 1)
                        if there(-2):
                            after(act, "oT", b - 2)
                            after(act, "rows", b - 2, 2)
                            a.activation(OnT[:, u], psum[0:D, ROW_BANK, 0:ROWS], ACT.Copy).then_inc(at["oT_sb"].sem, 1)
                        if there(2):
                            after(act, "xT", b + 2)
                            after(act, "qkv", b + 2, 2)
                            a.activation(xT[:, u], psum[0:D, X_BANK, X_AT:X_AT + ROWS], ACT.Copy).then_inc(at["xT_sb"].sem, 1)
                        if there(-1):
                            after(act, "aT", b - 1)
                            after(act, "heads", b - 1, 2)
                            a.activation(AwT[:, 1 - u].rearrange("p t h n -> p t (h n)"),
                                         psum[:, AT_BANK:AT_BANK + 2, :], ACT.Copy).then_inc(at["aT_sb"].sem, 1)
                        if there(0):
                            after(act, "shifted", b)
                            a.activation(Aw[:, u], Aw[:, u], ACT.Exp).then_inc(at["exped"].sem, 1)
                    pipeline(act, step, 3, 2)

                @block.gpsimd
                def _(pool):
                    g = nc.gpsimd

                    def step(b, u, there):
                        if there(1):
                            after(pool, "k_sb", b + 1)
                            after(pool, "scores", b + 1, 2)
                            g.tensor_tensor(Kd[:, 1 - u], bcast(Kw[:, 1 - u, :, None, :], [P, TT, H, WS]),
                                            bcast(w("head_mask")[:, None, :, None], [P, TT, H, WS]), ALU.mult).then_inc(at["kd"].sem, 1)
                        if there(0):
                            after(pool, "top", b)
                            aw = Aw[:, u].rearrange("p t h k -> p (t h) k")
                            g.tensor_tensor(aw, aw, bcast(wtop[:, u].rearrange("p t h -> p (t h)")[:, :, None], [P, TT * H, WS]),
                                            ALU.subtract).then_inc(at["shifted"].sem, 1)
                    pipeline(pool, step, 3, 2)

                @block.vector
                def _(dve):
                    v = nc.vector
                    v.memset(Qw[:], 0.0)
                    v.memset(Vd[:], 0.0).then_inc(ready, 1)
                    dve.wait_ge(ready, 1)

                    def normalised(b, u):
                        after(dve, "xT", b, 2)
                        normed(dve, 1, xn[:, u], b, at["xn"].sem)

                    def keep_q(b, u):
                        after(dve, "qkv", b)
                        after(dve, "scores", b, 2)
                        for odd in range(2):
                            last = v.tensor_scalar(Qw[odd * D:(odd + 1) * D, u, :, odd, :], psum[0:D, QK_BANK, 0:ROWS]
                                                   .rearrange("p (t n k) -> p t n k", t=TT, n=2)[:, :, odd, :],
                                                   DK ** -0.5, None, ALU.mult)
                        last.then_inc(at["q_sb"].sem, 1)

                    def keep_v(b, u):
                        after(dve, "heads", b, 2)
                        for odd in range(2):
                            vals = psum[odd * WS:(odd + 1) * WS, V_BANK, 0:TT * D].rearrange(
                                "p (t h s d) -> p t h (s d)", t=TT, h=HP, s=2)
                            for half in range(2):
                                mine = slice(half * DK, (half + 1) * DK)
                                last = v.tensor_copy(Vd[half * WS:(half + 1) * WS, u, odd::2, :, mine], vals[:, :, :, mine])
                        last.then_inc(at["v_sb"].sem, 1)

                    def biased(b, u):
                        after(dve, "scores", b)
                        after(dve, "aT", b, 2)
                        after(dve, "inv", b, 2)
                        aw = Aw[:, u].rearrange("p t h k -> p (t h) k")
                        v.tensor_tensor(
                            aw, psum[:, SCORE_BANK:SCORE_BANK + 2, :].rearrange("p t (h k) -> p (t h) k", k=WS),
                            bcast(w("rel")[:, None, :], [P, TT * H, WS]), ALU.add).then_inc(at["biased"].sem, 1)
                        after(dve, "biased", b)
                        v.tensor_reduce(wtop[:, u].rearrange("p t h -> p (t h)"), aw, X, ALU.max).then_inc(at["top"].sem, 1)

                    def sums(b, u):
                        after(dve, "exped", b)
                        wi = winv[:, u].rearrange("p t h -> p (t h)")
                        st = Steps(dve, sum_steps, 1, b)
                        st.link(v.tensor_reduce(wi, Aw[:, u].rearrange("p t h k -> p (t h) k"), X, ALU.add))
                        v.reciprocal(wi, wi).then_inc(at["inv"].sem, 1)

                    def scaled_heads(b, u):
                        after(dve, "heads", b)
                        after(dve, "inv", b)
                        after(dve, "oT", b, 2)
                        wi = winv[:, u].rearrange("p t h -> p (t h)")
                        v.tensor_tensor(On[:, u].rearrange("p t (h d) -> p (t h) d", d=DK),
                                        psum[:, HEAD_BANK, 0:TT * D].rearrange("p (n d) -> p n d", d=DK),
                                        bcast(wi[:, :, None], [P, TT * H, DK]), ALU.mult).then_inc(at["heads_sb"].sem, 1)

                    def added(b, u):
                        st = Steps(dve, row_steps, 1, b)
                        st.link(v.tensor_tensor(seq_rows(h_all, b), seq_rows(h_all, b),
                                                bcast(w("a_proj_b")[:, None, :], [P, TT, D]), ALU.add))
                        after(dve, "rows", b)
                        v.tensor_tensor(seq_rows(h_all, b), seq_rows(h_all, b),
                                        two_tiles(psum[:, ROW_BANK, ROWS:ROWS + TT * D]), ALU.add).then_inc(at["h_added"].sem, 1)

                    def measured(b, u):
                        row_moments(dve, 1, b, u, parts, small, at["h_added"])

                    def step(b, u, there):
                        if there(0):
                            biased(b, u)
                        if there(-1):
                            sums(b - 1, 1 - u)
                        if there(1):
                            keep_q(b + 1, 1 - u)
                        if there(-1):
                            scaled_heads(b - 1, 1 - u)
                        if there(1):
                            keep_v(b + 1, 1 - u)
                        if there(3):
                            normalised(b + 3, 1 - u)
                        if there(-2):
                            added(b - 2, u)
                            measured(b - 2, u)
                    pipeline(dve, step, 3, 2)
        with ExitStack() as ctx:
            layer_stats("moe_ln", 1e-5, on_the_way=True)
            EP = E // 2
            CE = PARTS_OF_C * E
            xn = sb(ctx, "moe_xn", [P, 2, TT, D])
            xT = sb(ctx, "moe_xT", [D, 2, ROWS])
            Pr = sb(ctx, "Pr", [P, 2, TT, E])
            eq, count, Left = (sb(ctx, n, [P, TT, E]) for n in ("eq", "count", "Left"))
            starts = sb(ctx, "starts", [P, TT, E])
            largest, best1, best2 = (sb(ctx, n, [P, TT]) for n in ("largest", "best1", "best2"))
            Cm = sb(ctx, "Cm", [P, TT, E])
            Chigh = sb(ctx, "Chigh", [P, TT, E], BF16)
            Cs = sb(ctx, "Cs", [P, 2, TT, CE])
            b2_parts = sb(ctx, "b2_parts", [CE, PARTS_OF_C, D], BF16)
            b2_rest, b2_high = sb(ctx, "b2_rest", [CE, D]), sb(ctx, "b2_high", [CE, D])
            cTh = sb(ctx, "cTh", [CE, 2, ROWS], BF16)
            expand = sb(ctx, "expand_sb", [CE, EP * P], BF16)
            Hd = sb(ctx, "Hd", [P, 2, EP, ROWS])
            X_BANK, LOGIT_BANK, C_BANK, SPREAD_BANK, HIDDEN_BANK, ROW_BANK = 0, 1, 2, 3, 5, 7
            names = ["xn", "xT", "xT_sb", "logits", "shifted", "exped", "chosen", "cT", "cT_sb", "hidden", "gelu",
                     "spread", "weighted", "rows", "h_added"]
            at = {n: Signal(f"moe_{n}") for n in names}
            joined, top_steps, choose_steps, ready = sem("moe_joined"), sem("moe_top_steps"), sem("moe_choose_steps"), sem("moe_prepared")
            choose_ready, b2_steps = sem("moe_starts_ready"), sem("moe_b2_steps")
            AHEAD, BEHIND = 3, 1

            def after(engine, name, b, before=0):
                engine.wait_ge(at[name].sem, at[name].done(b, before=before))

            with nc.Block() as block:
                @block.sync
                def _(sp):
                    open_signals(sp, list(at.values()))

                @block.tensor
                def _(pe):
                    t_ = nc.tensor

                    def transpose_x(b, u):
                        after(pe, "xn", b)
                        after(pe, "xT_sb", b, 1)
                        wait_apart(pe)
                        for t in range(TT):
                            last = t_.transpose(psum[0:D, X_BANK, t * P:(t + 1) * P], xn[:, u, t, :], ident)
                        last.then_inc(at["xT"].sem, 1)

                    def logits(b, u):
                        after(pe, "xT_sb", b)
                        after(pe, "shifted", b, 1)
                        for t in range(TT):
                            last = t_.matmul(psum[:, LOGIT_BANK, t * E:(t + 1) * E], xT[:, u, t * P:(t + 1) * P],
                                             w("router"), start=True, stop=True)
                        last.then_inc(at["logits"].sem, 1)

                    def transpose_c(b, u):
                        after(pe, "chosen", b)
                        after(pe, "cT_sb", b, 1)
                        wait_apart(pe)
                        for t in range(TT):
                            last = t_.transpose(psum[0:CE, C_BANK, t * P:(t + 1) * P], Cs[:, u, t, :], ident)
                        last.then_inc(at["cT"].sem, 1)

                    def hidden(b, u):
                        after(pe, "xT_sb", b)
                        after(pe, "gelu", b, 1)
                        for c in range(EP):
                            last = t_.matmul(psum[:, HIDDEN_BANK + c // 2, (c % 2) * ROWS:(c % 2 + 1) * ROWS],
                                             w("w1")[:, c * P:(c + 1) * P], xT[:, u], start=True, stop=True)
                        last.then_inc(at["hidden"].sem, 1)

                    def spread(b, u):
                        after(pe, "cT_sb", b)
                        after(pe, "weighted", b, 1)
                        for c in range(EP):
                            last = t_.matmul(psum[:, SPREAD_BANK + c // 2, (c % 2) * ROWS:(c % 2 + 1) * ROWS],
                                             expand[:, c * P:(c + 1) * P], cTh[:, u], start=True, stop=True)
                        last.then_inc(at["spread"].sem, 1)

                    def rows_out(b, u):
                        after(pe, "weighted", b)
                        after(pe, "h_added", b, 1)
                        for t in range(TT):
                            for c in range(EP):
                                t_.matmul(psum[:, ROW_BANK, t * D:(t + 1) * D], Hd[:, u, c, t * P:(t + 1) * P],
                                          w("w2")[:, c * D:(c + 1) * D], start=(c == 0), stop=False)
                            for part in range(PARTS_OF_C):
                                last = t_.matmul(psum[:, ROW_BANK, t * D:(t + 1) * D], cTh[:, u, t * P:(t + 1) * P],
                                                 b2_parts[:, part, :], start=False, stop=(part == PARTS_OF_C - 1))
                        last.then_inc(at["rows"].sem, 1)

                    def step(b, u, there):
                        if there(0):
                            transpose_c(b, u)
                            hidden(b, u)
                        if there(2):
                            transpose_x(b + 2, u)
                        if there(0):
                            spread(b, u)
                        if there(-1):
                            rows_out(b - 1, 1 - u)
                        if there(2):
                            logits(b + 2, u)

                    pe.wait_ge(ready, 1)
                    pipeline(pe, step, AHEAD, BEHIND)

                @block.scalar
                def _(act):
                    a = nc.scalar

                    def step(b, u, there):
                        if there(0):
                            after(act, "cT", b)
                            after(act, "rows", b, 2)
                            a.activation(cTh[:, u], psum[0:CE, C_BANK, 0:ROWS], ACT.Copy).then_inc(at["cT_sb"].sem, 1)
                        if there(2):
                            after(act, "xT", b + 2)
                            after(act, "hidden", b + 2, 2)
                            a.activation(xT[:, u], psum[0:D, X_BANK, 0:ROWS], ACT.Copy).then_inc(at["xT_sb"].sem, 1)
                        if there(0):
                            after(act, "hidden", b)
                            for c in range(EP):
                                last = a.activation(Hd[:, u, c], psum[:, HIDDEN_BANK + c // 2, (c % 2) * ROWS:(c % 2 + 1) * ROWS],
                                                    ACT.Gelu, bias=w("b1")[:, c:c + 1])
                            last.then_inc(at["gelu"].sem, 1)
                        if there(2):
                            after(act, "shifted", b + 2)
                            a.activation(Pr[:, u], Pr[:, u], ACT.Exp).then_inc(at["exped"].sem, 1)
                    pipeline(act, step, AHEAD, BEHIND)

                @block.vector
                def _(dve):
                    v = nc.vector
                    wide = [P, TT, E]
                    flat = lambda t: t.rearrange("p r e -> p (r e)")
                    over = lambda t: bcast(t[:][:, :, None], wide)

                    def normalised(b, u):
                        after(dve, "xT", b, 2)
                        normed(dve, 2, xn[:, u], b, at["xn"].sem)
                        after(dve, "xn", b)
                        v.tensor_tensor(seq_rows(h_all, b), seq_rows(h_all, b), xn[:, u], ALU.add).then_inc(joined, 1)

                    def less_top(b, u):
                        after(dve, "logits", b)
                        after(dve, "shifted", b, 1)
                        after(dve, "chosen", b, 2)
                        rows = psum[:, LOGIT_BANK, 0:TT * E].rearrange("p (t e) -> p t e", t=TT)
                        v.tensor_reduce(largest[:], rows, X, ALU.max).then_inc(top_steps, 1)
                        dve.wait_ge(top_steps, b + 1)
                        v.tensor_tensor(Pr[:, u], rows, over(largest), ALU.subtract).then_inc(at["shifted"].sem, 1)

                    def choose(b, u):
                        st = Steps(dve, choose_steps, CHOOSE_STEPS, b)
                        pr = Pr[:, u]
                        after(dve, "exped", b)
                        after(dve, "cT", b, 2)
                        st.link(v.tensor_reduce(best1[:], pr, X, ALU.add))
                        st.link(v.reciprocal(best1[:], best1[:]))
                        st.link(v.tensor_tensor(pr, pr, over(best1), ALU.mult))

                        def first_of_best(best, source):
                            st.link(v.tensor_reduce(best[:], source, X, ALU.max))
                            st.link(v.tensor_tensor(eq[:], source, over(best), ALU.is_equal))
                            wait_apart(dve)
                            st.link(v.tensor_tensor_scan(flat(count[:]), flat(starts[:]), flat(eq[:]), 0.0, ALU.mult, ALU.add))
                            wait_apart(dve)
                            st.link(v.scalar_tensor_tensor(flat(count[:]), flat(count[:]), 1.0, flat(eq[:]), ALU.is_equal, ALU.mult))

                        first_of_best(best1, pr)
                        st.step(v.tensor_tensor(Cm[:], pr, count[:], ALU.mult))
                        wait_apart(dve)
                        st.link(v.scalar_tensor_tensor(flat(Left[:]), flat(count[:]), -2.0, flat(pr), ALU.mult, ALU.add))
                        first_of_best(best2, Left[:])
                        st.step(v.tensor_tensor(best1[:], best1[:], best2[:], ALU.add))
                        st.link(v.tensor_tensor(count[:], pr, count[:], ALU.mult))
                        st.step(v.tensor_scalar(best1[:], best1[:], 1e-12, None, ALU.max))
                        st.link(v.tensor_tensor(Cm[:], Cm[:], count[:], ALU.add))
                        st.link(v.reciprocal(best1[:], best1[:]))
                        st.link(v.tensor_tensor(Cm[:], Cm[:], over(best1), ALU.mult))
                        for part in range(PARTS_OF_C - 1):
                            mine = Cs[:, u, :, part * E:(part + 1) * E]
                            st.link(v.tensor_copy(Chigh[:], Cm[:]))
                            st.link(v.tensor_copy(mine, Chigh[:]))
                            last = part == PARTS_OF_C - 2
                            rest = v.tensor_tensor(Cs[:, u, :, (part + 1) * E:] if last else Cm[:], Cm[:], mine, ALU.subtract)
                            if last:
                                rest.then_inc(at["chosen"].sem, 1)
                            else:
                                st.link(rest)
                        st.end()

                    def weighted(b, u):
                        after(dve, "gelu", b)
                        after(dve, "spread", b)
                        hd = Hd[:, u].rearrange("p c n -> p (c n)")
                        v.tensor_tensor(hd, hd, psum[:, SPREAD_BANK:SPREAD_BANK + 2, :].rearrange("p k n -> p (k n)"),
                                        ALU.mult).then_inc(at["weighted"].sem, 1)

                    def added(b, u):
                        after(dve, "rows", b)
                        dve.wait_ge(joined, b + 1)
                        v.tensor_tensor(seq_rows(h_all, b), seq_rows(h_all, b),
                                        two_tiles(psum[:, ROW_BANK, 0:TT * D]), ALU.add).then_inc(at["h_added"].sem, 1)

                    def step(b, u, there):
                        if there(1):
                            choose(b + 1, 1 - u)
                        if there(2):
                            less_top(b + 2, u)
                        if there(0):
                            weighted(b, u)
                        if there(3):
                            normalised(b + 3, 1 - u)
                        if there(-1):
                            added(b - 1, 1 - u)

                    CHOOSE_STEPS = 24
                    v.memset(starts[:], 1.0).then_inc(choose_ready, 1)
                    dve.wait_ge(choose_ready, 1)
                    v.memset(starts[:, :, 0:1], 0.0).then_inc(choose_ready, 1)
                    st = Steps(dve, b2_steps)
                    st.link(v.tensor_copy(b2_parts[:, 0, :], w("b2")))
                    st.link(v.tensor_copy(b2_high[:], b2_parts[:, 0, :]))
                    st.link(v.tensor_tensor(b2_rest[:], w("b2"), b2_high[:], ALU.subtract))
                    st.link(v.tensor_copy(b2_parts[:, 1, :], b2_rest[:]))
                    st.link(v.tensor_copy(b2_high[:], b2_parts[:, 1, :]))
                    st.link(v.tensor_tensor(b2_parts[:, 2, :], b2_rest[:], b2_high[:], ALU.subtract))
                    v.tensor_copy(expand[:], w("expand")).then_inc(ready, 1)
                    dve.wait_ge(choose_ready, 2)
                    pipeline(dve, step, AHEAD, BEHIND)

        stored = sem("stored")
        with nc.Block() as block:
            @block.sync
            def _(sp):
                sp.dma_start(out, h_all[:]).then_inc(stored, 16)
                sp.wait_ge(stored, 16)


def kernel(**inputs):
    import numpy as np
    import concourse.bacc as _bacc
    from concourse.bass_utils import run_bass_kernel_spmd as _run

    a = {k: np.asarray(v) for k, v in inputs.items()}
    rows = lambda v: np.broadcast_to(np.reshape(v, (1, -1)), (P, np.size(v)))
    x = a["x"].reshape(B, NCHUNK, CHUNK).transpose(2, 0, 1)
    x_chunks = np.zeros((P, B, NCHUNK + 1), np.float32)
    x_chunks[:, :, :NCHUNK] = x

    tok_w = a["L0_tok_W"].T
    rel = a["L1_attn_rel_bias"]
    q_at, k_at = np.meshgrid(np.arange(WS), np.arange(WS), indexing="ij")
    rel_tile = rel[k_at - q_at + WS - 1]
    pad_mask = np.ones((P, TT), np.float32)
    pad_mask[P - 1, TT - 1] = 0
    head_mask = (np.arange(P)[:, None] % D // DK == np.arange(H)[None, :]).astype(np.float32)
    query = (np.arange(P) % QB)[:, None]
    last_key = np.where(np.arange(QB)[None, :] > query, NEG, 0).astype(np.float32)
    expand = np.zeros((E, E // 2, P), np.float32)
    for e in range(E):
        expand[e, e // 2, (e % 2) * D:(e % 2 + 1) * D] = 1
    qkv = a["L1_attn_w_qkv"]
    taps = a["L0_attn_conv_w"].transpose(1, 2, 0)
    conv = np.zeros((2, D, TAP_PAIRS, D), np.float32)
    conv[0], conv[1, :, :TAP_PAIRS - 1] = taps[:, 0::2], taps[:, 1::2]
    conv = conv.reshape(P, TAP_PAIRS * D)
    pack = {
        "tok_w0": tok_w[:P], "tok_w1": tok_w[P:], "tok_b": rows(a["L0_tok_b"]),
        "tok_gamma": rows(a["L0_tok_gamma"]), "tok_beta": rows(a["L0_tok_beta"]),
        "ident": np.eye(P, dtype=np.float32), "pad_mask": pad_mask, "head_mask": head_mask,
        "conv": conv,
        "conv_b": rows(a["L0_attn_conv_b"]), "sqrt_beta": rows(a["L0_attn_sqrt_beta"]),
        "ln_w": a["L0_attn_ln_w"][:, None], "ln_b": a["L0_attn_ln_b"][:, None],
        "ln_b_wide": np.broadcast_to(a["L0_attn_ln_b"][:, None], (D, P)),
        "q_w": a["L0_attn_q_w"].T, "k_w": a["L0_attn_k_w"].T, "v_w": a["L0_attn_v_w"].T,
        "q_b": a["L0_attn_q_b"][:, None], "k_b": np.tile(a["L0_attn_k_b"], 2)[:, None], "v_b": rows(a["L0_attn_v_b"]),
        "out_w": a["L0_attn_out_w"].T, "out_b": rows(a["L0_attn_out_b"]),
        "gammas": np.repeat(a["L0_attn_gammas"].reshape(H), QB)[:, None],
        "fx_wT": np.concatenate([a["L0_ffn_W_fx"], a["L0_ffn_b_fx"][None]]).reshape(D + 1, H, D)
        .transpose(2, 1, 0).reshape(D, H * (D + 1)),
        "x_w": a["L0_ffn_W_x"].reshape(D, H, D).transpose(2, 1, 0).reshape(D, H * D),
        "x_b": a["L0_ffn_b_x"].reshape(H, D).T, "slice_w": a["L0_ffn_W_slice"],
        "slice_b": np.broadcast_to(a["L0_ffn_b_slice"][None], (D + 1, G)), "temp": rows(a["L0_ffn_temperature"]),
        "fq_w": a["L0_ffn_W_q"].T, "fk_w": a["L0_ffn_W_k"].T, "fv_w": a["L0_ffn_W_v"].T,
        "fout_w": a["L0_ffn_W_out"].reshape(H, D, D).transpose(1, 0, 2).reshape(D, H * D),
        "fout_b": rows(a["L0_ffn_b_out"]),
        "a_qk": qkv[0:2 * D].T, "a_v": qkv[2 * D:].T, "a_proj": a["L1_attn_w_proj"].T,
        "a_proj_b": rows(a["L1_attn_b_proj"]), "rel": np.concatenate([rel_tile, rel_tile]),
        "router": a["L1_ffn_router_w"].T,
        "w1": a["L1_ffn_w1"].transpose(1, 0, 2).reshape(D, E * D),
        "b1": a["L1_ffn_b1"].reshape(E // 2, P).T,
        "w2": a["L1_ffn_w2"].reshape(E // 2, P, D).transpose(1, 0, 2).reshape(P, (E // 2) * D),
        "b2": np.concatenate([a["L1_ffn_b2"]] * PARTS_OF_C),
        "expand": np.concatenate([expand.reshape(E, -1)] * PARTS_OF_C), "last_key": last_key,
    }
    cols, total = weight_columns()
    weights = np.zeros((P, total), np.float32)
    for name, (at, r, n) in cols.items():
        weights[:r, at:at + n] = pack[name]
    tables = np.zeros((P, 2, PACKED), np.float32)
    tables[:, 1] = 1
    for j in range(NQ):
        key = np.arange(SPAN[j])[None, :]
        tables[:, 0, OFF[j]:OFF[j] + SPAN[j]] = np.maximum(QB * j + query - key, 0)
        tables[:, 1, OFF[j] + SPAN[j] - 1] = 0

    nc = _bacc.Bacc("TRN2", target_bir_lowering=False, num_devices=1)
    arrays = {"x_chunks": x_chunks, "weights": weights, "tables": tables}
    args = [nc.dram_tensor(k, v.shape, F32, kind="ExternalInput").ap() for k, v in arrays.items()]
    out = nc.dram_tensor("out", (P, B * TT, D), F32, kind="ExternalOutput").ap()
    build(nc, *args, out)
    got = _run(nc, [arrays], core_ids=[0]).results[0]["out"]
    return got.reshape(P, B, TT, D).transpose(1, 2, 0, 3).reshape(B, ROWS, D)[:, :TOK]
```
